# Optimizing a Trainium2 kernel written in Bass

```python
import numpy as np
import jax
import jax.numpy as jnp

def _softmax(x, axis=-1):
    return jax.nn.softmax(x, axis=axis)

def _gelu(x):
    return jax.nn.gelu(x, approximate=True)

def _silu(x):
    return jax.nn.silu(x)

def _sigmoid(x):
    return jax.nn.sigmoid(x)

def _layernorm(x, axis=-1, eps=1e-05):
    m = jnp.mean(x, axis=axis, keepdims=True)
    v = jnp.var(x, axis=axis, keepdims=True)
    return (x - m) / jnp.sqrt(v + eps)

def _scatter_add(tgt, idx, src, axis=0):
    return tgt.at[idx].add(src)

def _segment_sum(src, seg, n):
    return jax.ops.segment_sum(src, seg, n)
kernel_name = 'mk_vit_tower_d1_tok_img256_r4_b861c9'

def setup_inputs(seed: int=0):
    np.random.seed(seed)
    _w = jnp.asarray

    def _rec_inputs():
        import jax
        import jax.numpy as jnp
        _rk = jax.random.key(seed)
        x = -0.000125008 + 0.999885 * jax.random.normal(jax.random.fold_in(_rk, 1), (128, 64, 64, 64), jnp.float32)
        return x
    x = _rec_inputs()

    def _L0_tok_setup():
        import jax, jax.numpy as jnp
        import numpy as np
        B, C, H, W = (32, 64, 64, 64)
        STRIDE, HEADS = (4, 8)

        def _ln(x, w, b):
            mu = x.mean(-1, keepdims=True)
            var = ((x - mu) ** 2).mean(-1, keepdims=True)
            return (x - mu) * jax.lax.rsqrt(var + 1e-05) * w + b
        key = jax.random.key(seed)
        ks = jax.random.split(key, 4)
        return {'features': jax.random.normal(ks[0], (B, C, H, W), dtype=jnp.float32), 'ln_q_w': jnp.ones((C,), jnp.float32), 'ln_q_b': jnp.zeros((C,), jnp.float32), 'Wq': jax.random.normal(ks[1], (C, C), dtype=jnp.float32) * 0.02, 'ln_kv_w': jnp.ones((C,), jnp.float32), 'ln_kv_b': jnp.zeros((C,), jnp.float32), 'Wkv': jax.random.normal(ks[2], (2 * C, C), dtype=jnp.float32) * 0.02, 'proj_w': jax.random.normal(ks[3], (C, C), dtype=jnp.float32) * 0.02, 'proj_b': jnp.zeros((C,), jnp.float32), 'conv_stride': STRIDE, 'num_heads': HEADS}
    _L0_tok_all = _L0_tok_setup()
    _L0_tok_in = {k: v for k, v in _L0_tok_all.items() if k in ('ln_q_w', 'ln_q_b', 'Wq', 'ln_kv_w', 'ln_kv_b', 'Wkv', 'proj_w', 'proj_b')}
    del _L0_tok_all

    def _L0_attn_setup():
        import math
        import jax, jax.numpy as jnp
        import numpy as np
        EPS_DIV = 1e-07
        EPS_NORM = 1e-12

        def _l2_normalize(x, axis):
            n = jnp.sqrt(jnp.sum(x * x, axis=axis, keepdims=True))
            return x / jnp.maximum(n, EPS_NORM)
        key = jax.random.key(seed)
        ks = jax.random.split(key, 5)
        b, N, C = (8, 1024, 64)
        x = jax.random.normal(ks[0], (b, N, C), dtype=jnp.float32)
        W_qkv = jax.random.normal(ks[1], (C, 3 * C), dtype=jnp.float32) * (1.0 / math.sqrt(C))
        b_qkv = jax.random.normal(ks[2], (3 * C,), dtype=jnp.float32) * 0.02
        W_out = jax.random.normal(ks[3], (C, C), dtype=jnp.float32) * (1.0 / math.sqrt(C))
        b_out = jax.random.normal(ks[4], (C,), dtype=jnp.float32) * 0.02
        return {'x': x, 'W_qkv': W_qkv, 'b_qkv': b_qkv, 'W_out': W_out, 'b_out': b_out}
    _L0_attn_all = _L0_attn_setup()
    _L0_attn_in = {k: v for k, v in _L0_attn_all.items() if k in ('W_qkv', 'b_qkv', 'W_out', 'b_out')}
    del _L0_attn_all

    def _L0_ffn_setup():
        import jax, jax.numpy as jnp
        import numpy as np
        B, T, C = (64, 96, 64)
        NH, NKV = (4, 2)
        HD = C // NH
        NREP = NH // NKV
        NE, TOPK = (8, 2)
        HID = int(8 / 3 * C)
        EPS_RMS = 1e-06

        def _rope_tables(t_len):
            inv_freq = 1.0 / 10000.0 ** (np.arange(0, HD, 2, dtype=np.float32) / HD)
            t = np.arange(t_len, dtype=np.float32)
            freqs = np.outer(t, inv_freq)
            emb = np.concatenate([freqs, freqs], axis=-1)
            return (jnp.asarray(np.cos(emb)), jnp.asarray(np.sin(emb)))

        def _rotate_half(x):
            h = x.shape[-1] // 2
            return jnp.concatenate([-x[..., h:], x[..., :h]], axis=-1)

        def _rmsnorm(v, w):
            return v * jax.lax.rsqrt(jnp.mean(v * v, axis=-1, keepdims=True) + EPS_RMS) * w
        key = jax.random.key(seed)
        ks = jax.random.split(key, 10)
        s = lambda k, shape: jax.random.normal(k, shape, jnp.float32) * 0.02
        return {'x': jax.random.normal(ks[0], (B, T, C), jnp.float32), 'ln1_w': jnp.ones((C,), jnp.float32), 'ln2_w': jnp.ones((C,), jnp.float32), 'wq': s(ks[1], (NH * HD, C)), 'wk': s(ks[2], (NKV * HD, C)), 'wv': s(ks[3], (NKV * HD, C)), 'wo': s(ks[4], (C, C)), 'router_w': s(ks[5], (NE, C)), 'w1': s(ks[6], (NE, HID, C)), 'w2': s(ks[7], (NE, C, HID)), 'w3': s(ks[8], (NE, HID, C))}
    _L0_ffn_all = _L0_ffn_setup()
    _L0_ffn_in = {k: v for k, v in _L0_ffn_all.items() if k in ('ln1_w', 'ln2_w', 'wq', 'wk', 'wv', 'wo', 'router_w', 'w1', 'w2', 'w3')}
    del _L0_ffn_all
    return {'x': x, 'L0_tok_ln_q_w': _L0_tok_in['ln_q_w'], 'L0_tok_ln_q_b': _L0_tok_in['ln_q_b'], 'L0_tok_Wq': _L0_tok_in['Wq'], 'L0_tok_ln_kv_w': _L0_tok_in['ln_kv_w'], 'L0_tok_ln_kv_b': _L0_tok_in['ln_kv_b'], 'L0_tok_Wkv': _L0_tok_in['Wkv'], 'L0_tok_proj_w': _L0_tok_in['proj_w'], 'L0_tok_proj_b': _L0_tok_in['proj_b'], 'L0_attn_W_qkv': _L0_attn_in['W_qkv'], 'L0_attn_b_qkv': _L0_attn_in['b_qkv'], 'L0_attn_W_out': _L0_attn_in['W_out'], 'L0_attn_b_out': _L0_attn_in['b_out'], 'L0_ffn_ln1_w': _L0_ffn_in['ln1_w'], 'L0_ffn_ln2_w': _L0_ffn_in['ln2_w'], 'L0_ffn_wq': _L0_ffn_in['wq'], 'L0_ffn_wk': _L0_ffn_in['wk'], 'L0_ffn_wv': _L0_ffn_in['wv'], 'L0_ffn_wo': _L0_ffn_in['wo'], 'L0_ffn_router_w': _L0_ffn_in['router_w'], 'L0_ffn_w1': _L0_ffn_in['w1'], 'L0_ffn_w2': _L0_ffn_in['w2'], 'L0_ffn_w3': _L0_ffn_in['w3']}

def reference(x, L0_tok_ln_q_w, L0_tok_ln_q_b, L0_tok_Wq, L0_tok_ln_kv_w, L0_tok_ln_kv_b, L0_tok_Wkv, L0_tok_proj_w, L0_tok_proj_b, L0_attn_W_qkv, L0_attn_b_qkv, L0_attn_W_out, L0_attn_b_out, L0_ffn_ln1_w, L0_ffn_ln2_w, L0_ffn_wq, L0_ffn_wk, L0_ffn_wv, L0_ffn_wo, L0_ffn_router_w, L0_ffn_w1, L0_ffn_w2, L0_ffn_w3):
    import jax
    import jax.numpy as jnp

    def _L0_tok_ref(features, ln_q_w, ln_q_b, Wq, ln_kv_w, ln_kv_b, Wkv, proj_w, proj_b, conv_stride, num_heads):
        import jax, jax.numpy as jnp
        import numpy as np
        B, C, H, W = (32, 64, 64, 64)
        STRIDE, HEADS = (4, 8)

        def _ln(x, w, b):
            mu = x.mean(-1, keepdims=True)
            var = ((x - mu) ** 2).mean(-1, keepdims=True)
            return (x - mu) * jax.lax.rsqrt(var + 1e-05) * w + b
        s = conv_stride
        b, c, hh, ww = features.shape
        h, w = (hh // s, ww // s)
        hw, n, d = (h * w, s * s, c // num_heads)
        scale = c ** (-0.5)
        x = features.reshape(b, c, h, s, w, s)
        reduce_feats = x.mean((3, 5)).reshape(b, c, hw).transpose(0, 2, 1)
        unf = x.transpose(0, 1, 2, 4, 3, 5).reshape(b, c, hw, n).transpose(0, 2, 3, 1)
        q = _ln(reduce_feats, ln_q_w, ln_q_b) @ Wq.T
        q = q.reshape(b, hw, num_heads, d).transpose(0, 2, 1, 3)
        kv = _ln(unf, ln_kv_w, ln_kv_b) @ Wkv.T
        kv = kv.reshape(b, hw, n, 2, num_heads, d).transpose(3, 0, 4, 1, 2, 5)
        k, v = (kv[0], kv[1])
        attn = jax.nn.softmax(jnp.einsum('bhpd,bhpnd->bhpn', q * scale, k), axis=-1)
        aggre = jnp.einsum('bhpn,bhpnd->bhpd', attn, v)
        aggre = aggre.transpose(0, 2, 1, 3).reshape(b, hw, c)
        return reduce_feats + aggre @ proj_w.T + proj_b

    def _L0_attn_ref(x, W_qkv, b_qkv, W_out, b_out):
        import math
        import jax, jax.numpy as jnp
        import numpy as np
        EPS_DIV = 1e-07
        EPS_NORM = 1e-12

        def _l2_normalize(x, axis):
            n = jnp.sqrt(jnp.sum(x * x, axis=axis, keepdims=True))
            return x / jnp.maximum(n, EPS_NORM)
        b, N, C = x.shape
        qkv = x @ W_qkv + b_qkv
        q, k, v = jnp.split(qkv, 3, axis=2)
        q = q - jnp.mean(q, axis=2, keepdims=True)
        k = k - jnp.mean(k, axis=2, keepdims=True)
        q2 = q * q
        k2 = k * k
        q2s = jnp.sum(q2, axis=2, keepdims=True)
        k2s = jnp.sum(k2, axis=2, keepdims=True)
        k2 = _l2_normalize(k2 / (k2s + EPS_DIV), axis=-2)
        q2 = _l2_normalize(q2 / (q2s + EPS_DIV), axis=-1)
        kv = jnp.einsum('bnc,bnd->bcd', k2, v)
        t2 = jnp.einsum('bnc,bcd->bnd', q2, kv) / math.sqrt(N)
        attn = v + t2
        return attn @ W_out + b_out

    def _L0_ffn_ref(x, ln1_w, ln2_w, wq, wk, wv, wo, router_w, w1, w2, w3):
        import jax, jax.numpy as jnp
        import numpy as np
        B, T, C = (64, 96, 64)
        NH, NKV = (4, 2)
        HD = C // NH
        NREP = NH // NKV
        NE, TOPK = (8, 2)
        HID = int(8 / 3 * C)
        EPS_RMS = 1e-06

        def _rope_tables(t_len):
            inv_freq = 1.0 / 10000.0 ** (np.arange(0, HD, 2, dtype=np.float32) / HD)
            t = np.arange(t_len, dtype=np.float32)
            freqs = np.outer(t, inv_freq)
            emb = np.concatenate([freqs, freqs], axis=-1)
            return (jnp.asarray(np.cos(emb)), jnp.asarray(np.sin(emb)))

        def _rotate_half(x):
            h = x.shape[-1] // 2
            return jnp.concatenate([-x[..., h:], x[..., :h]], axis=-1)

        def _rmsnorm(v, w):
            return v * jax.lax.rsqrt(jnp.mean(v * v, axis=-1, keepdims=True) + EPS_RMS) * w
        Bx, Tx, Cx = x.shape
        h = _rmsnorm(x, ln1_w)
        q = (h @ wq.T).reshape(Bx, Tx, NH, HD).transpose(0, 2, 1, 3)
        k = (h @ wk.T).reshape(Bx, Tx, NKV, HD).transpose(0, 2, 1, 3)
        v = (h @ wv.T).reshape(Bx, Tx, NKV, HD).transpose(0, 2, 1, 3)
        cos, sin = _rope_tables(Tx)
        cos, sin = (cos[None, None], sin[None, None])
        q = q * cos + _rotate_half(q) * sin
        k = k * cos + _rotate_half(k) * sin
        k = jnp.repeat(k, NREP, axis=1)
        v = jnp.repeat(v, NREP, axis=1)
        scores = jnp.einsum('bhtd,bhsd->bhts', q, k) / jnp.sqrt(jnp.float32(HD))
        causal = jnp.tril(jnp.ones((Tx, Tx), dtype=bool))
        scores = jnp.where(causal[None, None], scores, jnp.float32(-1e+30))
        att = jax.nn.softmax(scores, axis=-1)
        y = jnp.einsum('bhts,bhsd->bhtd', att, v).transpose(0, 2, 1, 3).reshape(Bx, Tx, Cx)
        x = x + y @ wo.T
        flat = _rmsnorm(x, ln2_w).reshape(-1, Cx)
        probs = jax.nn.softmax(flat @ router_w.T, axis=-1)
        tp, ti = jax.lax.top_k(probs, TOPK)
        tp = tp / (jnp.sum(tp, axis=-1, keepdims=True) + 1e-09)
        weights = jnp.sum(tp[..., None] * jax.nn.one_hot(ti, NE, dtype=flat.dtype), axis=1)
        out = jnp.zeros_like(flat)
        for e in range(NE):
            hh = jax.nn.silu(flat @ w1[e].T) * (flat @ w3[e].T)
            out = out + weights[:, e:e + 1] * (hh @ w2[e].T)
        return x + out.reshape(Bx, Tx, Cx)
    h = _L0_tok_ref(x, L0_tok_ln_q_w, L0_tok_ln_q_b, L0_tok_Wq, L0_tok_ln_kv_w, L0_tok_ln_kv_b, L0_tok_Wkv, L0_tok_proj_w, L0_tok_proj_b, 4, 8)
    h = h + _L0_attn_ref(_layernorm(h, axis=-1), L0_attn_W_qkv, L0_attn_b_qkv, L0_attn_W_out, L0_attn_b_out)
    h = h + _L0_ffn_ref(_layernorm(h, axis=-1), L0_ffn_ln1_w, L0_ffn_ln2_w, L0_ffn_wq, L0_ffn_wk, L0_ffn_wv, L0_ffn_wo, L0_ffn_router_w, L0_ffn_w1, L0_ffn_w2, L0_ffn_w3)
    return h

_drawn_inputs = setup_inputs


def setup_inputs(seed=0):
    import zlib

    import numpy as np

    out = dict(_drawn_inputs(seed))
    spreads = {'L0_tok_ln_q_w': (1.0, 0.6),
     'L0_tok_ln_q_b': (0.0, 0.8),
     'L0_tok_ln_kv_w': (1.0, 0.6),
     'L0_tok_ln_kv_b': (0.0, 0.307),
     'L0_tok_proj_b': (0.0, 0.1),
     'L0_ffn_ln1_w': (1.0, 0.6),
     'L0_ffn_ln2_w': (1.0, 0.6)}
    factors = {'L0_tok_Wq': 8.0,
     'L0_attn_b_out': 4.676,
     'L0_ffn_wq': 8.0,
     'L0_ffn_wk': 8.0,
     'L0_ffn_wv': 6.884,
     'L0_ffn_wo': 4.413,
     'L0_ffn_router_w': 8.0,
     'L0_ffn_w1': 8.0,
     'L0_ffn_w2': 8.0,
     'L0_ffn_w3': 8.0}
    for name, (base, spread) in spreads.items():
        noise = np.random.default_rng([zlib.crc32(name.encode()), seed]).standard_normal(out[name].shape)
        drawn = base * np.exp(spread * noise) if base else spread * noise
        out[name] = jnp.asarray(drawn.astype(out[name].dtype))
    for name, factor in factors.items():
        out[name] = (out[name] * factor).astype(out[name].dtype)
    return out
```

```python
from contextlib import ExitStack

import concourse.bass as bass
from concourse import mybir

F32 = mybir.dt.float32
F32R = mybir.dt.float32r
BF16 = mybir.dt.bfloat16
ALU = mybir.AluOpType
ACT = mybir.ActivationFunctionType
AX = mybir.AxisListType

IMAGES, CH, SIDE, PATCH, HEADS = 128, 64, 64, 4, 8
PAIRS = IMAGES // 2
PIX = SIDE * SIDE
NPATCH = PIX // PATCH ** 2
CHUNKS = PIX // 512
LN_EPS = 1e-5


def columns(*parts):
    at, out = 0, {}
    for name, width in parts:
        out[name] = at
        at += width
    out["end"] = at
    return out


A_W = columns(("wkv", 128), ("wv_swapped", 128), ("proj", 128), ("wq", 128), ("lnkv_w", 1), ("lnkv_b", 1),
              ("lnq_w", 1), ("lnq_b", 1), ("proj_b", 1))
A_C = columns(("centre", 128), ("mean", 128), ("mean0", 32), ("mean1", 32), ("head0", 32), ("head1", 32),
              ("spread", CHUNKS * 128))
GROUPS = PAIRS // 2
DIV_EPS, NORM_EPS = 1e-7, 1e-12
B_W = columns(("wqkv", 192), ("wv_t", 128), ("w_out", 64), ("bv_rep", 128), ("bias", 192), ("b_out", 64))
B_C = columns(("ident", 128), ("centre", 128), ("ones", 1))
RMS_EPS = 1e-6
C_W = columns(("w_in", 448), ("wo", 128), ("router", 16), ("ln1_w", 1), ("ln2_w", 1))
C_C = columns(("ident", 128), ("mask", 1024), ("rope_q", 256), ("rope_kc", 256), ("rope_ks", 256), ("lower", 64))


EXPERTS, HIDDEN = 8, int(8 / 3 * 64)
TAIL = HIDDEN - 128
PER_TAIL = 128 // TAIL
TAIL_EXPERTS = [list(range(e, min(e + PER_TAIL, EXPERTS))) for e in range(0, EXPERTS, PER_TAIL)]
UNITS = len(TAIL_EXPERTS) + EXPERTS
D_W = columns(("w1", UNITS * 128), ("w3", UNITS * 128), ("w2", 2 * EXPERTS * 64))


def new_semaphore(nc, held, name):
    held.append(nc.alloc_semaphore(name=name))
    return held[-1]


def tokenize_phase(nc, held, x, wpack, cpack, h1_out):
    with ExitStack() as ctx:
        def sb(name, shape, dt=F32):
            return ctx.enter_context(nc.sbuf_tensor(name, shape, dt))

        def sem(name):
            return new_semaphore(nc, held, name)

        wsb = sb("a_wsb", [128, A_W["end"]])
        csb = sb("a_csb", [128, A_C["end"]])

        def w(name, width):
            return wsb[:, A_W[name]:A_W[name] + width]

        def c(name, width):
            return csb[:, A_C[name]:A_C[name] + width]

        kv_fold = sb("a_kv_fold", [128, 128])
        kv_w = sb("a_kv_w", [128, 128])
        spread_heads = sb("a_spread_heads", [128, CHUNKS * 128], F32R)
        v_bias = sb("a_v_bias", [128, 1])
        proj_bias = sb("a_proj_bias", [128, 1])
        lnq_w16 = sb("a_lnq_w16", [128, 1])
        eps = sb("a_eps", [128, 1])
        LNV = sb("a_lnv", [128, 512])
        LNQ = sb("a_lnq", [128, NPATCH])

        X = [sb(f"a_x{k}", [128, PIX]) for k in range(4)]
        XSQ = [sb(f"a_xsq{k}", [128, PIX]) for k in range(2)]
        T1 = sb("a_pool1", [128, PIX // 2])
        T2 = sb("a_pool2", [128, PIX // 4])
        T3 = sb("a_pool3", [128, PIX // 8])
        SUM = [sb(f"a_sum{k}", [128, NPATCH]) for k in range(4)]
        CEN = sb("a_cen", [128, NPATCH])
        CSQ = sb("a_csq", [128, NPATCH])
        SDQ = sb("a_sdq", [128, NPATCH])
        RSQ = sb("a_rsq", [128, NPATCH])
        XN = sb("a_xn", [128, NPATCH])
        XA = sb("a_xa", [128, NPATCH])
        Q = [sb(f"a_q{k}", [128, NPATCH]) for k in range(2)]
        PROD = sb("a_prod", [128, PIX])
        MSQ = sb("a_msq", [128, 512])
        VAR = sb("a_var", [128, 512])
        SDP = sb("a_sdp", [128, 512])
        RSTD = [sb(f"a_rstd{k}", [128, 512]) for k in range(2)]
        LG = sb("a_lg", [128, 512])
        MX = sb("a_mx", [128, 32])
        LS = sb("a_ls", [128, 512])
        EX = sb("a_ex", [128, 512])
        ZS = sb("a_zs", [128, 32])
        RZ = sb("a_rz", [128, 32])
        ER = sb("a_er", [128, 512])
        WT = sb("a_wt", [128, 512])
        WHI = sb("a_whi", [128, 512], F32R)
        WLO = sb("a_wlo", [128, 512], F32R)
        WBC = [sb(f"a_wbc{k}", [128, 512]) for k in range(2)]
        VW = [sb(f"a_vw{k}", [128, 512]) for k in range(2)]
        AG = [sb(f"a_ag{k}", [128, NPATCH]) for k in range(2)]
        PJ = sb("a_pj", [128, NPATCH])
        H1 = [sb(f"a_h1_{k}", [128, NPATCH]) for k in range(2)]

        def bank(name):
            return ctx.enter_context(nc.psum_tensor(name, [128, 512], F32))

        pK = [bank("a_pk0"), bank("a_pk1")]
        pV = [bank("a_pv0"), bank("a_pv1")]
        pB0, pMU, pEX, pM = (bank(n) for n in ("a_pb0", "a_pmu", "a_pex", "a_pm"))
        pB = [pB0, pEX]
        pL = pMU

        names = ("consts_loaded prep_dve prep_pe prep_act prep_pool k_ready v_ready wbc_ready prod_ready log_ready vw_ready "
                 "ag_ready wbc_copied stats_ready mean_ready varq_ready qproj_ready pj_mm xsq_ready sum_step "
                 "sum_ready er_ready cen_ready rsq_ready xn_ready csq_ready lnq_ready lnv_ready xa_ready q_ready msq_ready "
                 "var_ready sdp_ready rstd_ready logit_ready max_ready shift_ready exp_ready z_ready rz_ready "
                 "wt_ready whi_ready wlo_ready pj_ready h1_ready").split()
        S = {n: sem("a_" + n) for n in names}
        x_loaded = [sem(f"a_x_loaded{k}") for k in range(4)]
        h1_stored = [sem(f"a_h1_stored{k}") for k in range(2)]

        LAG = 2
        x_view = x.rearrange("(i m) c h w -> i (m c) (h w)", m=2)

        def wait(eng, name, value):
            if not isinstance(value, int) or value > 0:
                eng.wait_ge(S[name], value)

        def has(t):
            return not isinstance(t, int) or 0 <= t < PAIRS

        def run_steps(eng, step):
            for t in range(4):
                step(t, t)
            with eng.Fori(0, PAIRS // 4 - 2) as j:
                for u in range(4):
                    step(4 * j + (4 + u), u)
            for t in range(PAIRS - 4, PAIRS + 1):
                step(t, t % 4)

        def x_wait(eng, t, u):
            eng.wait_ge(x_loaded[u], 4 * (t - u) + 16)

        def patch_row(ap, row):
            return ap[:, row * 256:(row + 1) * 256].rearrange("p (s w t) -> p w s t", s=4, w=16, t=4)

        def by_patch(ap):
            return ap.rearrange("p (q n) -> p q n", n=16)

        def over_pixels(ap):
            return ap.unsqueeze(2).broadcast_to([128, 32, 16])

        block = ctx.enter_context(nc.Block())

        @block.sync
        def _(sp):
            sp.dma_start(wsb[:], wpack).then_inc(S["consts_loaded"], 16)
            sp.dma_start(csb[:], cpack).then_inc(S["consts_loaded"], 16)

            def load(t, u):
                wait(sp, "v_ready", CHUNKS * (t - 3))
                sp.dma_start(X[u][:], x_view[bass.ds(t, 1)].rearrange("o p f -> (o p) f")).then_inc(x_loaded[u], 16)

            def store(t, u):
                sp.wait_ge(S["h1_ready"], t + 1)
                sp.dma_start(h1_out[bass.ds(t, 1)].rearrange("o p f -> (o p) f"), H1[u % 2][:]).then_inc(h1_stored[u % 2], 16)

            for t in range(3):
                load(t, t)

            def step(t, u):
                if has(t + 3):
                    load(t + 3, (u + 3) % 4)
                if has(t - 2):
                    store(t - 2, (u + 2) % 4)

            run_steps(sp, step)
            store(PAIRS - 1, 3)
            for k in range(2):
                sp.wait_ge(h1_stored[k], 16 * PAIRS // 2)

        @block.gpsimd
        def _(pool):
            nc.gpsimd.memset(eps[:], LN_EPS).then_inc(S["prep_pool"], 1)

            def sums(t, u):
                x_wait(pool, t, u)
                wait(pool, "sum_ready", t)
                x4 = X[u][:].rearrange("p (a s f) -> p a s f", s=4, f=64)
                t1 = T1[:].rearrange("p (a s f) -> p a s f", s=2, f=64)
                t2 = T2[:].rearrange("p (q n) -> p q n", n=4)
                t3 = T3[:].rearrange("p (q n) -> p q n", n=2)
                nc.gpsimd.tensor_tensor(t1, x4[:, :, 0:2], x4[:, :, 2:4], ALU.add).then_inc(S["sum_step"], 1)
                pool.wait_ge(S["sum_step"], 3 * t + 1)
                nc.gpsimd.tensor_tensor(T2[:].rearrange("p (a f) -> p a f", f=64), t1[:, :, 0], t1[:, :, 1],
                                        ALU.add).then_inc(S["sum_step"], 1)
                pool.wait_ge(S["sum_step"], 3 * t + 2)
                nc.gpsimd.tensor_tensor(t3, t2[:, :, 0:2], t2[:, :, 2:4], ALU.add).then_inc(S["sum_step"], 1)
                pool.wait_ge(S["sum_step"], 3 * t + 3)
                wait(pool, "h1_ready", t - 3)
                nc.gpsimd.tensor_tensor(SUM[u][:], t3[:, :, 0], t3[:, :, 1], ALU.add).then_inc(S["sum_ready"], 1)

            def weigh(t, u):
                pool.wait_ge(S["exp_ready"], t + 1)
                pool.wait_ge(S["rstd_ready"], t + 1)
                wait(pool, "wt_ready", t)
                nc.gpsimd.tensor_tensor(ER[:], EX[:], RSTD[u % 2][:], ALU.mult).then_inc(S["er_ready"], 1)

            sums(0, 0)
            sums(1, 1)

            def step(t, u):
                if has(t + 2):
                    sums(t + 2, (u + 2) % 4)
                if has(t):
                    weigh(t, u)

            run_steps(pool, step)

        @block.scalar
        def _(act):
            act.wait_ge(S["consts_loaded"], 32)
            act.wait_ge(S["prep_pool"], 1)
            nc.scalar.activation(spread_heads[:], c("spread", CHUNKS * 128), ACT.Copy).then_inc(S["prep_act"], 1)
            act.wait_ge(S["prep_pe"], 1)
            nc.scalar.activation(kv_w[:], pM[:, 0:128], ACT.Copy).then_inc(S["prep_act"], 1)
            act.wait_ge(S["prep_pe"], 2)
            nc.scalar.activation(v_bias[:], pB0[:, 0:1], ACT.Copy).then_inc(S["prep_act"], 1)
            act.wait_ge(S["prep_pe"], 3)
            nc.scalar.activation(proj_bias[:], pB0[:, 2:3], ACT.Identity, bias=w("proj_b", 1)).then_inc(S["prep_act"], 1)
            act.wait_ge(S["prep_act"], 4)
            act.wait_ge(S["prep_dve"], 2)

            def squares(t, u):
                x_wait(act, t, u)
                wait(act, "stats_ready", t - 1)
                for h in range(2):
                    a = slice(h * PIX // 2, (h + 1) * PIX // 2)
                    nc.scalar.activation(XSQ[u % 2][:, a], X[u][:, a], ACT.Square).then_inc(S["xsq_ready"], 1)

            def q_squares(t):
                act.wait_ge(S["cen_ready"], t + 1)
                nc.scalar.activation(CSQ[:], CEN[:], ACT.Square, scale=1.0 / 16).then_inc(S["csq_ready"], 1)

            def q_log(t):
                act.wait_ge(S["varq_ready"], t + 1)
                wait(act, "rsq_ready", t)
                nc.scalar.activation(LNQ[:], pM[:, 256:512], ACT.Ln, bias=eps[:]).then_inc(S["lnq_ready"], 1)

            def pixel_log(t):
                act.wait_ge(S["sdp_ready"], t + 1)
                wait(act, "rstd_ready", t)
                nc.scalar.activation(LNV[:], SDP[:], ACT.Ln).then_inc(S["lnv_ready"], 1)

            def q_rsd(t):
                act.wait_ge(S["lnq_ready"], t + 1)
                wait(act, "xn_ready", t)
                nc.scalar.activation(RSQ[:], LNQ[:], ACT.Exp, scale=-0.5).then_inc(S["rsq_ready"], 1)

            def pixel_rstd(t, u):
                act.wait_ge(S["lnv_ready"], t + 1)
                wait(act, "er_ready", t - 1)
                wait(act, "logit_ready", t - 1)
                nc.scalar.activation(RSTD[u % 2][:], LNV[:], ACT.Exp, scale=-0.5).then_inc(S["rstd_ready"], 1)

            def q_affine(t):
                act.wait_ge(S["xn_ready"], t + 1)
                wait(act, "qproj_ready", t)
                nc.scalar.activation(XA[:], XN[:], ACT.Identity, bias=w("lnq_b", 1), scale=lnq_w16[:]).then_inc(S["xa_ready"], 1)

            def q_copy(t, u):
                act.wait_ge(S["qproj_ready"], t + 1)
                wait(act, "prod_ready", CHUNKS * (t - 1))
                nc.scalar.activation(Q[u % 2][:], pM[:, 0:256], ACT.Copy, scale=64.0 ** -0.5).then_inc(S["q_ready"], 1)

            def mean_squares(t):
                act.wait_ge(S["stats_ready"], t + 1)
                wait(act, "var_ready", t)
                nc.scalar.activation(MSQ[:], pMU[:], ACT.Square).then_inc(S["msq_ready"], 1)

            def project_out(t):
                act.wait_ge(S["pj_mm"], t + 1)
                wait(act, "h1_ready", t)
                nc.scalar.activation(PJ[:], pM[:, 256:512], ACT.Identity, bias=proj_bias[:]).then_inc(S["pj_ready"], 1)

            def spread(t, g):
                act.wait_ge(S["wbc_ready"], CHUNKS * t + (g + 1))
                wait(act, "vw_ready", CHUNKS * t + (g - 1))
                nc.scalar.activation(WBC[g % 2][:], pB[g % 2][:], ACT.Copy).then_inc(S["wbc_copied"], 1)

            def exponent(t):
                act.wait_ge(S["shift_ready"], t + 1)
                wait(act, "wt_ready", t)
                nc.scalar.activation(EX[:], LS[:], ACT.Exp).then_inc(S["exp_ready"], 1)

            def weights_hi(t):
                act.wait_ge(S["wt_ready"], t + 1)
                wait(act, "wbc_ready", CHUNKS * t)
                nc.scalar.activation(WHI[:], WT[:], ACT.Copy).then_inc(S["whi_ready"], 1)

            squares(0, 0)
            q_squares(0)
            q_log(0)
            q_rsd(0)
            q_affine(0)
            q_copy(0, 0)
            squares(1, 1)

            def step(t, u):
                if has(t - 2):
                    project_out(t - 2)
                if has(t):
                    mean_squares(t)
                for g in range(CHUNKS + LAG):
                    if has(t - 1) and g >= LAG:
                        spread(t - 1, g - LAG)
                    if has(t + 1):
                        if g == 1:
                            q_squares(t + 1)
                        if g == 4:
                            q_log(t + 1)
                        if g == 6:
                            q_affine(t + 1)
                        if g == 8:
                            q_copy(t + 1, u + 1)
                    if g == 4:
                        if has(t):
                            pixel_log(t)
                        if has(t + 1):
                            q_rsd(t + 1)
                        if has(t):
                            pixel_rstd(t, u)
                    if g == 5 and has(t + 2):
                        squares(t + 2, (u + 2) % 4)
                if has(t):
                    exponent(t)
                    weights_hi(t)

            run_steps(act, step)
            project_out(PAIRS - 1)

        @block.tensor
        def _(pe):
            pe.wait_ge(S["consts_loaded"], 32)
            pe.wait_ge(S["prep_dve"], 1)
            nc.tensor.matmul(pM[:, 0:128], c("centre", 128), kv_fold[:], start=True, stop=True).then_inc(S["prep_pe"], 1)
            nc.tensor.matmul(pB0[:, 0:1], w("wv_swapped", 128), w("lnkv_b", 1), start=True, stop=True).then_inc(S["prep_pe"], 1)
            pe.wait_ge(S["prep_act"], 3)
            nc.tensor.matmul(pB0[:, 2:3], w("proj", 128), v_bias[:], start=True, stop=True).then_inc(S["prep_pe"], 1)
            pe.wait_ge(S["prep_act"], 4)

            def q_mean(t, u):
                pe.wait_ge(S["sum_ready"], t + 1)
                wait(pe, "pj_ready", t - 2)
                wait(pe, "q_ready", t)
                nc.tensor.matmul(pM[:, 0:256], c("mean", 128), SUM[u][:], start=True, stop=True).then_inc(S["mean_ready"], 1)

            def q_var(t):
                pe.wait_ge(S["csq_ready"], t + 1)
                nc.tensor.matmul(pM[:, 256:512], c("mean", 128), CSQ[:], start=True, stop=True).then_inc(S["varq_ready"], 1)

            def q_project(t):
                pe.wait_ge(S["xa_ready"], t + 1)
                nc.tensor.matmul(pM[:, 0:256], w("wq", 128), XA[:], start=True, stop=True).then_inc(S["qproj_ready"], 1)

            def statistics(t, u):
                x_wait(pe, t, u)
                pe.wait_ge(S["xsq_ready"], 2 * t + 2)
                wait(pe, "var_ready", t)
                wait(pe, "wbc_copied", CHUNKS * (t - 1))
                wait(pe, "logit_ready", t)
                for src, dst in ((XSQ[u % 2], pEX), (X[u], pMU)):
                    for sub in range(2):
                        for r in range(2):
                            for q in range(4):
                                last = nc.tensor.matmul(
                                    dst[32 * q:32 * q + 32, 256 * r:256 * r + 256], c(f"mean{sub}", 32),
                                    patch_row(src, 2 * (2 * q + sub) + r), start=(sub == 0 and r == 0),
                                    stop=(sub == 1), skip_group_check=True)
                last.then_inc(S["stats_ready"], 1)

            def logits(t):
                pe.wait_ge(S["prod_ready"], CHUNKS * t + CHUNKS)
                wait(pe, "var_ready", t + 1)
                for sub in range(2):
                    for q in range(4):
                        g = 2 * q + sub
                        last = nc.tensor.matmul(pL[32 * q:32 * q + 32, :], c(f"head{sub}", 32), PROD[:, 512 * g:512 * g + 512],
                                                start=(sub == 0), stop=(sub == 1))
                last.then_inc(S["log_ready"], 1)

            def keys_values(t, u, p):
                g = p - LAG
                k, v = has(t) and p < CHUNKS, has(t - 1) and g >= 0
                if k and p >= 2:
                    wait(pe, "prod_ready", CHUNKS * t + (p - 1))
                if v:
                    wait(pe, "vw_ready", CHUNKS * t + (g - CHUNKS - 1))
                    spread_weights(t - 1, g)
                for r in range(2):
                    o = slice(256 * r, 256 * r + 256)
                    if k:
                        for i in (0, 64):
                            last_k = nc.tensor.matmul(pK[p % 2][i:i + 64, o], kv_w[i:i + 64, 0:64],
                                                      patch_row(X[u], 2 * p + r)[i:i + 64], start=True, stop=True)
                    if v:
                        for i in (0, 64):
                            last_v = nc.tensor.matmul(pV[g % 2][64 - i:128 - i, o], kv_w[i:i + 64, 64:128],
                                                      patch_row(X[(u + 3) % 4], 2 * g + r)[i:i + 64], start=True, stop=True)
                if k:
                    last_k.then_inc(S["k_ready"], 1)
                if v:
                    last_v.then_inc(S["v_ready"], 1)

            def spread_weights(t, g):
                if g == 0:
                    pe.wait_ge(S["whi_ready"], t + 1)
                    pe.wait_ge(S["wlo_ready"], t + 1)
                wait(pe, "wbc_copied", CHUNKS * t + (g - 1))
                if g == 1:
                    wait(pe, "var_ready", t + 2 if has(t + 1) else PAIRS)
                rows = spread_heads[:, 128 * g:128 * g + 128]
                nc.tensor.matmul(pB[g % 2][:], rows, WHI[:], start=True, stop=False)
                nc.tensor.matmul(pB[g % 2][:], rows, WLO[:], start=False, stop=True).then_inc(S["wbc_ready"], 1)

            def project(t, u):
                pe.wait_ge(S["ag_ready"], CHUNKS * t + CHUNKS)
                wait(pe, "q_ready", t + 3 if has(t + 2) else PAIRS)
                nc.tensor.matmul(pM[:, 256:512], w("proj", 128), AG[u % 2][:], start=True, stop=True).then_inc(S["pj_mm"], 1)

            q_mean(0, 0)
            statistics(0, 0)
            q_var(0)
            q_project(0)

            def step(t, u):
                for g in range(CHUNKS + LAG):
                    keys_values(t, u, g)
                    if has(t + 1):
                        if g == 0:
                            q_mean(t + 1, (u + 1) % 4)
                        if g == 3:
                            q_var(t + 1)
                        if g == 7:
                            q_project(t + 1)
                if has(t):
                    logits(t)
                if has(t + 1):
                    statistics(t + 1, (u + 1) % 4)
                if has(t - 1):
                    project(t - 1, u + 3)

            run_steps(pe, step)

        @block.vector
        def _(dve):
            dve.wait_ge(S["consts_loaded"], 32)
            nc.vector.tensor_scalar(kv_fold[:], w("wkv", 128), w("lnkv_w", 1), None, ALU.mult).then_inc(S["prep_dve"], 1)
            nc.vector.tensor_scalar(lnq_w16[:], w("lnq_w", 1), 1.0 / 16, None, ALU.mult).then_inc(S["prep_dve"], 1)

            def q_centre(t, u):
                dve.wait_ge(S["mean_ready"], t + 1)
                wait(dve, "csq_ready", t)
                wait(dve, "xn_ready", t)
                nc.vector.tensor_tensor(CEN[:], SUM[u][:], pM[:, 0:256], ALU.subtract).then_inc(S["cen_ready"], 1)

            def q_norm(t):
                dve.wait_ge(S["rsq_ready"], t + 1)
                wait(dve, "xa_ready", t)
                nc.vector.tensor_tensor(XN[:], CEN[:], RSQ[:], ALU.mult).then_inc(S["xn_ready"], 1)

            def pixel_var(t):
                dve.wait_ge(S["msq_ready"], t + 1)
                wait(dve, "sdp_ready", t)
                nc.vector.tensor_tensor(VAR[:], pEX[:], MSQ[:], ALU.subtract).then_inc(S["var_ready"], 1)
                dve.wait_ge(S["var_ready"], t + 1)
                wait(dve, "rstd_ready", t)
                nc.vector.tensor_scalar(SDP[:], VAR[:], 0.0, LN_EPS, ALU.max, ALU.add).then_inc(S["sdp_ready"], 1)

            def products(t, u, g):
                dve.wait_ge(S["k_ready"], CHUNKS * t + (g + 1))
                if g == 0:
                    dve.wait_ge(S["q_ready"], t + 1)
                    wait(dve, "log_ready", t)
                nc.vector.tensor_tensor(by_patch(PROD[:, 512 * g:512 * g + 512]), by_patch(pK[g % 2][:]),
                                        over_pixels(Q[u % 2][:, 32 * g:32 * g + 32]), ALU.mult).then_inc(S["prod_ready"], 1)

            def values(t, g):
                dve.wait_ge(S["v_ready"], CHUNKS * t + (g + 1))
                dve.wait_ge(S["wbc_copied"], CHUNKS * t + (g + 1))
                wait(dve, "ag_ready", CHUNKS * t + (g - 1))
                nc.vector.tensor_tensor(VW[g % 2][:], pV[g % 2][:], WBC[g % 2][:], ALU.mult).then_inc(S["vw_ready"], 1)

            def value_sums(t, u, g):
                dve.wait_ge(S["vw_ready"], CHUNKS * t + (g + 1))
                if g == 0:
                    wait(dve, "pj_mm", t - 1)
                nc.vector.tensor_reduce(AG[u % 2][:, 32 * g:32 * g + 32], by_patch(VW[g % 2][:]), AX.X,
                                        ALU.add).then_inc(S["ag_ready"], 1)

            def h1_sum(t, u):
                dve.wait_ge(S["pj_ready"], t + 1)
                if not isinstance(t, int) or t >= 2:
                    dve.wait_ge(h1_stored[u % 2], 8 * (t - u % 2))
                nc.vector.scalar_tensor_tensor(H1[u % 2][:], SUM[u % 4][:], 1.0 / 16, PJ[:], ALU.mult,
                                               ALU.add).then_inc(S["h1_ready"], 1)

            def softmax_logits(t, u):
                dve.wait_ge(S["log_ready"], t + 1)
                dve.wait_ge(S["rstd_ready"], t + 1)
                wait(dve, "shift_ready", t)
                nc.vector.tensor_tensor(LG[:], pL[:], RSTD[u % 2][:], ALU.mult).then_inc(S["logit_ready"], 1)
                dve.wait_ge(S["logit_ready"], t + 1)
                nc.vector.tensor_reduce(MX[:], by_patch(LG[:]), AX.X, ALU.max).then_inc(S["max_ready"], 1)
                dve.wait_ge(S["max_ready"], t + 1)
                wait(dve, "exp_ready", t)
                nc.vector.tensor_tensor(by_patch(LS[:]), by_patch(LG[:]), over_pixels(MX[:]),
                                        ALU.subtract).then_inc(S["shift_ready"], 1)

            def softmax_weights(t):
                dve.wait_ge(S["exp_ready"], t + 1)
                wait(dve, "rz_ready", t)
                nc.vector.tensor_reduce(ZS[:], by_patch(EX[:]), AX.X, ALU.add).then_inc(S["z_ready"], 1)
                dve.wait_ge(S["z_ready"], t + 1)
                wait(dve, "wt_ready", t)
                nc.vector.reciprocal(RZ[:], ZS[:]).then_inc(S["rz_ready"], 1)
                dve.wait_ge(S["rz_ready"], t + 1)
                dve.wait_ge(S["er_ready"], t + 1)
                wait(dve, "wlo_ready", t)
                nc.vector.tensor_tensor(by_patch(WT[:]), by_patch(ER[:]), over_pixels(RZ[:]),
                                        ALU.mult).then_inc(S["wt_ready"], 1)

            def weights_lo(t):
                dve.wait_ge(S["whi_ready"], t + 1)
                nc.vector.tensor_tensor(WLO[:], WT[:], WHI[:].bitcast(F32), ALU.subtract).then_inc(S["wlo_ready"], 1)

            q_centre(0, 0)
            q_norm(0)

            def step(t, u):
                if has(t - 2):
                    h1_sum(t - 2, u + 2)
                if has(t):
                    pixel_var(t)
                for g in range(CHUNKS + LAG):
                    if has(t) and g < CHUNKS:
                        products(t, u, g)
                    if has(t - 1) and g >= LAG:
                        values(t - 1, g - LAG)
                        if g > LAG:
                            value_sums(t - 1, u + 3, g - LAG - 1)
                    if has(t + 1):
                        if g == 0:
                            q_centre(t + 1, (u + 1) % 4)
                        if g == 5:
                            q_norm(t + 1)
                if has(t - 1):
                    value_sums(t - 1, u + 3, CHUNKS - 1)
                if has(t):
                    softmax_logits(t, u)
                    softmax_weights(t)
                    weights_lo(t)

            run_steps(dve, step)
            h1_sum(PAIRS - 1, 3)
def linear_attention_phase(nc, held, h1, wpack, cpack, h2_out):
    with ExitStack() as ctx:
        def sb(name, shape, dt=F32):
            return ctx.enter_context(nc.sbuf_tensor("b_" + name, shape, dt))

        wsb = sb("wsb", [128, B_W["end"]])
        csb = sb("csb", [128, B_C["end"]])

        def w(name, width):
            return wsb[:, B_W[name]:B_W[name] + width]

        def c(name, width):
            return csb[:, B_C[name]:B_C[name] + width]

        w_raw = sb("w_raw", [128, 256])
        w_mid = sb("w_mid", [128, 256])
        w_mean = sb("w_mean", [128, 2])
        w_all = sb("w_all", [128, 256])
        bias = sb("bias", [128, 256])
        b_mean = sb("b_mean", [128, 2])
        w_out16 = sb("w_out16", [128, 64])
        eps = sb("eps", [128, 1])

        H = [sb(f"h{k}", [128, 512]) for k in range(4)]
        HT = [sb(f"ht{k}", [128, 512]) for k in range(2)]
        HSQ = sb("hsq", [128, 512])
        S1, S2, M2, V0, V1 = (sb(n, [128, 8]) for n in ("s1", "s2", "m2", "v0", "v1"))
        SD1 = sb("sd1", [128, 8])
        RSTD = sb("rstd", [128, 8])
        QKV = [sb(f"qkv{k}", [128, 4, 4, 128]) for k in range(4)]
        Q2 = sb("q2", [128, 512])
        K2 = sb("k2", [128, 512])
        SS, SE, F = (sb(n, [128, 16]) for n in ("ss", "se", "f"))
        Q2N = [sb(f"q2n{k}", [128, 512]) for k in range(2)]
        K2N = [sb(f"k2n{k}", [128, 512]) for k in range(2)]
        VOH = [sb(f"voh{k}", [128, 512]) for k in range(2)]
        Q2S = sb("q2s", [128, 512])
        K2S = [sb(f"k2s{k}", [128, 512]) for k in range(2)]
        NQ = sb("nq", [128, 8])
        NQM = [sb(f"nqm{k}", [128, 8]) for k in range(2)]
        SDQ, RQ = sb("sdq", [128, 8]), sb("rq", [128, 8])
        QT = sb("qt", [128, 512])
        KVD = sb("kvd", [128, 2, 128])
        NKM, SDK, RK = (sb(n, [128, 2]) for n in ("nkm", "sdk", "rk"))
        MX = sb("mx", [128, 2, 128])
        O1 = sb("o1", [128, 512])
        H2 = [sb(f"h2_{k}", [128, 512]) for k in range(2)]

        def bank(name):
            return ctx.enter_context(nc.psum_tensor("b_" + name, [128, 512], F32))

        pT, pQT, pKV, pOUT = (bank(n) for n in ("pt", "pqt", "pkv", "pout"))
        pQ = [bank(f"pq{k}") for k in range(4)]

        names = ("consts_loaded prep_pe prep_act prep_dve prep_pool ht_mm qkv_mm kv_mm qt_mm m_mm out_mm "
                 "ht_ready hsq_ready sums_ready m2_ready v0_ready v1_ready sd1_ready rstd_ready qkv_ready "
                 "sq_ready ss_ready se_ready f_ready scaled_ready voh_ready q2s_ready k2s_ready nq_ready nqm_ready "
                 "sdq_ready rq_ready qt_ready kvd_ready nkm_ready sdk_ready rk_ready mx_ready o1_ready h2_ready").split()
        S = {n: new_semaphore(nc, held, "b_" + n) for n in names}
        h_loaded = [new_semaphore(nc, held, f"b_h_loaded{k}") for k in range(4)]
        h2_stored = [new_semaphore(nc, held, f"b_h2_stored{k}") for k in range(2)]

        def wait(eng, name, value):
            if not isinstance(value, int) or value > 0:
                eng.wait_ge(S[name], value)

        def has(t):
            return not isinstance(t, int) or 0 <= t < GROUPS

        def run_steps(eng, step):
            for t in range(4):
                step(t, t)
            with eng.Fori(0, GROUPS // 4 - 2) as j:
                for u in range(4):
                    step(4 * j + (4 + u), u)
            for t in range(GROUPS - 4, GROUPS + 2):
                step(t, t % 4)

        def tiles(ap):
            return ap.rearrange("p (k c) -> p k c", c=64)

        def by_half(ap):
            return ap.rearrange("p (q c) -> p q c", c=128)

        def each(ap, n=64):
            return ap.unsqueeze(2).broadcast_to([128, ap.shape[1], n])

        h1_view = h1.rearrange("(s j) p f -> s p j f", j=2)

        block = ctx.enter_context(nc.Block())

        @block.sync
        def _(sp):
            sp.dma_start(wsb[:], wpack).then_inc(S["consts_loaded"], 16)
            sp.dma_start(csb[:], cpack).then_inc(S["consts_loaded"], 16)

            def load(t, u):
                wait(sp, "qkv_mm", 2 * (t - 3))
                sp.dma_start(H[u][:].rearrange("p (j f) -> p j f", j=2),
                             h1_view[bass.ds(t, 1)].rearrange("o p j f -> (o p) j f")).then_inc(h_loaded[u], 16)

            def store(t, u):
                sp.wait_ge(S["h2_ready"], t + 1)
                sp.dma_start(h2_out[bass.ds(t, 1)].rearrange("o p f -> (o p) f"), H2[u % 2][:]).then_inc(h2_stored[u % 2], 16)

            for t in range(3):
                load(t, t)

            def step(t, u):
                if has(t + 3):
                    load(t + 3, (u + 3) % 4)
                if has(t - 2):
                    store(t - 2, (u + 2) % 4)

            run_steps(sp, step)
            for k in range(2):
                sp.wait_ge(h2_stored[k], 16 * GROUPS // 2)

        @block.gpsimd
        def _(pool):
            nc.gpsimd.memset(eps[:], LN_EPS).then_inc(S["prep_pool"], 1)
            nc.gpsimd.memset(KVD[:], 0.0).then_inc(S["prep_pool"], 1)
            nc.gpsimd.memset(MX[:], 0.0).then_inc(S["prep_pool"], 1)

            def scale(t, u):
                pool.wait_ge(S["f_ready"], t + 1)
                wait(pool, "qt_mm", t - 1)
                nc.gpsimd.tensor_tensor(tiles(Q2N[u % 2][:]), tiles(Q2[:]), each(F[:, 0:8]), ALU.mult).then_inc(S["scaled_ready"], 1)
                nc.gpsimd.tensor_tensor(tiles(K2N[u % 2][:]), tiles(K2[:]), each(F[:, 8:16]), ALU.mult).then_inc(S["scaled_ready"], 1)
                wait(pool, "h2_ready", t - 1)
                nc.gpsimd.tensor_tensor(by_half(VOH[u % 2][:]), QKV[u][:, :, 3, :], by_half(HT[u % 2][:]), ALU.add).then_inc(S["voh_ready"], 1)

            def step(t, u):
                if has(t - 1):
                    scale(t - 1, (u + 3) % 4)

            run_steps(pool, step)

        @block.scalar
        def _(act):
            act.wait_ge(S["prep_pe"], 1)
            nc.scalar.activation(w_raw[:, 192:256], pQ[0][:, 0:64], ACT.Copy).then_inc(S["prep_act"], 1)
            nc.scalar.activation(w_raw[:, 0:192], w("wqkv", 192), ACT.Copy).then_inc(S["prep_act"], 1)
            act.wait_ge(S["prep_pe"], 2)
            nc.scalar.activation(w_mid[:], pQ[1][:, 0:256], ACT.Copy).then_inc(S["prep_act"], 1)
            act.wait_ge(S["prep_pool"], 3)

            def transposed(t, u):
                act.wait_ge(S["ht_mm"], t + 1)
                wait(act, "voh_ready", t - 1)
                nc.scalar.activation(HT[u % 2][:], pT[:], ACT.Copy).then_inc(S["ht_ready"], 1)
                wait(act, "sums_ready", 2 * t)
                nc.scalar.activation(HSQ[:], pT[:], ACT.Square).then_inc(S["hsq_ready"], 1)

            def squares(t, u):
                act.wait_ge(S["qkv_ready"], 8 * t + 8)
                wait(act, "scaled_ready", 2 * t)
                nc.scalar.activation(by_half(Q2[:]), QKV[u][:, :, 0, :], ACT.Square).then_inc(S["sq_ready"], 1)
                nc.scalar.activation(by_half(K2[:]), QKV[u][:, :, 1, :], ACT.Square).then_inc(S["sq_ready"], 1)

            def products_out(t):
                act.wait_ge(S["qt_mm"], t + 1)
                wait(act, "out_mm", t)
                nc.scalar.activation(QT[:], pQT[:], ACT.Copy).then_inc(S["qt_ready"], 1)
                act.wait_ge(S["kv_mm"], t + 1)
                wait(act, "m_mm", t)
                for i in range(2):
                    r = slice(64 * i, 64 * i + 64)
                    nc.scalar.activation(KVD[r, :, r], pKV[r, 0:256].rearrange("p (j c) -> p j c", j=2)[:, :, r],
                                         ACT.Copy).then_inc(S["kvd_ready"], 1)

            def fourths(t, u):
                act.wait_ge(S["scaled_ready"], 2 * t + 2)
                wait(act, "nq_ready", t)
                nc.scalar.activation(Q2S[:], Q2N[u % 2][:], ACT.Square).then_inc(S["q2s_ready"], 1)
                wait(act, "kv_mm", t - 1)
                nc.scalar.activation(K2S[u % 2][:], K2N[u % 2][:], ACT.Square).then_inc(S["k2s_ready"], 1)

            def roots(t, u):
                if has(t):
                    act.wait_ge(S["v1_ready"], t + 1)
                    wait(act, "rstd_ready", t)
                    nc.scalar.activation(SD1[:], V1[:], ACT.Sqrt, bias=eps[:]).then_inc(S["sd1_ready"], 1)
                if has(t - 2):
                    act.wait_ge(S["nqm_ready"], t - 1)
                    wait(act, "rq_ready", t - 2)
                    nc.scalar.activation(SDQ[:], NQM[u % 2][:], ACT.Sqrt).then_inc(S["sdq_ready"], 1)
                    act.wait_ge(S["nkm_ready"], t - 1)
                    wait(act, "rk_ready", t - 2)
                    nc.scalar.activation(SDK[:], NKM[:], ACT.Sqrt).then_inc(S["sdk_ready"], 1)

            def step(t, u):
                if has(t):
                    transposed(t, u)
                if has(t - 1):
                    squares(t - 1, (u + 3) % 4)
                if has(t - 2):
                    products_out(t - 2)
                roots(t, u)
                if has(t - 1):
                    fourths(t - 1, (u + 3) % 4)

            run_steps(act, step)

        @block.tensor
        def _(pe):
            pe.wait_ge(S["consts_loaded"], 32)
            nc.tensor.matmul(pQ[0][:, 0:64], wsb[0:64, B_W["wv_t"]:B_W["wv_t"] + 128], wsb[0:64, B_W["w_out"]:B_W["w_out"] + 64],
                             start=True, stop=True)
            nc.tensor.matmul(pQ[2][:, 0:64], wsb[0:64, B_W["bv_rep"]:B_W["bv_rep"] + 128], wsb[0:64, B_W["w_out"]:B_W["w_out"] + 64],
                             start=True, stop=True).then_inc(S["prep_pe"], 1)
            pe.wait_ge(S["prep_act"], 2)
            nc.tensor.matmul(pQ[1][:, 0:256], c("centre", 128), w_raw[:], start=True, stop=True).then_inc(S["prep_pe"], 1)
            pe.wait_ge(S["prep_dve"], 8)

            def transpose_in(t, u):
                pe.wait_ge(h_loaded[u], 4 * (t - u) + 16)
                wait(pe, "ht_ready", t)
                wait(pe, "hsq_ready", t)
                for q in range(4):
                    last = nc.tensor.transpose(pT[:, 128 * q:128 * q + 128], H[u][:, 128 * q:128 * q + 128], c("ident", 128))
                last.then_inc(S["ht_mm"], 1)

            def project(t, u):
                for j in range(2):
                    wait(pe, "qkv_ready", 8 * (t - 1) + 4 * j + 4)
                    for h in range(2):
                        for i in range(2):
                            r = slice(64 * i, 64 * i + 64)
                            q = 2 * j + h
                            last = nc.tensor.matmul(pQ[2 * j + i][:, 256 * h:256 * h + 256], H[u][r, 128 * q:128 * q + 128],
                                                    w_all[r, :], start=True, stop=True)
                    last.then_inc(S["qkv_mm"], 1)

            def products(t, u):
                pe.wait_ge(S["scaled_ready"], 2 * t + 2)
                wait(pe, "qt_ready", t)
                for q in range(4):
                    last = nc.tensor.transpose(pQT[:, 128 * q:128 * q + 128], Q2N[u % 2][:, 128 * q:128 * q + 128], c("ident", 128))
                last.then_inc(S["qt_mm"], 1)
                pe.wait_ge(S["k2s_ready"], t + 1)
                wait(pe, "mx_ready", 2 * t)
                for j in range(2):
                    for h in range(2):
                        q = 2 * j + h
                        nc.tensor.matmul(pKV[:, 128 * j:128 * j + 128], QKV[u][:, q, 2, :],
                                         K2N[u % 2][:, 128 * q:128 * q + 128], start=(h == 0), stop=(h == 1))
                for j in range(2):
                    for h in range(2):
                        q = 2 * j + h
                        last = nc.tensor.matmul(pKV[:, 256 + j:257 + j], K2S[u % 2][:, 128 * q:128 * q + 128], c("ones", 1),
                                                start=(h == 0), stop=(h == 1))
                last.then_inc(S["kv_mm"], 1)

            def fold_output(t):
                pe.wait_ge(S["kvd_ready"], 2 * t + 2)
                pe.wait_ge(S["nkm_ready"], t + 1)
                for j in range(2):
                    last = nc.tensor.matmul(pKV[:, 384 + 64 * j:448 + 64 * j], KVD[:, j, :], w_out16[:], start=True, stop=True)
                last.then_inc(S["m_mm"], 1)

            def outputs(t):
                pe.wait_ge(S["mx_ready"], 2 * t + 2)
                wait(pe, "o1_ready", t)
                for q in range(4):
                    last = nc.tensor.matmul(pOUT[:, 128 * q:128 * q + 128], QT[:, 128 * q:128 * q + 128], MX[:, q // 2, :],
                                            start=True, stop=True)
                last.then_inc(S["out_mm"], 1)

            def step(t, u):
                if has(t):
                    transpose_in(t, u)
                if has(t - 2):
                    products(t - 2, (u + 2) % 4)
                if has(t):
                    project(t, u)
                if has(t - 2):
                    fold_output(t - 2)
                    outputs(t - 2)

            run_steps(pe, step)

        @block.vector
        def _(dve):
            dve.wait_ge(S["consts_loaded"], 32)
            nc.vector.tensor_scalar(w_out16[:], w("w_out", 64), 1.0 / 16, None, ALU.mult).then_inc(S["prep_dve"], 1)
            bqk = w("bias", 128).rearrange("p (a c) -> p a c", a=2)
            nc.vector.tensor_reduce(b_mean[:], bqk, AX.X, ALU.add).then_inc(S["prep_dve"], 1)
            dve.wait_ge(S["prep_dve"], 2)
            nc.vector.scalar_tensor_tensor(bias[:, 0:128].rearrange("p (a c) -> p a c", a=2), each(b_mean[:]), -1.0 / 64, bqk,
                                           ALU.mult, ALU.add).then_inc(S["prep_dve"], 1)
            nc.vector.tensor_copy(bias[:, 128:192], wsb[:, B_W["bias"] + 128:B_W["bias"] + 192]).then_inc(S["prep_dve"], 1)
            dve.wait_ge(S["prep_pe"], 1)
            nc.vector.tensor_tensor(bias[:, 192:256], pQ[2][:, 0:64], w("b_out", 64), ALU.add).then_inc(S["prep_dve"], 1)
            dve.wait_ge(S["prep_act"], 3)
            wqk = w_mid[:, 0:128].rearrange("p (a c) -> p a c", a=2)
            nc.vector.tensor_reduce(w_mean[:], wqk, AX.X, ALU.add).then_inc(S["prep_dve"], 1)
            dve.wait_ge(S["prep_dve"], 6)
            nc.vector.scalar_tensor_tensor(w_all[:, 0:128].rearrange("p (a c) -> p a c", a=2), each(w_mean[:]), -1.0 / 64, wqk,
                                           ALU.mult, ALU.add).then_inc(S["prep_dve"], 1)
            nc.vector.tensor_copy(w_all[:, 128:256], w_mid[:, 128:256]).then_inc(S["prep_dve"], 1)
            dve.wait_ge(S["prep_dve"], 8)
            dve.wait_ge(S["prep_pool"], 3)

            def statistics(t, u):
                dve.wait_ge(S["ht_ready"], t + 1)
                wait(dve, "v0_ready", t)
                nc.vector.tensor_reduce(S1[:], tiles(HT[u % 2][:]), AX.X, ALU.add).then_inc(S["sums_ready"], 1)
                dve.wait_ge(S["hsq_ready"], t + 1)
                nc.vector.tensor_reduce(S2[:], tiles(HSQ[:]), AX.X, ALU.add).then_inc(S["sums_ready"], 1)
                dve.wait_ge(S["sums_ready"], 2 * t + 2)
                nc.vector.tensor_tensor(M2[:], S1[:], S1[:], ALU.mult).then_inc(S["m2_ready"], 1)
                dve.wait_ge(S["m2_ready"], t + 1)
                nc.vector.scalar_tensor_tensor(V0[:], S2[:], 64.0, M2[:], ALU.mult, ALU.subtract).then_inc(S["v0_ready"], 1)
                dve.wait_ge(S["v0_ready"], t + 1)
                wait(dve, "sd1_ready", t)
                nc.vector.tensor_scalar(V1[:], V0[:], 1.0 / 4096, 0.0, ALU.mult, ALU.max).then_inc(S["v1_ready"], 1)

            def square_sums(t):
                dve.wait_ge(S["sq_ready"], 2 * t + 2)
                wait(dve, "se_ready", t)
                nc.vector.tensor_reduce(SS[:, 0:8], tiles(Q2[:]), AX.X, ALU.add).then_inc(S["ss_ready"], 1)
                nc.vector.tensor_reduce(SS[:, 8:16], tiles(K2[:]), AX.X, ALU.add).then_inc(S["ss_ready"], 1)
                dve.wait_ge(S["ss_ready"], 2 * t + 2)
                wait(dve, "f_ready", t)
                nc.vector.tensor_scalar(SE[:], SS[:], DIV_EPS, None, ALU.add).then_inc(S["se_ready"], 1)
                dve.wait_ge(S["se_ready"], t + 1)
                wait(dve, "scaled_ready", 2 * t)
                nc.vector.reciprocal(F[:], SE[:]).then_inc(S["f_ready"], 1)

            def key_norms(t):
                dve.wait_ge(S["kvd_ready"], 2 * t + 2)
                wait(dve, "sdk_ready", t)
                nc.vector.tensor_scalar(NKM[:], pKV[:, 256:258], NORM_EPS ** 2, None, ALU.max).then_inc(S["nkm_ready"], 1)

            def query_norms(t, u):
                dve.wait_ge(S["q2s_ready"], t + 1)
                wait(dve, "nqm_ready", t)
                nc.vector.tensor_reduce(NQ[:], tiles(Q2S[:]), AX.X, ALU.add).then_inc(S["nq_ready"], 1)
                dve.wait_ge(S["nq_ready"], t + 1)
                wait(dve, "sdq_ready", t - 1)
                nc.vector.tensor_scalar(NQM[u % 2][:], NQ[:], NORM_EPS ** 2, None, ALU.max).then_inc(S["nqm_ready"], 1)

            def scale_projections(t, u):
                dve.wait_ge(S["sd1_ready"], t + 1)
                nc.vector.reciprocal(RSTD[:], SD1[:]).then_inc(S["rstd_ready"], 1)
                dve.wait_ge(S["rstd_ready"], t + 1)
                wait(dve, "voh_ready", t - 3)
                wait(dve, "kv_mm", t - 3)
                for j in range(2):
                    dve.wait_ge(S["qkv_mm"], 2 * t + (j + 1))
                    for h in range(2):
                        for i in range(2):
                            q = 2 * j + h
                            nc.vector.scalar_tensor_tensor(
                                QKV[u][:, q, :, 64 * i:64 * i + 64],
                                pQ[2 * j + i][:, 256 * h:256 * h + 256].rearrange("p (b c) -> p b c", b=4),
                                RSTD[:, 2 * q + i:2 * q + i + 1], bias[:].rearrange("p (b c) -> p b c", b=4),
                                ALU.mult, ALU.add).then_inc(S["qkv_ready"], 1)

            def fold_norms(t):
                dve.wait_ge(S["sdk_ready"], t + 1)
                nc.vector.reciprocal(RK[:], SDK[:]).then_inc(S["rk_ready"], 1)
                dve.wait_ge(S["sdq_ready"], t + 1)
                nc.vector.reciprocal(RQ[:], SDQ[:]).then_inc(S["rq_ready"], 1)
                dve.wait_ge(S["m_mm"], t + 1)
                dve.wait_ge(S["rk_ready"], t + 1)
                wait(dve, "out_mm", t)
                dve.wait_ge(S["kvd_ready"], 2 * t + 2)
                for i in range(2):
                    r = slice(64 * i, 64 * i + 64)
                    nc.vector.tensor_tensor(MX[r, :, r], pKV[r, 384:512].rearrange("p (j c) -> p j c", j=2),
                                            RK[r, :].unsqueeze(2).broadcast_to([64, 2, 64]), ALU.mult).then_inc(S["mx_ready"], 1)

            def finish(t, u):
                dve.wait_ge(S["out_mm"], t + 1)
                dve.wait_ge(S["rq_ready"], t + 1)
                wait(dve, "h2_ready", t)
                nc.vector.tensor_tensor(tiles(O1[:]), tiles(pOUT[:]), each(RQ[:]), ALU.mult).then_inc(S["o1_ready"], 1)
                dve.wait_ge(S["o1_ready"], t + 1)
                dve.wait_ge(S["voh_ready"], t + 1)
                if not isinstance(t, int) or t >= 2:
                    dve.wait_ge(h2_stored[u % 2], 8 * (t - u % 2))
                nc.vector.tensor_tensor(H2[u % 2][:], O1[:], VOH[u % 2][:], ALU.add).then_inc(S["h2_ready"], 1)

            def step(t, u):
                if has(t):
                    statistics(t, u)
                if has(t - 1):
                    square_sums(t - 1)
                if has(t - 2):
                    key_norms(t - 2)
                if has(t):
                    scale_projections(t, u)
                if has(t - 2):
                    fold_norms(t - 2)
                    finish(t - 2, u)
                if has(t - 1):
                    query_norms(t - 1, (u + 1) % 2)

            run_steps(dve, step)
def causal_attention_phase(nc, held, h2, wpack, cpack, res_out, flat_out, gates_out):
    with ExitStack() as ctx:
        def sb(name, shape, dt=F32):
            return ctx.enter_context(nc.sbuf_tensor("c_" + name, shape, dt))

        wsb = sb("wsb", [128, C_W["end"]])
        csb = sb("csb", [128, C_C["end"]])

        def w(name, width):
            return wsb[:, C_W[name]:C_W[name] + width]

        def c(name, width):
            return csb[:, C_C[name]:C_C[name] + width]

        w_in = sb("w_in", [128, 3 * 128 + 64])
        ident_b = sb("ident_b", [128, 128], BF16)
        mask_b = sb("mask_b", [128, 2, 512], BF16)
        eps_ln = sb("eps_ln", [128, 1])
        eps_rms = sb("eps_rms", [128, 1])

        H2 = [sb(f"h2_{k}", [128, 512]) for k in range(4)]
        HSQ = sb("hsq", [128, 512])
        S1, S2, M2, V0, V1, VE, RV, MU2, NM, RS, SDM, RR = (
            sb(n, [128, 8]) for n in ("s1", "s2", "m2", "v0", "v1", "ve", "rv", "mu2", "nm", "rs", "sdm", "rr"))
        U0 = sb("u0", [128, 512])
        U = [sb(f"u_{k}", [128, 512]) for k in range(4)]
        UR = [sb(f"ur{k}", [128, 512]) for k in range(2)]
        URT = sb("urt", [128, 512])
        VT = [sb(f"vt{k}", [128, 4, 64]) for k in range(2)]
        QC = [[sb(f"qc{k}_{i}", [128, 512]) for i in range(2)] for k in range(2)]
        KR = [[sb(f"kr{k}_{i}", [128, 512]) for i in range(2)] for k in range(2)]
        KC = sb("kc", [128, 512])
        KS = sb("ks", [128, 512])
        MX = [sb(f"mx{k}", [128, 4]) for k in range(3)]
        PR = [sb(f"pr{k}", [128, 512]) for k in range(2)]
        PTS = [sb(f"pts{k}", [128, 512]) for k in range(2)]
        SUM = [sb(f"sum{k}", [128, 32]) for k in range(2)]
        RSUM = sb("rsum", [128, 32])
        Y = sb("y", [128, 512])
        YT = sb("yt", [128, 512])
        X1 = sb("x1", [128, 512])
        XSQ = sb("xsq", [128, 512])
        S3, SDX, R2 = (sb(n, [128, 8]) for n in ("s3", "sdx", "r2"))
        XR = sb("xr", [128, 512])
        RES = [sb(f"res{k}", [128, 512]) for k in range(2)]
        FT = [sb(f"ft{k}", [128, 512]) for k in range(2)]
        RL, RLS, RE, RP, RK, SEL, W0 = (sb(n, [128, 64]) for n in ("rl", "rls", "re", "rp", "rk", "sel", "w0"))
        RMX, RZ, RRZ, WS, WSE, RWS = (sb(n, [128, 8]) for n in ("rmx", "rz", "rrz", "ws", "wse", "rws"))
        GT, EQ, EQM, BEFORE = (sb(n, [128, 512]) for n in ("gt", "eq", "eqm", "before"))
        G = [sb(f"g{k}", [128, 64]) for k in range(2)]

        def bank(name):
            return ctx.enter_context(nc.psum_tensor("c_" + name, [128, 512], F32))

        pS = [bank(f"ps{k}") for k in range(3)]
        pPT = [bank(f"ppt{k}") for k in range(2)]
        pY = bank("py")
        pA, pB = bank("pa"), bank("pb")

        names = ("consts_loaded prep_act prep_dve prep_pool "
                 "hsq_ready sums_ready m2_ready v0_ready v1_ready ve_ready rv_ready mu2_ready nm_ready rs_ready "
                 "sdm_ready rr_ready u0_ready u_ready ur_ready ut_mm urt_ready v_mm vt_ready q_mm qc_ready "
                 "k_mm kc_ready ks_ready kr_ready scores_ready max_ready exp_ready pt_mm pts_ready pv_mm rsum_ready "
                 "y_ready yt_mm yt_ready wo_mm x1_ready xsq_ready s3_ready sdx_ready r2_ready xr_ready res_ready "
                 "ft_mm ft_ready router_mm rl_ready rmx_ready rls_ready re_ready rz_ready rrz_ready rp_ready "
                 "gt_ready eq_ready eqm_ready before_ready rank_ready sel_ready w0_ready ws_ready wse_ready rws_ready "
                 "g_ready").split()
        S = {n: new_semaphore(nc, held, "c_" + n) for n in names}
        h_loaded = [new_semaphore(nc, held, f"c_h_loaded{k}") for k in range(4)]
        res_stored, flat_stored, gates_stored = (
            [new_semaphore(nc, held, f"c_{n}_stored{k}") for k in range(2)] for n in ("res", "flat", "gates"))

        def wait(eng, name, value):
            if not isinstance(value, int) or value > 0:
                eng.wait_ge(S[name], value)

        def has(t):
            return not isinstance(t, int) or 0 <= t < GROUPS

        def run_steps(eng, step):
            for t in range(-2, 4):
                step(t, t % 4)
            with eng.Fori(0, GROUPS // 4 - 2) as j:
                for u in range(4):
                    step(4 * j + (4 + u), u)
            for t in range(GROUPS - 4, GROUPS + 2):
                step(t, t % 4)

        def slot_wait(eng, sems, t, u):
            if not isinstance(t, int) or t >= 2:
                eng.wait_ge(sems[u % 2], 8 * (t - u % 2))

        def tiles(ap, n=64):
            return ap.rearrange("p (k c) -> p k c", c=n)

        def each(ap, n=64):
            return ap.unsqueeze(2).broadcast_to([128, ap.shape[1], n])

        block = ctx.enter_context(nc.Block())

        @block.sync
        def _(sp):
            sp.dma_start(wsb[:], wpack).then_inc(S["consts_loaded"], 16)
            sp.dma_start(csb[:], cpack).then_inc(S["consts_loaded"], 16)

            def load(t, u):
                wait(sp, "res_ready", t - 3)
                sp.dma_start(H2[u][:], h2[bass.ds(t, 1)].rearrange("o p f -> (o p) f")).then_inc(h_loaded[u], 16)

            def store(t, u):
                for name, buf, dst, sems in (("res_ready", RES, res_out, res_stored), ("ft_ready", FT, flat_out, flat_stored)):
                    sp.wait_ge(S[name], t + 1)
                    sp.dma_start(dst[bass.ds(t, 1)].rearrange("o p f -> (o p) f"), buf[u % 2][:]).then_inc(sems[u % 2], 16)

            def store_gates(t, u):
                sp.wait_ge(S["g_ready"], t + 1)
                sp.dma_start(gates_out[bass.ds(t, 1)].rearrange("o p f -> (o p) f"), G[u % 2][:]).then_inc(gates_stored[u % 2], 16)

            load(0, 0)

            def step(t, u):
                if has(t + 3):
                    load(t + 3, (u + 3) % 4)
                if has(t - 1):
                    store(t - 1, u + 3)
                if has(t - 2):
                    store_gates(t - 2, u + 2)

            run_steps(sp, step)
            for sems in (res_stored, flat_stored, gates_stored):
                for k in range(2):
                    sp.wait_ge(sems[k], 16 * GROUPS // 2)

        @block.gpsimd
        def _(pool):
            nc.gpsimd.memset(eps_ln[:], LN_EPS).then_inc(S["prep_pool"], 1)
            nc.gpsimd.memset(eps_rms[:], RMS_EPS).then_inc(S["prep_pool"], 1)

            def residual(t, u):
                pool.wait_ge(S["x1_ready"], t + 1)
                slot_wait(pool, res_stored, t, u)
                nc.gpsimd.tensor_tensor(RES[u % 2][:], H2[u][:], X1[:], ALU.add).then_inc(S["res_ready"], 1)

            def flat(t, u):
                pool.wait_ge(S["r2_ready"], t + 1)
                wait(pool, "ft_mm", t)
                nc.gpsimd.tensor_tensor(tiles(XR[:]), tiles(X1[:]), each(R2[:]), ALU.mult).then_inc(S["xr_ready"], 1)

            def centre(t, u):
                pool.wait_ge(h_loaded[u], 4 * (t - u) + 16)
                pool.wait_ge(S["nm_ready"], t + 1)
                wait(pool, "u_ready", t)
                nc.gpsimd.tensor_tensor(tiles(U0[:]), tiles(H2[u][:]), each(NM[:]), ALU.subtract).then_inc(S["u0_ready"], 1)

            def normalise(t, u):
                pool.wait_ge(S["u0_ready"], t + 1)
                pool.wait_ge(S["rs_ready"], t + 1)
                wait(pool, "x1_ready", t - 3)
                nc.gpsimd.tensor_tensor(tiles(U[u][:]), tiles(U0[:]), each(RS[:]), ALU.mult).then_inc(S["u_ready"], 1)

            def rms_normalise(t, u):
                pool.wait_ge(S["u_ready"], t + 1)
                pool.wait_ge(S["rr_ready"], t + 1)
                wait(pool, "ut_mm", t - 1)
                nc.gpsimd.tensor_tensor(tiles(UR[u % 2][:]), tiles(U[u][:]), each(RR[:]), ALU.mult).then_inc(S["ur_ready"], 1)

            def rotate_key(t, u, i):
                pool.wait_ge(S["kc_ready"], 2 * t + (i + 1))
                pool.wait_ge(S["ks_ready"], 2 * t + (i + 1))
                wait(pool, "scores_ready", 12 * (t - 1))
                nc.gpsimd.tensor_tensor(KR[u % 2][i][:], KC[:], KS[:], ALU.add).then_inc(S["kr_ready"], 1)

            def step(t, u):
                if has(t + 2):
                    centre(t + 2, (u + 2) % 4)
                if has(t - 1):
                    residual(t - 1, (u + 3) % 4)
                    flat(t - 1, u)
                if has(t + 2):
                    normalise(t + 2, (u + 2) % 4)
                if has(t + 1):
                    rotate_key(t + 1, u + 1, 0)
                if has(t + 2):
                    rms_normalise(t + 2, (u + 2) % 4)
                if has(t + 1):
                    rotate_key(t + 1, u + 1, 1)

            run_steps(pool, step)

        @block.scalar
        def _(act):
            act.wait_ge(S["consts_loaded"], 32)
            nc.scalar.activation(ident_b[:], c("ident", 128), ACT.Copy).then_inc(S["prep_act"], 1)
            nc.scalar.activation(mask_b[:], c("mask", 1024).rearrange("p (a f) -> p a f", a=2), ACT.Copy).then_inc(S["prep_act"], 1)
            act.wait_ge(S["prep_pool"], 2)

            def squares(t, u):
                act.wait_ge(h_loaded[u], 4 * (t - u) + 16)
                wait(act, "sums_ready", 2 * t)
                nc.scalar.activation(HSQ[:], H2[u][:], ACT.Square).then_inc(S["hsq_ready"], 1)

            def roots(t):
                if has(t + 2):
                    act.wait_ge(S["rv_ready"], t + 3)
                    wait(act, "u_ready", t + 2)
                    nc.scalar.activation(RS[:], RV[:], ACT.Sqrt).then_inc(S["rs_ready"], 1)
                    act.wait_ge(S["mu2_ready"], t + 3)
                    wait(act, "rr_ready", t + 2)
                    nc.scalar.activation(SDM[:], MU2[:], ACT.Sqrt, bias=eps_rms[:]).then_inc(S["sdm_ready"], 1)
                if has(t - 1):
                    act.wait_ge(S["s3_ready"], t)
                    wait(act, "r2_ready", t - 1)
                    nc.scalar.activation(SDX[:], S3[:], ACT.Sqrt, bias=eps_rms[:], scale=1.0 / 64).then_inc(S["sdx_ready"], 1)

            def exponents(t, u, n):
                part, head = divmod(n, 4)
                act.wait_ge(S["max_ready"], 12 * t + (n + 1))
                wait(act, "pt_mm", 12 * t + (n - 1))
                if n == 0:
                    wait(act, "rsum_ready", t - 1)
                segments = 4 if part == 0 else 2
                for b in range(segments):
                    k = (4 * (b // 2) + b % 2) if part == 0 else 4 * (part - 1) + 2 + b
                    o = slice(b * 512 // segments, (b + 1) * 512 // segments)
                    last = nc.scalar.activation(PR[n % 2][:, o], pS[n % 3][:, o], ACT.Exp, bias=MX[n % 3][:, b:b + 1],
                                                accum_out=SUM[u % 2][:, 4 * k + head:4 * k + head + 1])
                last.then_inc(S["exp_ready"], 1)

            def copy_yt(t):
                act.wait_ge(S["yt_mm"], t + 1)
                wait(act, "wo_mm", t)
                nc.scalar.activation(YT[:], pA[:], ACT.Copy).then_inc(S["yt_ready"], 1)

            def copy_urt(t):
                act.wait_ge(S["ut_mm"], t + 1)
                wait(act, "k_mm", 4 * t)
                nc.scalar.activation(URT[:], pB[:], ACT.Copy).then_inc(S["urt_ready"], 1)

            def copy_v(t, u):
                act.wait_ge(S["v_mm"], t + 1)
                wait(act, "pv_mm", 12 * (t - 1))
                nc.scalar.activation(VT[u % 2][:], pB[:, 0:256].rearrange("p (q f) -> p q f", q=4), ACT.Copy).then_inc(S["vt_ready"], 1)

            def x_squares(t):
                act.wait_ge(S["x1_ready"], t + 1)
                wait(act, "s3_ready", t)
                nc.scalar.activation(XSQ[:], X1[:], ACT.Square).then_inc(S["xsq_ready"], 1)

            def copy_ft(t, u):
                act.wait_ge(S["ft_mm"], t + 1)
                wait(act, "router_mm", t - 1)
                slot_wait(act, flat_stored, t, u)
                nc.scalar.activation(FT[u % 2][:], pA[:], ACT.Copy, scale=w("ln2_w", 1)).then_inc(S["ft_ready"], 1)

            def router_exp(t):
                act.wait_ge(S["rls_ready"], t + 1)
                wait(act, "rp_ready", t)
                nc.scalar.activation(RE[:], RLS[:], ACT.Exp).then_inc(S["re_ready"], 1)

            def step(t, u):
                if has(t):
                    exponents(t, u, 0)
                for n in range(13):
                    if has(t) and n + 1 < 12:
                        exponents(t, u, n + 1)
                    if n == 0 and has(t - 1):
                        copy_yt(t - 1)
                    if n == 0 and has(t + 2):
                        squares(t + 2, (u + 2) % 4)
                    if n == 1 and has(t + 1):
                        copy_urt(t + 1)
                    if n == 2 and has(t - 2):
                        router_exp(t - 2)
                    if n == 3 and has(t + 1):
                        copy_v(t + 1, u + 1)
                    if n == 3 and has(t - 1):
                        x_squares(t - 1)
                    if n == 5:
                        roots(t)
                    if n == 8 and has(t - 1):
                        copy_ft(t - 1, u + 1)

            run_steps(act, step)

        @block.tensor
        def _(pe):
            pe.wait_ge(S["consts_loaded"], 32)
            pe.wait_ge(S["prep_act"], 2)
            pe.wait_ge(S["prep_dve"], 4)

            def scores(t, u, n):
                part, head = divmod(n, 4)
                if n == 0:
                    pe.wait_ge(S["qc_ready"], 2 * t + 2)
                    pe.wait_ge(S["kr_ready"], 2 * t + 2)
                wait(pe, "exp_ready", 12 * t + (n - 2))
                nc.tensor.matmul(pS[n % 3][:], ident_b[:], mask_b[:, min(part, 1), :], start=True, stop=False)
                r = slice(32 * head, 32 * head + 32)
                q, k = QC[u % 2], KR[u % 2]
                if part == 0:
                    for m in range(4):
                        o = 256 * (m // 2)
                        last = nc.tensor.matmul(pS[n % 3][:, 128 * m:128 * m + 128], q[m % 2][r, o:o + 128], k[m % 2][r, o:o + 128],
                                                start=False, stop=(m == 3))
                else:
                    o = 256 * (part - 1)
                    for i in range(2):
                        last = nc.tensor.matmul(pS[n % 3][:, 256 * i:256 * i + 256], q[i][r, o + 128:o + 256], k[i][r, o:o + 256],
                                                start=False, stop=(i == 1))
                last.then_inc(S["scores_ready"], 1)

            def transpose_probs(t, n):
                pe.wait_ge(S["exp_ready"], 12 * t + (n + 1))
                wait(pe, "pts_ready", 12 * t + (n - 1))
                for b in range(4):
                    o = slice(128 * b, 128 * b + 128)
                    last = nc.tensor.transpose(pPT[n % 2][:, o], PR[n % 2][:, o], c("ident", 128))
                last.then_inc(S["pt_mm"], 1)

            def values(t, u, n):
                part, head = divmod(n, 4)
                pe.wait_ge(S["pts_ready"], 12 * t + (n + 1))
                if n == 0:
                    pe.wait_ge(S["vt_ready"], t + 1)
                    wait(pe, "y_ready", t)
                for b in range(4):
                    if part == 0:
                        j, i, kb, qb, first, final = b // 2, b % 2, 0, 0, True, True
                    else:
                        j, i, kb, qb = part - 1, b // 2, b % 2, 1
                        first, final = kb == 0, kb == 1
                    o = 64 * (4 * j + 2 * qb + i) + 16 * head
                    v = 32 * i + 16 * (head // 2)
                    last = nc.tensor.matmul(pY[:, o:o + 16], PTS[n % 2][:, 128 * b:128 * b + 128], VT[u % 2][:, 2 * j + kb, v:v + 16],
                                            start=first, stop=final)
                last.then_inc(S["pv_mm"], 1)

            def transpose_four(dst, src, done):
                for q in range(4):
                    last = nc.tensor.transpose(dst[:, 128 * q:128 * q + 128], src[:, 128 * q:128 * q + 128], c("ident", 128))
                last.then_inc(S[done], 1)

            def use0_yt(t):
                pe.wait_ge(S["y_ready"], t + 1)
                if has(t + 1):
                    pe.wait_ge(S["ks_ready"], 2 * t + 4)
                wait(pe, "ft_ready", t)
                transpose_four(pA, Y, "yt_mm")

            def use1_ut(t, u):
                pe.wait_ge(S["ur_ready"], t + 1)
                wait(pe, "rl_ready", t - 2)
                wait(pe, "kc_ready", 2 * t)
                transpose_four(pB, UR[u % 2], "ut_mm")

            def use2_wo(t):
                pe.wait_ge(S["yt_ready"], t + 1)
                for q in range(4):
                    last = nc.tensor.matmul(pA[:, 128 * q:128 * q + 128], YT[:, 128 * q:128 * q + 128], w("wo", 128), start=True, stop=True)
                last.then_inc(S["wo_mm"], 1)

            def use3_v(t):
                pe.wait_ge(S["urt_ready"], t + 1)
                for q in range(4):
                    last = nc.tensor.matmul(pB[:, 64 * q:64 * q + 64], URT[:, 128 * q:128 * q + 128], w_in[:, 384:448], start=True, stop=True)
                last.then_inc(S["v_mm"], 1)

            def project(dst, i, which, done):
                r = slice(64 * i, 64 * i + 64)
                nc.tensor.matmul(dst[:], w_in[r, 128 * which:128 * which + 128], URT[r, :], start=True, stop=True).then_inc(S[done], 1)

            def use4_q0(t):
                wait(pe, "x1_ready", t - 1)
                wait(pe, "ks_ready", 2 * t)
                project(pA, 0, 0, "q_mm")

            def use5_q1(t):
                pe.wait_ge(S["vt_ready"], t + 1)
                project(pB, 1, 0, "q_mm")

            def use6_k0(t):
                pe.wait_ge(S["qc_ready"], 2 * t + 1)
                project(pA, 0, 1, "k_mm")

            def use7_ks0(t):
                pe.wait_ge(S["qc_ready"], 2 * t + 2)
                project(pB, 0, 2, "k_mm")

            def use8_ft(t):
                pe.wait_ge(S["xr_ready"], t + 1)
                if has(t + 2):
                    pe.wait_ge(S["kc_ready"], 2 * t + 5)
                transpose_four(pA, XR, "ft_mm")

            def use9_k1(t):
                pe.wait_ge(S["ks_ready"], 2 * t + 1)
                project(pB, 1, 1, "k_mm")

            def use10_ks1(t):
                pe.wait_ge(S["kc_ready"], 2 * t + 1)
                wait(pe, "ft_ready", t - 1)
                project(pA, 1, 2, "k_mm")

            def use11_router(t, u):
                pe.wait_ge(S["ft_ready"], t + 1)
                if has(t + 2):
                    pe.wait_ge(S["kc_ready"], 2 * t + 6)
                wait(pe, "rl_ready", t)
                for q in range(4):
                    last = nc.tensor.matmul(pB[:, 16 * q:16 * q + 16], FT[u % 2][:, 128 * q:128 * q + 128], w("router", 16), start=True, stop=True)
                last.then_inc(S["router_mm"], 1)

            def step(t, u):
                if has(t):
                    scores(t, u, 0)
                    scores(t, u, 1)
                for n in range(13):
                    if has(t):
                        if n + 2 < 12:
                            scores(t, u, n + 2)
                        if n < 12:
                            transpose_probs(t, n)
                        if n:
                            values(t, u, n - 1)
                    if has(t - 1):
                        if n == 0:
                            use0_yt(t - 1)
                        if n == 2:
                            use2_wo(t - 1)
                        if n == 8:
                            use8_ft(t - 1)
                        if n == 11:
                            use11_router(t - 1, u + 1)
                    if has(t + 1):
                        if n == 1:
                            use1_ut(t + 1, u + 1)
                        for m, use in ((3, use3_v), (4, use4_q0), (5, use5_q1), (6, use6_k0), (7, use7_ks0), (9, use9_k1), (10, use10_ks1)):
                            if n == m:
                                use(t + 1)

            run_steps(pe, step)

        @block.vector
        def _(dve):
            dve.wait_ge(S["consts_loaded"], 32)
            for a, b in ((0, 128), (128, 256), (256, 384), (384, 448)):
                nc.vector.tensor_scalar(w_in[:, a:b], wsb[:, C_W["w_in"] + a:C_W["w_in"] + b], w("ln1_w", 1), None,
                                        ALU.mult).then_inc(S["prep_dve"], 1)

            def statistics(t, u):
                dve.wait_ge(h_loaded[u], 4 * (t - u) + 16)
                wait(dve, "v0_ready", t)
                wait(dve, "nm_ready", t)
                nc.vector.tensor_reduce(S1[:], tiles(H2[u][:]), AX.X, ALU.add).then_inc(S["sums_ready"], 1)
                dve.wait_ge(S["hsq_ready"], t + 1)
                nc.vector.tensor_reduce(S2[:], tiles(HSQ[:]), AX.X, ALU.add).then_inc(S["sums_ready"], 1)
                dve.wait_ge(S["sums_ready"], 2 * t + 2)
                nc.vector.tensor_tensor(M2[:], S1[:], S1[:], ALU.mult).then_inc(S["m2_ready"], 1)
                wait(dve, "u0_ready", t)
                nc.vector.tensor_scalar(NM[:], S1[:], 1.0 / 64, None, ALU.mult).then_inc(S["nm_ready"], 1)

            def variances(t):
                dve.wait_ge(S["m2_ready"], t + 1)
                nc.vector.scalar_tensor_tensor(V0[:], S2[:], 64.0, M2[:], ALU.mult, ALU.subtract).then_inc(S["v0_ready"], 1)
                dve.wait_ge(S["v0_ready"], t + 1)
                wait(dve, "mu2_ready", t)
                nc.vector.tensor_scalar(V1[:], V0[:], 1.0 / 4096, 0.0, ALU.mult, ALU.max).then_inc(S["v1_ready"], 1)
                dve.wait_ge(S["v1_ready"], t + 1)
                wait(dve, "rv_ready", t)
                nc.vector.tensor_scalar(VE[:], V1[:], LN_EPS, None, ALU.add).then_inc(S["ve_ready"], 1)
                dve.wait_ge(S["ve_ready"], t + 1)
                wait(dve, "rs_ready", t)
                nc.vector.reciprocal(RV[:], VE[:]).then_inc(S["rv_ready"], 1)
                dve.wait_ge(S["rv_ready"], t + 1)
                wait(dve, "sdm_ready", t)
                nc.vector.tensor_tensor(MU2[:], V1[:], RV[:], ALU.mult).then_inc(S["mu2_ready"], 1)

            def rms_factor(t):
                dve.wait_ge(S["sdm_ready"], t + 1)
                wait(dve, "ur_ready", t)
                nc.vector.reciprocal(RR[:], SDM[:]).then_inc(S["rr_ready"], 1)

            def maxima(t, n):
                part = n // 4
                dve.wait_ge(S["scores_ready"], 12 * t + (n + 1))
                wait(dve, "exp_ready", 12 * t + (n - 2))
                segments = 4 if part == 0 else 2
                nc.vector.tensor_reduce(MX[n % 3][:, 0:segments], pS[n % 3][:].rearrange("p (b f) -> p b f", b=segments),
                                        AX.X, ALU.max, negate=True).then_inc(S["max_ready"], 1)

            def copy_probs(t, n):
                dve.wait_ge(S["pt_mm"], 12 * t + (n + 1))
                wait(dve, "pv_mm", 12 * t + (n - 1))
                nc.vector.tensor_copy(PTS[n % 2][:], pPT[n % 2][:]).then_inc(S["pts_ready"], 1)

            def normalise_values(t, u):
                dve.wait_ge(S["exp_ready"], 12 * t + 12)
                wait(dve, "y_ready", t)
                nc.vector.reciprocal(RSUM[:], SUM[u % 2][:]).then_inc(S["rsum_ready"], 1)
                dve.wait_ge(S["rsum_ready"], t + 1)
                dve.wait_ge(S["pv_mm"], 12 * t + 12)
                wait(dve, "yt_mm", t)
                nc.vector.tensor_tensor(tiles(Y[:], 16), tiles(pY[:], 16), each(RSUM[:], 16), ALU.mult).then_inc(S["y_ready"], 1)

            def add_attention(t, u):
                dve.wait_ge(S["wo_mm"], t + 1)
                wait(dve, "xsq_ready", t)
                wait(dve, "res_ready", t)
                wait(dve, "xr_ready", t)
                nc.vector.tensor_tensor(X1[:], U[u][:], pA[:], ALU.add).then_inc(S["x1_ready"], 1)

            def x_sums(t):
                dve.wait_ge(S["xsq_ready"], t + 1)
                wait(dve, "sdx_ready", t)
                nc.vector.tensor_reduce(S3[:], tiles(XSQ[:]), AX.X, ALU.add).then_inc(S["s3_ready"], 1)

            def x_factor(t):
                dve.wait_ge(S["sdx_ready"], t + 1)
                wait(dve, "xr_ready", t)
                nc.vector.reciprocal(R2[:], SDX[:]).then_inc(S["r2_ready"], 1)

            def with_table(dst, src, name):
                t = c(name, 256).unsqueeze(1).broadcast_to([128, 2, 256])
                return nc.vector.tensor_tensor(dst.rearrange("p (j f) -> p j f", j=2), src.rearrange("p (j f) -> p j f", j=2), t, ALU.mult)

            def rotate_query(t, u, i):
                dve.wait_ge(S["q_mm"], 2 * t + (i + 1))
                wait(dve, "scores_ready", 12 * (t - 1))
                with_table(QC[u % 2][i][:], (pA, pB)[i][:], "rope_q").then_inc(S["qc_ready"], 1)

            def key_cos(t, i):
                dve.wait_ge(S["k_mm"], 4 * t + (1 if i == 0 else 3))
                wait(dve, "kr_ready", 2 * t + i)
                with_table(KC[:], (pA, pB)[i][:], "rope_kc").then_inc(S["kc_ready"], 1)

            def key_sin(t, i):
                dve.wait_ge(S["k_mm"], 4 * t + (2 if i == 0 else 4))
                wait(dve, "kr_ready", 2 * t + i)
                with_table(KS[:], (pB, pA)[i][:], "rope_ks").then_inc(S["ks_ready"], 1)

            def router_logits(t):
                dve.wait_ge(S["router_mm"], t + 1)
                wait(dve, "rls_ready", t)
                nc.vector.tensor_copy(RL[:], pB[:, 0:64]).then_inc(S["rl_ready"], 1)

            def router_shift(t):
                dve.wait_ge(S["rl_ready"], t + 1)
                nc.vector.tensor_reduce(RMX[:], tiles(RL[:], 8), AX.X, ALU.max).then_inc(S["rmx_ready"], 1)
                dve.wait_ge(S["rmx_ready"], t + 1)
                wait(dve, "re_ready", t)
                nc.vector.tensor_tensor(tiles(RLS[:], 8), tiles(RL[:], 8), each(RMX[:], 8), ALU.subtract).then_inc(S["rls_ready"], 1)

            def router_probs(t):
                dve.wait_ge(S["re_ready"], t + 1)
                nc.vector.tensor_reduce(RZ[:], tiles(RE[:], 8), AX.X, ALU.add).then_inc(S["rz_ready"], 1)
                dve.wait_ge(S["rz_ready"], t + 1)
                wait(dve, "rp_ready", t)
                nc.vector.reciprocal(RRZ[:], RZ[:]).then_inc(S["rrz_ready"], 1)
                dve.wait_ge(S["rrz_ready"], t + 1)
                wait(dve, "w0_ready", t)
                nc.vector.tensor_tensor(tiles(RP[:], 8), tiles(RE[:], 8), each(RRZ[:], 8), ALU.mult).then_inc(S["rp_ready"], 1)

            def pairs(ap):
                return ap.rearrange("p (k e f) -> p k e f", k=8, e=8)

            def rivals():
                return tiles(RP[:], 8).unsqueeze(2).broadcast_to([128, 8, 8, 8])

            def own():
                return tiles(RP[:], 8).unsqueeze(3).broadcast_to([128, 8, 8, 8])

            def router_greater(t):
                dve.wait_ge(S["rp_ready"], t + 1)
                wait(dve, "before_ready", t)
                nc.vector.tensor_tensor(pairs(GT[:]), rivals(), own(), ALU.is_gt).then_inc(S["gt_ready"], 1)

            def router_equal(t):
                wait(dve, "eqm_ready", t)
                nc.vector.tensor_tensor(pairs(EQ[:]), rivals(), own(), ALU.is_equal).then_inc(S["eq_ready"], 1)
                dve.wait_ge(S["eq_ready"], t + 1)
                wait(dve, "before_ready", t)
                nc.vector.tensor_tensor(tiles(EQM[:]), tiles(EQ[:]), c("lower", 64).unsqueeze(1).broadcast_to([128, 8, 64]),
                                        ALU.mult).then_inc(S["eqm_ready"], 1)

            def router_rank(t):
                dve.wait_ge(S["gt_ready"], t + 1)
                dve.wait_ge(S["eqm_ready"], t + 1)
                wait(dve, "rank_ready", t)
                nc.vector.tensor_tensor(BEFORE[:], GT[:], EQM[:], ALU.add).then_inc(S["before_ready"], 1)
                dve.wait_ge(S["before_ready"], t + 1)
                wait(dve, "sel_ready", t)
                nc.vector.tensor_reduce(RK[:], tiles(BEFORE[:], 8), AX.X, ALU.add).then_inc(S["rank_ready"], 1)

            def router_select(t):
                dve.wait_ge(S["rank_ready"], t + 1)
                wait(dve, "w0_ready", t)
                nc.vector.tensor_scalar(SEL[:], RK[:], 2.0, None, ALU.is_lt).then_inc(S["sel_ready"], 1)
                dve.wait_ge(S["sel_ready"], t + 1)
                wait(dve, "g_ready", t)
                nc.vector.tensor_tensor(W0[:], RP[:], SEL[:], ALU.mult).then_inc(S["w0_ready"], 1)

            def router_gates(t, u):
                dve.wait_ge(S["w0_ready"], t + 1)
                nc.vector.tensor_reduce(WS[:], tiles(W0[:], 8), AX.X, ALU.add).then_inc(S["ws_ready"], 1)
                dve.wait_ge(S["ws_ready"], t + 1)
                wait(dve, "rws_ready", t)
                nc.vector.tensor_scalar(WSE[:], WS[:], 1e-9, None, ALU.add).then_inc(S["wse_ready"], 1)
                dve.wait_ge(S["wse_ready"], t + 1)
                wait(dve, "g_ready", t)
                nc.vector.reciprocal(RWS[:], WSE[:]).then_inc(S["rws_ready"], 1)
                dve.wait_ge(S["rws_ready"], t + 1)
                slot_wait(dve, gates_stored, t, u)
                nc.vector.tensor_tensor(tiles(G[u % 2][:], 8), tiles(W0[:], 8), each(RWS[:], 8), ALU.mult).then_inc(S["g_ready"], 1)

            def step(t, u):
                if has(t):
                    maxima(t, 0)
                for n in range(13):
                    if has(t):
                        if n + 1 < 12:
                            maxima(t, n + 1)
                        if n < 12:
                            copy_probs(t, n)
                    if has(t + 2):
                        if n == 1:
                            statistics(t + 2, (u + 2) % 4)
                        if n == 2:
                            variances(t + 2)
                        if n == 7:
                            rms_factor(t + 2)
                    if has(t + 1):
                        if n == 4:
                            rotate_query(t + 1, u + 1, 0)
                        if n == 5:
                            rotate_query(t + 1, u + 1, 1)
                        if n == 6:
                            key_cos(t + 1, 0)
                        if n == 7:
                            key_sin(t + 1, 0)
                        if n == 9:
                            key_cos(t + 1, 1)
                        if n == 10:
                            key_sin(t + 1, 1)
                    if has(t - 1):
                        if n == 2:
                            add_attention(t - 1, (u + 3) % 4)
                        if n == 4:
                            x_sums(t - 1)
                        if n == 6:
                            x_factor(t - 1)
                        if n == 11:
                            router_logits(t - 1)
                    if has(t - 2):
                        if n == 0:
                            router_shift(t - 2)
                        if n == 3:
                            router_probs(t - 2)
                        if n == 5:
                            router_greater(t - 2)
                        if n == 8:
                            router_equal(t - 2)
                        if n == 9:
                            router_rank(t - 2)
                        if n == 10:
                            router_select(t - 2)
                        if n == 12:
                            router_gates(t - 2, u)
                if has(t):
                    normalise_values(t, u)

            run_steps(dve, step)
def experts_phase(nc, held, flat, gates, res, wpack, out):
    STEPS = 2 * GROUPS
    with ExitStack() as ctx:
        def sb(name, shape, dt=F32):
            return ctx.enter_context(nc.sbuf_tensor("d_" + name, shape, dt))

        wsb = sb("wsb", [128, D_W["end"]])
        w_high = sb("w_high", [128, 2, UNITS * 128], F32R)
        w_low = sb("w_low", [128, 2, UNITS * 128], F32R)
        F2 = [sb(f"f2_{k}", [128, 512]) for k in range(4)]
        HL = [sb(f"hl{k}", [128, 512], F32R) for k in range(2)]
        SG = [sb(f"sg{k}", [128, 512]) for k in range(2)]
        HH = [sb(f"hh{k}", [128, 512]) for k in range(4)]
        GB = [sb(f"g{k}", [128, 64]) for k in range(2)]
        RB = [sb(f"r{k}", [128, 512]) for k in range(2)]
        GY = [sb(f"gy{k}", [128, 4, 512]) for k in range(2)]
        Y4 = sb("y4", [128, 4, 256])
        Y2 = sb("y2", [128, 4, 128])
        Y1 = sb("y1", [128, 4, 64])
        OUT = [sb(f"out{k}", [128, 512]) for k in range(2)]

        def bank(name):
            return ctx.enter_context(nc.psum_tensor("d_" + name, [128, 512], F32))

        pH1 = [bank(f"ph1_{k}") for k in range(2)]
        pH3 = [bank(f"ph3_{k}") for k in range(2)]
        pY = [bank(f"py{k}") for k in range(4)]

        names = ("weights_loaded w_high_ready w_low_ready high_ready low_ready hidden_mm silu_ready hh_ready w2_mm "
                 "gated_ready y4_ready y2_ready y1_ready out_ready").split()
        S = {n: new_semaphore(nc, held, "d_" + n) for n in names}
        f_loaded = [new_semaphore(nc, held, f"d_f_loaded{k}") for k in range(4)]
        g_loaded, r_loaded, out_stored = (
            [new_semaphore(nc, held, f"d_{n}{k}") for k in range(2)] for n in ("g_loaded", "r_loaded", "out_stored"))

        def wait(eng, name, value):
            if not isinstance(value, int) or value > 0:
                eng.wait_ge(S[name], value)

        def has(t):
            return not isinstance(t, int) or 0 <= t < STEPS

        def run_steps(eng, step):
            for t in range(-1, 4):
                step(t, t % 4)
            with eng.Fori(0, STEPS // 4 - 2) as j:
                for u in range(4):
                    step(4 * j + (4 + u), u)
            for t in range(STEPS - 4, STEPS + 1):
                step(t, t % 4)

        block = ctx.enter_context(nc.Block())

        @block.sync
        def _(sp):
            sp.dma_start(wsb[:], wpack).then_inc(S["weights_loaded"], 16)

            def load(s, v):
                wait(sp, "low_ready", 2 * s - 2)
                for i in range(2):
                    rows = flat[bass.ds(s, 1), 64 * i:64 * i + 64].rearrange("o p f -> (o p) f")
                    for half in range(2):
                        sp.dma_start(F2[2 * v + i][64 * half:64 * half + 64, :], rows).then_inc(f_loaded[2 * v + i], 16)
                wait(sp, "gated_ready", 8 * (s - 1))
                sp.dma_start(GB[v][:], gates[bass.ds(s, 1)].rearrange("o p f -> (o p) f")).then_inc(g_loaded[v], 16)
                wait(sp, "out_ready", 2 * (s - 1))
                sp.dma_start(RB[v][:], res[bass.ds(s, 1)].rearrange("o p f -> (o p) f")).then_inc(r_loaded[v], 16)

            def store(s, v):
                sp.wait_ge(S["out_ready"], 2 * s + 2)
                dst = out[bass.ds(s, 1)].rearrange("o q p c -> p (o q) c")
                sp.dma_start(dst, OUT[v][:].rearrange("p (q c) -> p q c", c=64)).then_inc(out_stored[v], 16)

            load(0, 0)
            load(1, 1)
            store(0, 0)
            with sp.Fori(0, GROUPS // 2 - 1) as j:
                for v in range(2):
                    load(2 * j + (2 + v), v)
                    store(2 * j + (1 + v), (1 + v) % 2)
            store(GROUPS - 1, 1)
            for v in range(2):
                sp.wait_ge(out_stored[v], 16 * GROUPS // 2)

        @block.gpsimd
        def _(pool):
            def fold(t, u):
                i, v = u % 2, u // 2
                gy = GY[i]
                pool.wait_ge(S["gated_ready"], 4 * t + 4)
                wait(pool, "y2_ready", t)
                nc.gpsimd.tensor_tensor(Y4[:], gy[:, :, 0:256], gy[:, :, 256:512], ALU.add).then_inc(S["y4_ready"], 1)
                pool.wait_ge(S["y4_ready"], t + 1)
                wait(pool, "y1_ready", t)
                nc.gpsimd.tensor_tensor(Y2[:], Y4[:, :, 0:128], Y4[:, :, 128:256], ALU.add).then_inc(S["y2_ready"], 1)
                pool.wait_ge(S["y2_ready"], t + 1)
                wait(pool, "out_ready", t)
                nc.gpsimd.tensor_tensor(Y1[:], Y2[:, :, 0:64], Y2[:, :, 64:128], ALU.add).then_inc(S["y1_ready"], 1)
                pool.wait_ge(S["y1_ready"], t + 1)
                pool.wait_ge(r_loaded[v], 4 * (t - u) + 16)
                if i == 0 and (not isinstance(t, int) or t >= 4):
                    pool.wait_ge(out_stored[v], 4 * (t - u))
                r = RB[v][:].rearrange("p (a h i c) -> p a h i c", a=2, h=2, i=2)[:, :, :, i]
                o = OUT[v][:].rearrange("p (a i h c) -> p a i h c", a=2, i=2, h=2)[:, :, i]
                y = Y1[:].rearrange("p (a h) c -> p a h c", a=2)
                nc.gpsimd.tensor_tensor(o, r, y, ALU.add).then_inc(S["out_ready"], 1)

            def step(t, u):
                if has(t - 1):
                    fold(t - 1, (u + 3) % 4)

            run_steps(pool, step)

        @block.scalar
        def _(act):
            act.wait_ge(S["weights_loaded"], 16)
            for k in range(2):
                nc.scalar.activation(w_high[:, k], wsb[:, UNITS * 128 * k:UNITS * 128 * (k + 1)], ACT.Copy).then_inc(S["w_high_ready"], 1)

            def high(t, u):
                act.wait_ge(f_loaded[u], 8 * (t - u) + 32)
                wait(act, "hidden_mm", UNITS * (t - 1))
                nc.scalar.activation(HL[u % 2][:], F2[u][:], ACT.Copy).then_inc(S["high_ready"], 1)

            def silu(t, u, n):
                k = (UNITS * u + n) % 2
                act.wait_ge(S["hidden_mm"], UNITS * t + (n + 1))
                wait(act, "hh_ready", UNITS * t + (n - 1))
                nc.scalar.activation(SG[k][:], pH1[k][:], ACT.Silu).then_inc(S["silu_ready"], 1)

            def step(t, u):
                for n in range(UNITS):
                    if has(t):
                        silu(t, u, n)
                    if n == 5 and has(t + 1):
                        high(t + 1, (u + 1) % 4)

            run_steps(act, step)

        @block.tensor
        def _(pe):
            pe.wait_ge(S["w_low_ready"], 2)

            def hidden(t, u, n):
                k = (UNITS * u + n) % 2
                if n == 0:
                    pe.wait_ge(S["low_ready"], t + 1)
                wait(pe, "hh_ready", UNITS * t + (n - 1))
                cols = slice(128 * n, 128 * n + 128)
                for m, dst in ((0, pH1[k]), (1, pH3[k])):
                    nc.tensor.matmul(dst[:], w_high[:, m, cols], HL[u % 2][:], start=True, stop=False)
                    last = nc.tensor.matmul(dst[:], w_low[:, m, cols], HL[u % 2][:], start=False, stop=True)
                last.then_inc(S["hidden_mm"], 1)

            def down(t, u, n):
                pe.wait_ge(S["hh_ready"], UNITS * t + (n + 1))
                if n < len(TAIL_EXPERTS):
                    experts, row = TAIL_EXPERTS[n], 0
                else:
                    experts, row = [n - len(TAIL_EXPERTS)], 1
                a, b = 64 * experts[0], 64 * (experts[-1] + 1)
                moving = wsb[:, D_W["w2"] + 512 * row + a:D_W["w2"] + 512 * row + b]
                for m in range(4):
                    if n == 0:
                        wait(pe, "gated_ready", 4 * (t - 1) + (m + 1))
                    last = nc.tensor.matmul(pY[m][:, a:b], HH[(UNITS * u + n) % 4][:, 128 * m:128 * m + 128], moving,
                                            start=n == 0, stop=n == UNITS - 1, skip_group_check=True)
                last.then_inc(S["w2_mm"], 1)

            def step(t, u):
                for n in range(UNITS):
                    if has(t):
                        hidden(t, u, n)
                    if n < 2 and has(t - 1):
                        down(t - 1, (u + 3) % 4, UNITS - 2 + n)
                    if n == 3 and has(t):
                        down(t, u, 0)
                    if n >= 3 and has(t):
                        down(t, u, n - 2)

            run_steps(pe, step)

        @block.vector
        def _(dve):
            for k in range(2):
                dve.wait_ge(S["w_high_ready"], k + 1)
                nc.vector.tensor_tensor(w_low[:, k], wsb[:, UNITS * 128 * k:UNITS * 128 * (k + 1)], w_high[:, k].bitcast(F32),
                                        ALU.subtract).then_inc(S["w_low_ready"], 1)

            def low(t, u):
                dve.wait_ge(S["high_ready"], t + 1)
                rows = HL[u % 2][64:128, :]
                nc.vector.tensor_tensor(rows, F2[u][64:128, :], rows.bitcast(F32), ALU.subtract).then_inc(S["low_ready"], 1)

            def product(t, u, n):
                g = UNITS * u + n
                dve.wait_ge(S["silu_ready"], UNITS * t + (n + 1))
                wait(dve, "w2_mm", UNITS * t + (n - 3))
                nc.vector.tensor_tensor(HH[g % 4][:], SG[g % 2][:], pH3[g % 2][:], ALU.mult).then_inc(S["hh_ready"], 1)

            def gated(t, u, m):
                v, i = u // 2, u % 2
                if m == 0:
                    dve.wait_ge(g_loaded[v], 4 * (t - u) + 16)
                    dve.wait_ge(S["w2_mm"], UNITS * t + UNITS)
                    wait(dve, "y4_ready", t - 1)
                k = 2 * m + i
                gate = GB[v][:, 8 * k:8 * k + 8].unsqueeze(2).broadcast_to([128, 8, 64])
                nc.vector.tensor_tensor(GY[i][:, m].rearrange("p (e c) -> p e c", c=64), pY[m][:].rearrange("p (e c) -> p e c", c=64),
                                        gate, ALU.mult).then_inc(S["gated_ready"], 1)

            def step(t, u):
                for n in range(UNITS):
                    if has(t):
                        product(t, u, n)
                    if n == 1 and has(t - 1):
                        for m in range(4):
                            gated(t - 1, (u + 3) % 4, m)
                    if n == 6 and has(t + 1):
                        low(t + 1, (u + 1) % 4)

            run_steps(dve, step)


def _pair(a, np):
    return np.concatenate([a, a], 0)


def _blocks(a, np, swap=False):
    out = np.zeros((128, 128), a.dtype)
    for i in range(2):
        o = 1 - i if swap else i
        out[64 * i:64 * i + 64, 64 * o:64 * o + 64] = a
    return out


def pack_a(inputs, np):
    g = {k[len("L0_tok_"):]: np.asarray(v) for k, v in inputs.items() if k.startswith("L0_tok_")}
    col = lambda v: _pair(v.reshape(64, 1), np)
    return np.ascontiguousarray(np.concatenate([
        _pair(g["Wkv"].T, np), _blocks(g["Wkv"][64:].T, np, True), _blocks(g["proj_w"].T, np, True),
        _blocks(g["Wq"].T, np), col(g["ln_kv_w"]), col(g["ln_kv_b"]), col(g["ln_q_w"]), col(g["ln_q_b"]),
        col(g["proj_b"])], 1))


def consts_a(np):
    p = np.arange(128)
    same = (p[:, None] // 64 == p[None] // 64).astype(np.float32)
    c = np.arange(32)
    parts = [np.eye(128, dtype=np.float32) - same / 64, same / 64]
    for sub in range(2):
        parts.append(((c[None] // 16 == sub) & (p[:, None] // 64 == (c[None] % 16) // 8)) / np.float32(64))
    for sub in range(2):
        parts.append((c[None] // 16 == sub) & (p[:, None] // 8 == c[None] % 16))
    head = (1 - p // 64) * 8 + (p % 64) // 8
    for g in range(CHUNKS):
        parts.append((p[:, None] // 16 == g) & (p[:, None] % 16 == head[None]))
    return np.ascontiguousarray(np.concatenate(parts, 1).astype(np.float32))


def pack_b(inputs, np):
    g = {k[len("L0_attn_"):]: np.asarray(v) for k, v in inputs.items() if k.startswith("L0_attn_")}
    rows = lambda v: np.broadcast_to(v[None], (128, v.shape[0]))
    wv, bv = g["W_qkv"][:, 128:], g["b_qkv"][128:]
    return np.ascontiguousarray(np.concatenate([
        _pair(g["W_qkv"], np), _pair(np.concatenate([wv.T, wv.T], 1), np), _pair(g["W_out"], np),
        _pair(np.broadcast_to(bv[:, None], (64, 128)), np), rows(g["b_qkv"]), rows(g["b_out"])], 1))


def consts_b(np):
    p = np.arange(128)
    same = (p[:, None] // 64 == p[None] // 64).astype(np.float32)
    eye = np.eye(128, dtype=np.float32)
    return np.ascontiguousarray(np.concatenate([eye, eye - same / 64, np.ones((128, 1), np.float32)], 1))


def pack_c(inputs, np):
    g = {k[len("L0_ffn_"):]: np.asarray(v) for k, v in inputs.items() if k.startswith("L0_ffn_")}
    swap = (np.arange(16) + 8) % 16
    q = g["wq"].reshape(4, 16, 64)
    k = g["wk"].reshape(2, 16, 64)[np.array([0, 0, 1, 1])]
    q = np.concatenate([q, q[:, swap]], 1).reshape(128, 64).T
    kc = np.concatenate([k, k], 1).reshape(128, 64).T
    ks = np.concatenate([k[:, swap], k[:, swap]], 1).reshape(128, 64).T

    def blocks(a):
        out = np.zeros((128, 2 * a.shape[1]), a.dtype)
        out[:64, :a.shape[1]] = a
        out[64:, a.shape[1]:] = a
        return out

    col = lambda v: _pair(v.reshape(64, 1), np)
    return np.ascontiguousarray(np.concatenate([
        _pair(q, np), _pair(kc, np), _pair(ks, np), blocks(g["wv"].T), blocks(g["wo"].T), blocks(g["router_w"].T),
        col(g["ln1_w"]), col(g["ln2_w"])], 1))


def consts_c(np):
    p = np.arange(128)
    later = np.where(p[None] > p[:, None], np.float32(-1e30), np.float32(0))
    zero = np.zeros((128, 128), np.float32)
    mask = [later] * 4 + [zero, later] * 2
    inv_freq = 1.0 / 10000.0 ** (np.arange(0, 16, 2, dtype=np.float32) / 16)
    freqs = np.outer(np.arange(256, dtype=np.float32), inv_freq)
    emb = np.concatenate([freqs, freqs], axis=-1)
    cos, sin = np.cos(emb).T, np.sin(emb).T
    sin = np.where(np.arange(16)[:, None] < 8, -sin, sin)
    rope_q = np.tile(np.concatenate([cos, sin], 0) * np.float32(0.25), (4, 1))
    lower = (np.arange(8)[None] < np.arange(8)[:, None]).astype(np.float32).reshape(1, 64)
    return np.ascontiguousarray(np.concatenate(
        [np.eye(128, dtype=np.float32)] + mask + [rope_q, np.tile(cos, (8, 1)), np.tile(sin, (8, 1)), np.tile(lower, (128, 1))],
        1).astype(np.float32))


def pack_d(inputs, np):
    w1, w2, w3 = (np.asarray(inputs["L0_ffn_" + n]) for n in ("w1", "w2", "w3"))

    def units(a):
        out = np.zeros((64, UNITS, 128), a.dtype)
        for n, experts in enumerate(TAIL_EXPERTS):
            for i, e in enumerate(experts):
                out[:, n, i * TAIL:(i + 1) * TAIL] = a[e, 128:].T
        for e in range(EXPERTS):
            out[:, len(TAIL_EXPERTS) + e] = a[e, :128].T
        return _pair(out.reshape(64, UNITS * 128), np)

    down = np.zeros((128, 2, EXPERTS, 64), w2.dtype)
    for e in range(EXPERTS):
        i = e % PER_TAIL
        down[i * TAIL:(i + 1) * TAIL, 0, e] = w2[e, :, 128:].T
        down[:, 1, e] = w2[e, :, :128].T
    return np.ascontiguousarray(np.concatenate([units(w1), units(w3), down.reshape(128, -1)], 1))


def end_phase(nc, held):
    nc.all_engine_barrier()
    nc.clear_and_free_semaphores(held)
    held.clear()
    nc.all_engine_barrier()


def build(nc, ap, out):
    def scratch(name, shape):
        return nc.dram_tensor(name, shape, F32).ap()

    tokens = scratch("tokens", [PAIRS, 128, NPATCH])
    mixed = scratch("mixed", [GROUPS, 128, 512])
    residual = scratch("residual", [GROUPS, 128, 512])
    flat = scratch("flat", [GROUPS, 128, 512])
    gates = scratch("gates", [GROUPS, 128, 8 * EXPERTS])
    held = []
    tokenize_phase(nc, held, ap["x"], ap["wa"], ap["ca"], tokens)
    end_phase(nc, held)
    linear_attention_phase(nc, held, tokens, ap["wb"], ap["cb"], mixed)
    end_phase(nc, held)
    causal_attention_phase(nc, held, mixed, ap["wc"], ap["cc"], residual, flat, gates)
    end_phase(nc, held)
    experts_phase(nc, held, flat, gates, residual, ap["wd"], out)


def kernel(**inputs):
    import numpy as np
    import concourse.bacc as bacc
    from concourse.bass_utils import run_bass_kernel_spmd

    arrays = {"x": np.ascontiguousarray(inputs["x"]), "wa": pack_a(inputs, np), "ca": consts_a(np),
              "wb": pack_b(inputs, np), "cb": consts_b(np), "wc": pack_c(inputs, np), "cc": consts_c(np),
              "wd": pack_d(inputs, np)}
    nc = bacc.Bacc("TRN2", target_bir_lowering=False, num_devices=1)
    ap = {n: nc.dram_tensor(f"in_{n}", a.shape, mybir.dt.from_np(a.dtype), kind="ExternalInput").ap() for n, a in arrays.items()}
    out = nc.dram_tensor("out_0_dram", (IMAGES, NPATCH, CH), F32, kind="ExternalOutput").ap()
    build(nc, ap, out.rearrange("(s a) (h p) c -> s (a h) p c", a=4, p=128))
    results = run_bass_kernel_spmd(nc, [{f"in_{n}": a for n, a in arrays.items()}], core_ids=[0])
    return results.results[0]["out_0_dram"]
```

```python
from contextlib import ExitStack

import concourse.bass as bass
from concourse import mybir

F32 = mybir.dt.float32
F32R = mybir.dt.float32r
BF16 = mybir.dt.bfloat16
ALU = mybir.AluOpType
ACT = mybir.ActivationFunctionType
AX = mybir.AxisListType

IMAGES, CH, SIDE, PATCH, HEADS = 128, 64, 64, 4, 8
PAIRS = IMAGES // 2
PIX = SIDE * SIDE
NPATCH = PIX // PATCH ** 2
CHUNKS = PIX // 512
LN_EPS = 1e-5


def columns(*parts):
    at, out = 0, {}
    for name, width in parts:
        out[name] = at
        at += width
    out["end"] = at
    return out


A_W = columns(("wkv", 128), ("wv_swapped", 128), ("proj", 128), ("wq", 128), ("lnkv_w", 1), ("lnkv_b", 1),
              ("lnq_w", 1), ("lnq_b", 1), ("proj_b", 1))
A_C = columns(("centre", 128), ("mean", 128), ("mean0", 32), ("mean1", 32), ("head0", 32), ("head1", 32),
              ("spread", CHUNKS * 128))
GROUPS = PAIRS // 2
DIV_EPS, NORM_EPS = 1e-7, 1e-12
B_W = columns(("wqkv", 192), ("wv_t", 128), ("w_out", 64), ("bv_rep", 128), ("bias", 192), ("b_out", 64))
B_C = columns(("ident", 128), ("centre", 128), ("ones", 1))
RMS_EPS = 1e-6
C_W = columns(("w_in", 448), ("wo", 64), ("router", 16), ("ln1_w", 1), ("ln2_w", 1))
C_C = columns(("ident", 128), ("mask", 1024), ("rope_q", 256), ("rope_kc", 256), ("rope_ks", 256), ("lower", 64))


EXPERTS, HIDDEN = 8, int(8 / 3 * 64)
TAIL = HIDDEN - 128
PER_TAIL = 128 // TAIL
TAIL_EXPERTS = [list(range(e, min(e + PER_TAIL, EXPERTS))) for e in range(0, EXPERTS, PER_TAIL)]
UNITS = len(TAIL_EXPERTS) + EXPERTS
D_W = columns(("w1", UNITS * 128), ("w3", UNITS * 128), ("w2", 2 * EXPERTS * 64))


def new_semaphore(nc, held, name):
    held.append(nc.alloc_semaphore(name=name))
    return held[-1]


def tokenize_phase(nc, held, x, wpack, cpack, h1_out):
    with ExitStack() as ctx:
        def sb(name, shape, dt=F32):
            return ctx.enter_context(nc.sbuf_tensor(name, shape, dt))

        def sem(name):
            return new_semaphore(nc, held, name)

        wsb = sb("a_wsb", [128, A_W["end"]])
        csb = sb("a_csb", [128, A_C["end"]])

        def w(name, width):
            return wsb[:, A_W[name]:A_W[name] + width]

        def c(name, width):
            return csb[:, A_C[name]:A_C[name] + width]

        kv_fold = sb("a_kv_fold", [128, 128])
        kv_w = sb("a_kv_w", [128, 128])
        spread_heads = sb("a_spread_heads", [128, CHUNKS * 128], F32R)
        v_bias = sb("a_v_bias", [128, 1])
        proj_bias = sb("a_proj_bias", [128, 1])
        lnq_w16 = sb("a_lnq_w16", [128, 1])
        eps = sb("a_eps", [128, 1])
        LNV = sb("a_lnv", [128, 512])
        LNQ = sb("a_lnq", [128, NPATCH])

        X = [sb(f"a_x{k}", [128, PIX]) for k in range(4)]
        XSQ = [sb(f"a_xsq{k}", [128, PIX]) for k in range(2)]
        T1 = sb("a_pool1", [128, PIX // 2])
        T2 = sb("a_pool2", [128, PIX // 4])
        T3 = sb("a_pool3", [128, PIX // 8])
        SUM = [sb(f"a_sum{k}", [128, NPATCH]) for k in range(4)]
        CEN = sb("a_cen", [128, NPATCH])
        CSQ = sb("a_csq", [128, NPATCH])
        SDQ = sb("a_sdq", [128, NPATCH])
        RSQ = sb("a_rsq", [128, NPATCH])
        XN = sb("a_xn", [128, NPATCH])
        XA = sb("a_xa", [128, NPATCH])
        Q = [sb(f"a_q{k}", [128, NPATCH]) for k in range(2)]
        PROD = sb("a_prod", [128, PIX])
        MSQ = sb("a_msq", [128, 512])
        VAR = sb("a_var", [128, 512])
        SDP = sb("a_sdp", [128, 512])
        RSTD = [sb(f"a_rstd{k}", [128, 512]) for k in range(2)]
        LG = sb("a_lg", [128, 512])
        MX = sb("a_mx", [128, 32])
        LS = sb("a_ls", [128, 512])
        EX = sb("a_ex", [128, 512])
        ZS = sb("a_zs", [128, 32])
        RZ = sb("a_rz", [128, 32])
        ER = sb("a_er", [128, 512])
        WT = sb("a_wt", [128, 512])
        WHI = sb("a_whi", [128, 512], F32R)
        WLO = sb("a_wlo", [128, 512], F32R)
        WBC = [sb(f"a_wbc{k}", [128, 512]) for k in range(2)]
        VW = [sb(f"a_vw{k}", [128, 512]) for k in range(2)]
        AG = [sb(f"a_ag{k}", [128, NPATCH]) for k in range(2)]
        PJ = sb("a_pj", [128, NPATCH])
        H1 = [sb(f"a_h1_{k}", [128, NPATCH]) for k in range(2)]

        def bank(name):
            return ctx.enter_context(nc.psum_tensor(name, [128, 512], F32))

        pK = [bank("a_pk0"), bank("a_pk1")]
        pV = [bank("a_pv0"), bank("a_pv1")]
        pB0, pMU, pEX, pM = (bank(n) for n in ("a_pb0", "a_pmu", "a_pex", "a_pm"))
        pB = [pB0, pEX]
        pL = pMU

        names = ("consts_loaded prep_dve prep_pe prep_act prep_pool k_ready v_ready wbc_ready prod_ready log_ready vw_ready "
                 "ag_ready wbc_copied stats_ready mean_ready varq_ready qproj_ready pj_mm xsq_ready sum_step "
                 "sum_ready er_ready cen_ready rsq_ready xn_ready csq_ready lnq_ready lnv_ready xa_ready q_ready msq_ready "
                 "var_ready sdp_ready rstd_ready logit_ready max_ready shift_ready exp_ready z_ready rz_ready "
                 "wt_ready whi_ready wlo_ready pj_ready h1_ready").split()
        S = {n: sem("a_" + n) for n in names}
        x_loaded = [sem(f"a_x_loaded{k}") for k in range(4)]
        h1_stored = [sem(f"a_h1_stored{k}") for k in range(2)]

        LAG = 2
        x_view = x.rearrange("(i m) c h w -> i (m c) (h w)", m=2)

        def wait(eng, name, value):
            if not isinstance(value, int) or value > 0:
                eng.wait_ge(S[name], value)

        def has(t):
            return not isinstance(t, int) or 0 <= t < PAIRS

        def run_steps(eng, step):
            for t in range(4):
                step(t, t)
            with eng.Fori(0, PAIRS // 4 - 2) as j:
                for u in range(4):
                    step(4 * j + (4 + u), u)
            for t in range(PAIRS - 4, PAIRS + 1):
                step(t, t % 4)

        def x_wait(eng, t, u):
            eng.wait_ge(x_loaded[u], 4 * (t - u) + 16)

        def patch_row(ap, row):
            return ap[:, row * 256:(row + 1) * 256].rearrange("p (s w t) -> p w s t", s=4, w=16, t=4)

        def by_patch(ap):
            return ap.rearrange("p (q n) -> p q n", n=16)

        def over_pixels(ap):
            return ap.unsqueeze(2).broadcast_to([128, 32, 16])

        block = ctx.enter_context(nc.Block())

        @block.sync
        def _(sp):
            sp.dma_start(wsb[:], wpack).then_inc(S["consts_loaded"], 16)
            sp.dma_start(csb[:], cpack).then_inc(S["consts_loaded"], 16)

            def load(t, u):
                wait(sp, "v_ready", CHUNKS * (t - 3))
                sp.dma_start(X[u][:], x_view[bass.ds(t, 1)].rearrange("o p f -> (o p) f")).then_inc(x_loaded[u], 16)

            def store(t, u):
                sp.wait_ge(S["h1_ready"], t + 1)
                sp.dma_start(h1_out[bass.ds(t, 1)].rearrange("o p f -> (o p) f"), H1[u % 2][:]).then_inc(h1_stored[u % 2], 16)

            for t in range(3):
                load(t, t)

            def step(t, u):
                if has(t + 3):
                    load(t + 3, (u + 3) % 4)
                if has(t - 2):
                    store(t - 2, (u + 2) % 4)

            run_steps(sp, step)
            store(PAIRS - 1, 3)
            for k in range(2):
                sp.wait_ge(h1_stored[k], 16 * PAIRS // 2)

        @block.gpsimd
        def _(pool):
            nc.gpsimd.memset(eps[:], LN_EPS).then_inc(S["prep_pool"], 1)

            def sums(t, u):
                x_wait(pool, t, u)
                wait(pool, "sum_ready", t)
                x4 = X[u][:].rearrange("p (a s f) -> p a s f", s=4, f=64)
                t1 = T1[:].rearrange("p (a s f) -> p a s f", s=2, f=64)
                t2 = T2[:].rearrange("p (q n) -> p q n", n=4)
                t3 = T3[:].rearrange("p (q n) -> p q n", n=2)
                nc.gpsimd.tensor_tensor(t1, x4[:, :, 0:2], x4[:, :, 2:4], ALU.add).then_inc(S["sum_step"], 1)
                pool.wait_ge(S["sum_step"], 3 * t + 1)
                nc.gpsimd.tensor_tensor(T2[:].rearrange("p (a f) -> p a f", f=64), t1[:, :, 0], t1[:, :, 1],
                                        ALU.add).then_inc(S["sum_step"], 1)
                pool.wait_ge(S["sum_step"], 3 * t + 2)
                nc.gpsimd.tensor_tensor(t3, t2[:, :, 0:2], t2[:, :, 2:4], ALU.add).then_inc(S["sum_step"], 1)
                pool.wait_ge(S["sum_step"], 3 * t + 3)
                wait(pool, "h1_ready", t - 3)
                nc.gpsimd.tensor_tensor(SUM[u][:], t3[:, :, 0], t3[:, :, 1], ALU.add).then_inc(S["sum_ready"], 1)

            def weigh(t, u):
                pool.wait_ge(S["exp_ready"], t + 1)
                pool.wait_ge(S["rstd_ready"], t + 1)
                wait(pool, "wt_ready", t)
                nc.gpsimd.tensor_tensor(ER[:], EX[:], RSTD[u % 2][:], ALU.mult).then_inc(S["er_ready"], 1)

            sums(0, 0)
            sums(1, 1)

            def step(t, u):
                if has(t + 2):
                    sums(t + 2, (u + 2) % 4)
                if has(t):
                    weigh(t, u)

            run_steps(pool, step)

        @block.scalar
        def _(act):
            act.wait_ge(S["consts_loaded"], 32)
            act.wait_ge(S["prep_pool"], 1)
            nc.scalar.activation(spread_heads[:], c("spread", CHUNKS * 128), ACT.Copy).then_inc(S["prep_act"], 1)
            act.wait_ge(S["prep_pe"], 1)
            nc.scalar.activation(kv_w[:], pM[:, 0:128], ACT.Copy).then_inc(S["prep_act"], 1)
            act.wait_ge(S["prep_pe"], 2)
            nc.scalar.activation(v_bias[:], pB0[:, 0:1], ACT.Copy).then_inc(S["prep_act"], 1)
            act.wait_ge(S["prep_pe"], 3)
            nc.scalar.activation(proj_bias[:], pB0[:, 2:3], ACT.Identity, bias=w("proj_b", 1)).then_inc(S["prep_act"], 1)
            act.wait_ge(S["prep_act"], 4)
            act.wait_ge(S["prep_dve"], 2)

            def squares(t, u, h):
                if h == 0:
                    x_wait(act, t, u)
                    wait(act, "stats_ready", t - 1)
                a = slice(h * PIX // 4, (h + 1) * PIX // 4)
                nc.scalar.activation(XSQ[u % 2][:, a], X[u][:, a], ACT.Square).then_inc(S["xsq_ready"], 1)

            def q_squares(t):
                act.wait_ge(S["cen_ready"], t + 1)
                nc.scalar.activation(CSQ[:], CEN[:], ACT.Square, scale=1.0 / 16).then_inc(S["csq_ready"], 1)

            def q_log(t):
                act.wait_ge(S["varq_ready"], t + 1)
                wait(act, "rsq_ready", t)
                nc.scalar.activation(LNQ[:], pM[:, 256:512], ACT.Ln, bias=eps[:]).then_inc(S["lnq_ready"], 1)

            def pixel_log(t):
                act.wait_ge(S["sdp_ready"], t + 1)
                wait(act, "rstd_ready", t)
                nc.scalar.activation(LNV[:], SDP[:], ACT.Ln).then_inc(S["lnv_ready"], 1)

            def q_rsd(t):
                act.wait_ge(S["lnq_ready"], t + 1)
                wait(act, "xn_ready", t)
                nc.scalar.activation(RSQ[:], LNQ[:], ACT.Exp, scale=-0.5).then_inc(S["rsq_ready"], 1)

            def pixel_rstd(t, u):
                act.wait_ge(S["lnv_ready"], t + 1)
                wait(act, "er_ready", t - 1)
                wait(act, "logit_ready", t - 1)
                nc.scalar.activation(RSTD[u % 2][:], LNV[:], ACT.Exp, scale=-0.5).then_inc(S["rstd_ready"], 1)

            def q_affine(t):
                act.wait_ge(S["xn_ready"], t + 1)
                wait(act, "qproj_ready", t)
                nc.scalar.activation(XA[:], XN[:], ACT.Identity, bias=w("lnq_b", 1), scale=lnq_w16[:]).then_inc(S["xa_ready"], 1)

            def q_copy(t, u):
                act.wait_ge(S["qproj_ready"], t + 1)
                wait(act, "prod_ready", CHUNKS * (t - 1))
                nc.scalar.activation(Q[u % 2][:], pM[:, 0:256], ACT.Copy, scale=64.0 ** -0.5).then_inc(S["q_ready"], 1)

            def mean_squares(t):
                act.wait_ge(S["stats_ready"], t + 1)
                wait(act, "var_ready", t)
                nc.scalar.activation(MSQ[:], pMU[:], ACT.Square).then_inc(S["msq_ready"], 1)

            def project_out(t):
                act.wait_ge(S["pj_mm"], t + 1)
                wait(act, "h1_ready", t)
                nc.scalar.activation(PJ[:], pM[:, 256:512], ACT.Identity, bias=proj_bias[:]).then_inc(S["pj_ready"], 1)

            def spread(t, g):
                act.wait_ge(S["wbc_ready"], CHUNKS * t + (g + 1))
                wait(act, "vw_ready", CHUNKS * t + (g - 1))
                nc.scalar.activation(WBC[g % 2][:], pB[g % 2][:], ACT.Copy).then_inc(S["wbc_copied"], 1)

            def exponent(t):
                act.wait_ge(S["shift_ready"], t + 1)
                wait(act, "wt_ready", t)
                nc.scalar.activation(EX[:], LS[:], ACT.Exp).then_inc(S["exp_ready"], 1)

            def weights_hi(t):
                act.wait_ge(S["wt_ready"], t + 1)
                wait(act, "wbc_ready", CHUNKS * t)
                nc.scalar.activation(WHI[:], WT[:], ACT.Copy).then_inc(S["whi_ready"], 1)

            for h in range(4):
                squares(0, 0, h)
            q_squares(0)
            q_log(0)
            q_rsd(0)
            q_affine(0)
            q_copy(0, 0)
            for h in range(4):
                squares(1, 1, h)

            def step(t, u):
                if has(t - 2):
                    project_out(t - 2)
                if has(t):
                    mean_squares(t)
                for g in range(CHUNKS + LAG):
                    if has(t - 1) and g >= LAG:
                        spread(t - 1, g - LAG)
                    if has(t + 1):
                        if g == 1:
                            q_squares(t + 1)
                        if g == 4:
                            q_log(t + 1)
                        if g == 6:
                            q_affine(t + 1)
                        if g == 8:
                            q_copy(t + 1, u + 1)
                    if g == 4:
                        if has(t):
                            pixel_log(t)
                        if has(t + 1):
                            q_rsd(t + 1)
                        if has(t):
                            pixel_rstd(t, u)
                    if g in (1, 3, 6, 8) and has(t + 2):
                        squares(t + 2, (u + 2) % 4, (1, 3, 6, 8).index(g))
                if has(t):
                    exponent(t)
                    weights_hi(t)

            run_steps(act, step)
            project_out(PAIRS - 1)

        @block.tensor
        def _(pe):
            pe.wait_ge(S["consts_loaded"], 32)
            pe.wait_ge(S["prep_dve"], 1)
            nc.tensor.matmul(pM[:, 0:128], c("centre", 128), kv_fold[:], start=True, stop=True).then_inc(S["prep_pe"], 1)
            nc.tensor.matmul(pB0[:, 0:1], w("wv_swapped", 128), w("lnkv_b", 1), start=True, stop=True).then_inc(S["prep_pe"], 1)
            pe.wait_ge(S["prep_act"], 3)
            nc.tensor.matmul(pB0[:, 2:3], w("proj", 128), v_bias[:], start=True, stop=True).then_inc(S["prep_pe"], 1)
            pe.wait_ge(S["prep_act"], 4)

            def q_mean(t, u):
                pe.wait_ge(S["sum_ready"], t + 1)
                wait(pe, "pj_ready", t - 2)
                wait(pe, "q_ready", t)
                nc.tensor.matmul(pM[:, 0:256], c("mean", 128), SUM[u][:], start=True, stop=True).then_inc(S["mean_ready"], 1)

            def q_var(t):
                pe.wait_ge(S["csq_ready"], t + 1)
                nc.tensor.matmul(pM[:, 256:512], c("mean", 128), CSQ[:], start=True, stop=True).then_inc(S["varq_ready"], 1)

            def q_project(t):
                pe.wait_ge(S["xa_ready"], t + 1)
                nc.tensor.matmul(pM[:, 0:256], w("wq", 128), XA[:], start=True, stop=True).then_inc(S["qproj_ready"], 1)

            def statistics(t, u):
                x_wait(pe, t, u)
                pe.wait_ge(S["xsq_ready"], 4 * t + 4)
                wait(pe, "var_ready", t)
                wait(pe, "wbc_copied", CHUNKS * (t - 1))
                for src, dst in ((XSQ[u % 2], pEX), (X[u], pMU)):
                    if dst is pMU:
                        wait(pe, "logit_ready", t)
                    for sub in range(2):
                        for r in range(2):
                            for q in range(4):
                                last = nc.tensor.matmul(
                                    dst[32 * q:32 * q + 32, 256 * r:256 * r + 256], c(f"mean{sub}", 32),
                                    patch_row(src, 2 * (2 * q + sub) + r), start=(sub == 0 and r == 0),
                                    stop=(sub == 1), skip_group_check=True)
                last.then_inc(S["stats_ready"], 1)

            def logits(t):
                pe.wait_ge(S["prod_ready"], CHUNKS * t + CHUNKS)
                wait(pe, "var_ready", t + 1)
                for sub in range(2):
                    for q in range(4):
                        g = 2 * q + sub
                        last = nc.tensor.matmul(pL[32 * q:32 * q + 32, :], c(f"head{sub}", 32), PROD[:, 512 * g:512 * g + 512],
                                                start=(sub == 0), stop=(sub == 1))
                last.then_inc(S["log_ready"], 1)

            def keys_values(t, u, p):
                g = p - LAG
                k, v = has(t) and p < CHUNKS, has(t - 1) and g >= 0
                if k and p >= 2:
                    wait(pe, "prod_ready", CHUNKS * t + (p - 1))
                if v:
                    wait(pe, "vw_ready", CHUNKS * t + (g - CHUNKS - 1))
                    spread_weights(t - 1, g)
                for r in range(2):
                    o = slice(256 * r, 256 * r + 256)
                    if k:
                        for i in (0, 64):
                            last_k = nc.tensor.matmul(pK[p % 2][i:i + 64, o], kv_w[i:i + 64, 0:64],
                                                      patch_row(X[u], 2 * p + r)[i:i + 64], start=True, stop=True)
                    if v:
                        for i in (0, 64):
                            last_v = nc.tensor.matmul(pV[g % 2][64 - i:128 - i, o], kv_w[i:i + 64, 64:128],
                                                      patch_row(X[(u + 3) % 4], 2 * g + r)[i:i + 64], start=True, stop=True)
                if k:
                    last_k.then_inc(S["k_ready"], 1)
                if v:
                    last_v.then_inc(S["v_ready"], 1)

            def spread_weights(t, g):
                if g == 0:
                    pe.wait_ge(S["whi_ready"], t + 1)
                    pe.wait_ge(S["wlo_ready"], t + 1)
                wait(pe, "wbc_copied", CHUNKS * t + (g - 1))
                if g == 1:
                    wait(pe, "var_ready", t + 2 if has(t + 1) else PAIRS)
                rows = spread_heads[:, 128 * g:128 * g + 128]
                nc.tensor.matmul(pB[g % 2][:], rows, WHI[:], start=True, stop=False)
                nc.tensor.matmul(pB[g % 2][:], rows, WLO[:], start=False, stop=True).then_inc(S["wbc_ready"], 1)

            def project(t, u):
                pe.wait_ge(S["ag_ready"], CHUNKS * t + CHUNKS)
                wait(pe, "q_ready", t + 3 if has(t + 2) else PAIRS)
                nc.tensor.matmul(pM[:, 256:512], w("proj", 128), AG[u % 2][:], start=True, stop=True).then_inc(S["pj_mm"], 1)

            q_mean(0, 0)
            statistics(0, 0)
            q_var(0)
            q_project(0)

            def step(t, u):
                for g in range(CHUNKS + LAG):
                    keys_values(t, u, g)
                    if has(t + 1):
                        if g == 0:
                            q_mean(t + 1, (u + 1) % 4)
                        if g == 3:
                            q_var(t + 1)
                        if g == 7:
                            q_project(t + 1)
                if has(t):
                    logits(t)
                if has(t + 1):
                    statistics(t + 1, (u + 1) % 4)
                if has(t - 1):
                    project(t - 1, u + 3)

            run_steps(pe, step)

        @block.vector
        def _(dve):
            dve.wait_ge(S["consts_loaded"], 32)
            nc.vector.tensor_scalar(kv_fold[:], w("wkv", 128), w("lnkv_w", 1), None, ALU.mult).then_inc(S["prep_dve"], 1)
            nc.vector.tensor_scalar(lnq_w16[:], w("lnq_w", 1), 1.0 / 16, None, ALU.mult).then_inc(S["prep_dve"], 1)

            def q_centre(t, u):
                dve.wait_ge(S["mean_ready"], t + 1)
                wait(dve, "csq_ready", t)
                wait(dve, "xn_ready", t)
                nc.vector.tensor_tensor(CEN[:], SUM[u][:], pM[:, 0:256], ALU.subtract).then_inc(S["cen_ready"], 1)

            def q_norm(t):
                dve.wait_ge(S["rsq_ready"], t + 1)
                wait(dve, "xa_ready", t)
                nc.vector.tensor_tensor(XN[:], CEN[:], RSQ[:], ALU.mult).then_inc(S["xn_ready"], 1)

            def pixel_var(t):
                dve.wait_ge(S["msq_ready"], t + 1)
                wait(dve, "sdp_ready", t)
                nc.vector.tensor_tensor(VAR[:], pEX[:], MSQ[:], ALU.subtract).then_inc(S["var_ready"], 1)
                dve.wait_ge(S["var_ready"], t + 1)
                wait(dve, "rstd_ready", t)
                nc.vector.tensor_scalar(SDP[:], VAR[:], 0.0, LN_EPS, ALU.max, ALU.add).then_inc(S["sdp_ready"], 1)

            def products(t, u, g):
                dve.wait_ge(S["k_ready"], CHUNKS * t + (g + 1))
                if g == 0:
                    dve.wait_ge(S["q_ready"], t + 1)
                    wait(dve, "log_ready", t)
                nc.vector.tensor_tensor(by_patch(PROD[:, 512 * g:512 * g + 512]), by_patch(pK[g % 2][:]),
                                        over_pixels(Q[u % 2][:, 32 * g:32 * g + 32]), ALU.mult).then_inc(S["prod_ready"], 1)

            def values(t, g):
                dve.wait_ge(S["v_ready"], CHUNKS * t + (g + 1))
                dve.wait_ge(S["wbc_copied"], CHUNKS * t + (g + 1))
                wait(dve, "ag_ready", CHUNKS * t + (g - 1))
                nc.vector.tensor_tensor(VW[g % 2][:], pV[g % 2][:], WBC[g % 2][:], ALU.mult).then_inc(S["vw_ready"], 1)

            def value_sums(t, u, g):
                dve.wait_ge(S["vw_ready"], CHUNKS * t + (g + 1))
                if g == 0:
                    wait(dve, "pj_mm", t - 1)
                nc.vector.tensor_reduce(AG[u % 2][:, 32 * g:32 * g + 32], by_patch(VW[g % 2][:]), AX.X,
                                        ALU.add).then_inc(S["ag_ready"], 1)

            def h1_sum(t, u):
                dve.wait_ge(S["pj_ready"], t + 1)
                if not isinstance(t, int) or t >= 2:
                    dve.wait_ge(h1_stored[u % 2], 8 * (t - u % 2))
                nc.vector.scalar_tensor_tensor(H1[u % 2][:], SUM[u % 4][:], 1.0 / 16, PJ[:], ALU.mult,
                                               ALU.add).then_inc(S["h1_ready"], 1)

            def softmax_logits(t, u):
                dve.wait_ge(S["log_ready"], t + 1)
                dve.wait_ge(S["rstd_ready"], t + 1)
                wait(dve, "shift_ready", t)
                nc.vector.tensor_tensor(LG[:], pL[:], RSTD[u % 2][:], ALU.mult).then_inc(S["logit_ready"], 1)
                dve.wait_ge(S["logit_ready"], t + 1)
                nc.vector.tensor_reduce(MX[:], by_patch(LG[:]), AX.X, ALU.max).then_inc(S["max_ready"], 1)
                dve.wait_ge(S["max_ready"], t + 1)
                wait(dve, "exp_ready", t)
                nc.vector.tensor_tensor(by_patch(LS[:]), by_patch(LG[:]), over_pixels(MX[:]),
                                        ALU.subtract).then_inc(S["shift_ready"], 1)

            def softmax_weights(t):
                dve.wait_ge(S["exp_ready"], t + 1)
                wait(dve, "rz_ready", t)
                nc.vector.tensor_reduce(ZS[:], by_patch(EX[:]), AX.X, ALU.add).then_inc(S["z_ready"], 1)
                dve.wait_ge(S["z_ready"], t + 1)
                wait(dve, "wt_ready", t)
                nc.vector.reciprocal(RZ[:], ZS[:]).then_inc(S["rz_ready"], 1)
                dve.wait_ge(S["rz_ready"], t + 1)
                dve.wait_ge(S["er_ready"], t + 1)
                wait(dve, "wlo_ready", t)
                nc.vector.tensor_tensor(by_patch(WT[:]), by_patch(ER[:]), over_pixels(RZ[:]),
                                        ALU.mult).then_inc(S["wt_ready"], 1)

            def weights_lo(t):
                dve.wait_ge(S["whi_ready"], t + 1)
                nc.vector.tensor_tensor(WLO[:], WT[:], WHI[:].bitcast(F32), ALU.subtract).then_inc(S["wlo_ready"], 1)

            q_centre(0, 0)
            q_norm(0)

            def step(t, u):
                if has(t - 2):
                    h1_sum(t - 2, u + 2)
                for g in range(CHUNKS + LAG):
                    if has(t) and g < CHUNKS:
                        products(t, u, g)
                    if has(t) and g == 0:
                        pixel_var(t)
                    if has(t - 1) and g >= LAG:
                        values(t - 1, g - LAG)
                        if g > LAG:
                            value_sums(t - 1, u + 3, g - LAG - 1)
                    if has(t + 1):
                        if g == 0:
                            q_centre(t + 1, (u + 1) % 4)
                        if g == 5:
                            q_norm(t + 1)
                if has(t - 1):
                    value_sums(t - 1, u + 3, CHUNKS - 1)
                if has(t):
                    softmax_logits(t, u)
                    softmax_weights(t)
                    weights_lo(t)

            run_steps(dve, step)
            h1_sum(PAIRS - 1, 3)
def linear_attention_phase(nc, held, h1, wpack, cpack, h2_out):
    with ExitStack() as ctx:
        def sb(name, shape, dt=F32):
            return ctx.enter_context(nc.sbuf_tensor("b_" + name, shape, dt))

        wsb = sb("wsb", [128, B_W["end"]])
        csb = sb("csb", [128, B_C["end"]])

        def w(name, width):
            return wsb[:, B_W[name]:B_W[name] + width]

        def c(name, width):
            return csb[:, B_C[name]:B_C[name] + width]

        w_raw = sb("w_raw", [128, 256])
        w_mid = sb("w_mid", [128, 256])
        w_mean = sb("w_mean", [128, 2])
        w_all = sb("w_all", [128, 256])
        bias = sb("bias", [128, 256])
        b_mean = sb("b_mean", [128, 2])
        w_out16 = sb("w_out16", [128, 64])
        eps = sb("eps", [128, 1])

        H = [sb(f"h{k}", [128, 512]) for k in range(4)]
        HT = [sb(f"ht{k}", [128, 512]) for k in range(2)]
        HSQ = sb("hsq", [128, 512])
        S1, S2, M2, V0, V1 = (sb(n, [128, 8]) for n in ("s1", "s2", "m2", "v0", "v1"))
        SD1 = sb("sd1", [128, 8])
        RSTD = sb("rstd", [128, 8])
        QKV = [sb(f"qkv{k}", [128, 4, 4, 128]) for k in range(4)]
        Q2 = sb("q2", [128, 512])
        K2 = sb("k2", [128, 512])
        SS, SE, F = (sb(n, [128, 16]) for n in ("ss", "se", "f"))
        Q2N = [sb(f"q2n{k}", [128, 512]) for k in range(2)]
        K2N = [sb(f"k2n{k}", [128, 512]) for k in range(2)]
        VOH = [sb(f"voh{k}", [128, 512]) for k in range(2)]
        Q2S = sb("q2s", [128, 512])
        K2S = [sb(f"k2s{k}", [128, 512]) for k in range(2)]
        NQ = sb("nq", [128, 8])
        NQM = [sb(f"nqm{k}", [128, 8]) for k in range(2)]
        SDQ, RQ = sb("sdq", [128, 8]), sb("rq", [128, 8])
        QT = sb("qt", [128, 512])
        KVD = sb("kvd", [128, 2, 128])
        NKM, SDK, RK = (sb(n, [128, 2]) for n in ("nkm", "sdk", "rk"))
        MX = sb("mx", [128, 2, 128])
        O1 = sb("o1", [128, 512])
        H2 = [sb(f"h2_{k}", [128, 512]) for k in range(2)]

        def bank(name):
            return ctx.enter_context(nc.psum_tensor("b_" + name, [128, 512], F32))

        pT, pQT, pKV, pOUT = (bank(n) for n in ("pt", "pqt", "pkv", "pout"))
        pQ = [bank(f"pq{k}") for k in range(4)]

        names = ("consts_loaded prep_pe prep_act prep_dve prep_pool ht_mm qkv_mm kv_mm qt_mm m_mm out_mm "
                 "ht_ready hsq_ready sums_ready m2_ready v0_ready v1_ready sd1_ready rstd_ready qkv_ready "
                 "sq_ready ss_ready se_ready f_ready scaled_ready voh_ready q2s_ready k2s_ready nq_ready nqm_ready "
                 "sdq_ready rq_ready qt_ready kvd_ready nkm_ready sdk_ready rk_ready mx_ready o1_ready h2_ready").split()
        S = {n: new_semaphore(nc, held, "b_" + n) for n in names}
        h_loaded = [new_semaphore(nc, held, f"b_h_loaded{k}") for k in range(4)]
        h2_stored = [new_semaphore(nc, held, f"b_h2_stored{k}") for k in range(2)]

        def wait(eng, name, value):
            if not isinstance(value, int) or value > 0:
                eng.wait_ge(S[name], value)

        def has(t):
            return not isinstance(t, int) or 0 <= t < GROUPS

        def run_steps(eng, step):
            for t in range(4):
                step(t, t)
            with eng.Fori(0, GROUPS // 4 - 2) as j:
                for u in range(4):
                    step(4 * j + (4 + u), u)
            for t in range(GROUPS - 4, GROUPS + 2):
                step(t, t % 4)

        def tiles(ap):
            return ap.rearrange("p (k c) -> p k c", c=64)

        def by_half(ap):
            return ap.rearrange("p (q c) -> p q c", c=128)

        def each(ap, n=64):
            return ap.unsqueeze(2).broadcast_to([128, ap.shape[1], n])

        h1_view = h1.rearrange("(s j) p f -> s p j f", j=2)

        block = ctx.enter_context(nc.Block())

        @block.sync
        def _(sp):
            sp.dma_start(wsb[:], wpack).then_inc(S["consts_loaded"], 16)
            sp.dma_start(csb[:], cpack).then_inc(S["consts_loaded"], 16)

            def load(t, u):
                wait(sp, "qkv_mm", 2 * (t - 3))
                sp.dma_start(H[u][:].rearrange("p (j f) -> p j f", j=2),
                             h1_view[bass.ds(t, 1)].rearrange("o p j f -> (o p) j f")).then_inc(h_loaded[u], 16)

            def store(t, u):
                sp.wait_ge(S["h2_ready"], t + 1)
                sp.dma_start(h2_out[bass.ds(t, 1)].rearrange("o p f -> (o p) f"), H2[u % 2][:]).then_inc(h2_stored[u % 2], 16)

            for t in range(3):
                load(t, t)

            def step(t, u):
                if has(t + 3):
                    load(t + 3, (u + 3) % 4)
                if has(t - 2):
                    store(t - 2, (u + 2) % 4)

            run_steps(sp, step)
            for k in range(2):
                sp.wait_ge(h2_stored[k], 16 * GROUPS // 2)

        @block.gpsimd
        def _(pool):
            nc.gpsimd.memset(eps[:], LN_EPS).then_inc(S["prep_pool"], 1)
            nc.gpsimd.memset(KVD[:], 0.0).then_inc(S["prep_pool"], 1)
            nc.gpsimd.memset(MX[:], 0.0).then_inc(S["prep_pool"], 1)

            def scale(t, u):
                pool.wait_ge(S["f_ready"], t + 1)
                wait(pool, "qt_mm", t - 1)
                nc.gpsimd.tensor_tensor(tiles(Q2N[u % 2][:]), tiles(Q2[:]), each(F[:, 0:8]), ALU.mult).then_inc(S["scaled_ready"], 1)
                nc.gpsimd.tensor_tensor(tiles(K2N[u % 2][:]), tiles(K2[:]), each(F[:, 8:16]), ALU.mult).then_inc(S["scaled_ready"], 1)
                wait(pool, "h2_ready", t - 1)
                nc.gpsimd.tensor_tensor(by_half(VOH[u % 2][:]), QKV[u][:, :, 3, :], by_half(HT[u % 2][:]), ALU.add).then_inc(S["voh_ready"], 1)

            def step(t, u):
                if has(t - 1):
                    scale(t - 1, (u + 3) % 4)

            run_steps(pool, step)

        @block.scalar
        def _(act):
            act.wait_ge(S["prep_pe"], 1)
            nc.scalar.activation(w_raw[:, 192:256], pQ[0][:, 0:64], ACT.Copy).then_inc(S["prep_act"], 1)
            nc.scalar.activation(w_raw[:, 0:192], w("wqkv", 192), ACT.Copy).then_inc(S["prep_act"], 1)
            act.wait_ge(S["prep_pe"], 2)
            nc.scalar.activation(w_mid[:], pQ[1][:, 0:256], ACT.Copy).then_inc(S["prep_act"], 1)
            act.wait_ge(S["prep_pool"], 3)

            def transposed(t, u):
                act.wait_ge(S["ht_mm"], t + 1)
                wait(act, "voh_ready", t - 1)
                nc.scalar.activation(HT[u % 2][:], pT[:], ACT.Copy).then_inc(S["ht_ready"], 1)
                wait(act, "sums_ready", 2 * t)
                nc.scalar.activation(HSQ[:], pT[:], ACT.Square).then_inc(S["hsq_ready"], 1)

            def squares(t, u):
                act.wait_ge(S["qkv_ready"], 8 * t + 8)
                wait(act, "scaled_ready", 2 * t)
                nc.scalar.activation(by_half(Q2[:]), QKV[u][:, :, 0, :], ACT.Square).then_inc(S["sq_ready"], 1)
                nc.scalar.activation(by_half(K2[:]), QKV[u][:, :, 1, :], ACT.Square).then_inc(S["sq_ready"], 1)

            def products_out(t):
                act.wait_ge(S["qt_mm"], t + 1)
                wait(act, "out_mm", t)
                nc.scalar.activation(QT[:], pQT[:], ACT.Copy).then_inc(S["qt_ready"], 1)
                act.wait_ge(S["kv_mm"], t + 1)
                wait(act, "m_mm", t)
                for i in range(2):
                    r = slice(64 * i, 64 * i + 64)
                    nc.scalar.activation(KVD[r, :, r], pKV[r, 0:256].rearrange("p (j c) -> p j c", j=2)[:, :, r],
                                         ACT.Copy).then_inc(S["kvd_ready"], 1)

            def fourths(t, u):
                act.wait_ge(S["scaled_ready"], 2 * t + 2)
                wait(act, "nq_ready", t)
                nc.scalar.activation(Q2S[:], Q2N[u % 2][:], ACT.Square).then_inc(S["q2s_ready"], 1)
                wait(act, "kv_mm", t - 1)
                nc.scalar.activation(K2S[u % 2][:], K2N[u % 2][:], ACT.Square).then_inc(S["k2s_ready"], 1)

            def roots(t, u):
                if has(t):
                    act.wait_ge(S["v1_ready"], t + 1)
                    wait(act, "rstd_ready", t)
                    nc.scalar.activation(SD1[:], V1[:], ACT.Sqrt, bias=eps[:]).then_inc(S["sd1_ready"], 1)
                if has(t - 2):
                    act.wait_ge(S["nqm_ready"], t - 1)
                    wait(act, "rq_ready", t - 2)
                    nc.scalar.activation(SDQ[:], NQM[u % 2][:], ACT.Sqrt).then_inc(S["sdq_ready"], 1)
                    act.wait_ge(S["nkm_ready"], t - 1)
                    wait(act, "rk_ready", t - 2)
                    nc.scalar.activation(SDK[:], NKM[:], ACT.Sqrt).then_inc(S["sdk_ready"], 1)

            def step(t, u):
                if has(t):
                    transposed(t, u)
                if has(t - 1):
                    squares(t - 1, (u + 3) % 4)
                if has(t - 2):
                    products_out(t - 2)
                roots(t, u)
                if has(t - 1):
                    fourths(t - 1, (u + 3) % 4)

            run_steps(act, step)

        @block.tensor
        def _(pe):
            pe.wait_ge(S["consts_loaded"], 32)
            nc.tensor.matmul(pQ[0][:, 0:64], wsb[0:64, B_W["wv_t"]:B_W["wv_t"] + 128], wsb[0:64, B_W["w_out"]:B_W["w_out"] + 64],
                             start=True, stop=True)
            nc.tensor.matmul(pQ[2][:, 0:64], wsb[0:64, B_W["bv_rep"]:B_W["bv_rep"] + 128], wsb[0:64, B_W["w_out"]:B_W["w_out"] + 64],
                             start=True, stop=True).then_inc(S["prep_pe"], 1)
            pe.wait_ge(S["prep_act"], 2)
            nc.tensor.matmul(pQ[1][:, 0:256], c("centre", 128), w_raw[:], start=True, stop=True).then_inc(S["prep_pe"], 1)
            pe.wait_ge(S["prep_dve"], 8)

            def transpose_in(t, u):
                pe.wait_ge(h_loaded[u], 4 * (t - u) + 16)
                wait(pe, "ht_ready", t)
                wait(pe, "hsq_ready", t)
                for q in range(4):
                    last = nc.tensor.transpose(pT[:, 128 * q:128 * q + 128], H[u][:, 128 * q:128 * q + 128], c("ident", 128))
                last.then_inc(S["ht_mm"], 1)

            def project(t, u):
                for j in range(2):
                    wait(pe, "qkv_ready", 8 * (t - 1) + 4 * j + 4)
                    for h in range(2):
                        for i in range(2):
                            r = slice(64 * i, 64 * i + 64)
                            q = 2 * j + h
                            last = nc.tensor.matmul(pQ[2 * j + i][:, 256 * h:256 * h + 256], H[u][r, 128 * q:128 * q + 128],
                                                    w_all[r, :], start=True, stop=True)
                    last.then_inc(S["qkv_mm"], 1)

            def products(t, u):
                pe.wait_ge(S["scaled_ready"], 2 * t + 2)
                wait(pe, "qt_ready", t)
                for q in range(4):
                    last = nc.tensor.transpose(pQT[:, 128 * q:128 * q + 128], Q2N[u % 2][:, 128 * q:128 * q + 128], c("ident", 128))
                last.then_inc(S["qt_mm"], 1)
                pe.wait_ge(S["k2s_ready"], t + 1)
                wait(pe, "mx_ready", 2 * t)
                for j in range(2):
                    for h in range(2):
                        q = 2 * j + h
                        nc.tensor.matmul(pKV[:, 128 * j:128 * j + 128], QKV[u][:, q, 2, :],
                                         K2N[u % 2][:, 128 * q:128 * q + 128], start=(h == 0), stop=(h == 1))
                for j in range(2):
                    for h in range(2):
                        q = 2 * j + h
                        last = nc.tensor.matmul(pKV[:, 256 + j:257 + j], K2S[u % 2][:, 128 * q:128 * q + 128], c("ones", 1),
                                                start=(h == 0), stop=(h == 1))
                last.then_inc(S["kv_mm"], 1)

            def fold_output(t):
                pe.wait_ge(S["kvd_ready"], 2 * t + 2)
                pe.wait_ge(S["nkm_ready"], t + 1)
                for j in range(2):
                    last = nc.tensor.matmul(pKV[:, 384 + 64 * j:448 + 64 * j], KVD[:, j, :], w_out16[:], start=True, stop=True)
                last.then_inc(S["m_mm"], 1)

            def outputs(t):
                pe.wait_ge(S["mx_ready"], 2 * t + 2)
                wait(pe, "o1_ready", t)
                for q in range(4):
                    last = nc.tensor.matmul(pOUT[:, 128 * q:128 * q + 128], QT[:, 128 * q:128 * q + 128], MX[:, q // 2, :],
                                            start=True, stop=True)
                last.then_inc(S["out_mm"], 1)

            def step(t, u):
                if has(t):
                    transpose_in(t, u)
                if has(t - 2):
                    products(t - 2, (u + 2) % 4)
                if has(t):
                    project(t, u)
                if has(t - 2):
                    fold_output(t - 2)
                    outputs(t - 2)

            run_steps(pe, step)

        @block.vector
        def _(dve):
            dve.wait_ge(S["consts_loaded"], 32)
            nc.vector.tensor_scalar(w_out16[:], w("w_out", 64), 1.0 / 16, None, ALU.mult).then_inc(S["prep_dve"], 1)
            bqk = w("bias", 128).rearrange("p (a c) -> p a c", a=2)
            nc.vector.tensor_reduce(b_mean[:], bqk, AX.X, ALU.add).then_inc(S["prep_dve"], 1)
            dve.wait_ge(S["prep_dve"], 2)
            nc.vector.scalar_tensor_tensor(bias[:, 0:128].rearrange("p (a c) -> p a c", a=2), each(b_mean[:]), -1.0 / 64, bqk,
                                           ALU.mult, ALU.add).then_inc(S["prep_dve"], 1)
            nc.vector.tensor_copy(bias[:, 128:192], wsb[:, B_W["bias"] + 128:B_W["bias"] + 192]).then_inc(S["prep_dve"], 1)
            dve.wait_ge(S["prep_pe"], 1)
            nc.vector.tensor_tensor(bias[:, 192:256], pQ[2][:, 0:64], w("b_out", 64), ALU.add).then_inc(S["prep_dve"], 1)
            dve.wait_ge(S["prep_act"], 3)
            wqk = w_mid[:, 0:128].rearrange("p (a c) -> p a c", a=2)
            nc.vector.tensor_reduce(w_mean[:], wqk, AX.X, ALU.add).then_inc(S["prep_dve"], 1)
            dve.wait_ge(S["prep_dve"], 6)
            nc.vector.scalar_tensor_tensor(w_all[:, 0:128].rearrange("p (a c) -> p a c", a=2), each(w_mean[:]), -1.0 / 64, wqk,
                                           ALU.mult, ALU.add).then_inc(S["prep_dve"], 1)
            nc.vector.tensor_copy(w_all[:, 128:256], w_mid[:, 128:256]).then_inc(S["prep_dve"], 1)
            dve.wait_ge(S["prep_dve"], 8)
            dve.wait_ge(S["prep_pool"], 3)

            def statistics(t, u):
                dve.wait_ge(S["ht_ready"], t + 1)
                wait(dve, "v0_ready", t)
                nc.vector.tensor_reduce(S1[:], tiles(HT[u % 2][:]), AX.X, ALU.add).then_inc(S["sums_ready"], 1)
                dve.wait_ge(S["hsq_ready"], t + 1)
                nc.vector.tensor_reduce(S2[:], tiles(HSQ[:]), AX.X, ALU.add).then_inc(S["sums_ready"], 1)
                dve.wait_ge(S["sums_ready"], 2 * t + 2)
                nc.vector.tensor_tensor(M2[:], S1[:], S1[:], ALU.mult).then_inc(S["m2_ready"], 1)
                dve.wait_ge(S["m2_ready"], t + 1)
                nc.vector.scalar_tensor_tensor(V0[:], S2[:], 64.0, M2[:], ALU.mult, ALU.subtract).then_inc(S["v0_ready"], 1)
                dve.wait_ge(S["v0_ready"], t + 1)
                wait(dve, "sd1_ready", t)
                nc.vector.tensor_scalar(V1[:], V0[:], 1.0 / 4096, 0.0, ALU.mult, ALU.max).then_inc(S["v1_ready"], 1)

            def square_sums(t):
                dve.wait_ge(S["sq_ready"], 2 * t + 2)
                wait(dve, "se_ready", t)
                nc.vector.tensor_reduce(SS[:, 0:8], tiles(Q2[:]), AX.X, ALU.add).then_inc(S["ss_ready"], 1)
                nc.vector.tensor_reduce(SS[:, 8:16], tiles(K2[:]), AX.X, ALU.add).then_inc(S["ss_ready"], 1)
                dve.wait_ge(S["ss_ready"], 2 * t + 2)
                wait(dve, "f_ready", t)
                nc.vector.tensor_scalar(SE[:], SS[:], DIV_EPS, None, ALU.add).then_inc(S["se_ready"], 1)
                dve.wait_ge(S["se_ready"], t + 1)
                wait(dve, "scaled_ready", 2 * t)
                nc.vector.reciprocal(F[:], SE[:]).then_inc(S["f_ready"], 1)

            def key_norms(t):
                dve.wait_ge(S["kvd_ready"], 2 * t + 2)
                wait(dve, "sdk_ready", t)
                nc.vector.tensor_scalar(NKM[:], pKV[:, 256:258], NORM_EPS ** 2, None, ALU.max).then_inc(S["nkm_ready"], 1)

            def query_norms(t, u):
                dve.wait_ge(S["q2s_ready"], t + 1)
                wait(dve, "nqm_ready", t)
                nc.vector.tensor_reduce(NQ[:], tiles(Q2S[:]), AX.X, ALU.add).then_inc(S["nq_ready"], 1)
                dve.wait_ge(S["nq_ready"], t + 1)
                wait(dve, "sdq_ready", t - 1)
                nc.vector.tensor_scalar(NQM[u % 2][:], NQ[:], NORM_EPS ** 2, None, ALU.max).then_inc(S["nqm_ready"], 1)

            def scale_projections(t, u):
                dve.wait_ge(S["sd1_ready"], t + 1)
                nc.vector.reciprocal(RSTD[:], SD1[:]).then_inc(S["rstd_ready"], 1)
                dve.wait_ge(S["rstd_ready"], t + 1)
                wait(dve, "voh_ready", t - 3)
                wait(dve, "kv_mm", t - 3)
                for j in range(2):
                    dve.wait_ge(S["qkv_mm"], 2 * t + (j + 1))
                    for h in range(2):
                        for i in range(2):
                            q = 2 * j + h
                            nc.vector.scalar_tensor_tensor(
                                QKV[u][:, q, :, 64 * i:64 * i + 64],
                                pQ[2 * j + i][:, 256 * h:256 * h + 256].rearrange("p (b c) -> p b c", b=4),
                                RSTD[:, 2 * q + i:2 * q + i + 1], bias[:].rearrange("p (b c) -> p b c", b=4),
                                ALU.mult, ALU.add).then_inc(S["qkv_ready"], 1)

            def fold_norms(t):
                dve.wait_ge(S["sdk_ready"], t + 1)
                nc.vector.reciprocal(RK[:], SDK[:]).then_inc(S["rk_ready"], 1)
                dve.wait_ge(S["sdq_ready"], t + 1)
                nc.vector.reciprocal(RQ[:], SDQ[:]).then_inc(S["rq_ready"], 1)
                dve.wait_ge(S["m_mm"], t + 1)
                dve.wait_ge(S["rk_ready"], t + 1)
                wait(dve, "out_mm", t)
                dve.wait_ge(S["kvd_ready"], 2 * t + 2)
                for i in range(2):
                    r = slice(64 * i, 64 * i + 64)
                    nc.vector.tensor_tensor(MX[r, :, r], pKV[r, 384:512].rearrange("p (j c) -> p j c", j=2),
                                            RK[r, :].unsqueeze(2).broadcast_to([64, 2, 64]), ALU.mult).then_inc(S["mx_ready"], 1)

            def finish(t, u):
                dve.wait_ge(S["out_mm"], t + 1)
                dve.wait_ge(S["rq_ready"], t + 1)
                wait(dve, "h2_ready", t)
                nc.vector.tensor_tensor(tiles(O1[:]), tiles(pOUT[:]), each(RQ[:]), ALU.mult).then_inc(S["o1_ready"], 1)
                dve.wait_ge(S["o1_ready"], t + 1)
                dve.wait_ge(S["voh_ready"], t + 1)
                if not isinstance(t, int) or t >= 2:
                    dve.wait_ge(h2_stored[u % 2], 8 * (t - u % 2))
                nc.vector.tensor_tensor(H2[u % 2][:], O1[:], VOH[u % 2][:], ALU.add).then_inc(S["h2_ready"], 1)

            def step(t, u):
                if has(t):
                    statistics(t, u)
                if has(t - 1):
                    square_sums(t - 1)
                if has(t - 2):
                    key_norms(t - 2)
                if has(t):
                    scale_projections(t, u)
                if has(t - 2):
                    fold_norms(t - 2)
                    finish(t - 2, u)
                if has(t - 1):
                    query_norms(t - 1, (u + 1) % 2)

            run_steps(dve, step)
def causal_attention_phase(nc, held, h2, wpack, cpack, res_out, flat_out, gates_out):
    with ExitStack() as ctx:
        def sb(name, shape, dt=F32):
            return ctx.enter_context(nc.sbuf_tensor("c_" + name, shape, dt))

        wsb = sb("wsb", [128, C_W["end"]])
        csb = sb("csb", [128, C_C["end"]])

        def w(name, width):
            return wsb[:, C_W[name]:C_W[name] + width]

        def c(name, width):
            return csb[:, C_C[name]:C_C[name] + width]

        w_in = sb("w_in", [128, 3 * 128 + 64])
        w_img = sb("w_img", [128, 2, 3 * 128])
        ident_b = sb("ident_b", [128, 128], BF16)
        mask_b = sb("mask_b", [128, 2, 512], BF16)
        eps_ln = sb("eps_ln", [128, 1])
        eps_rms = sb("eps_rms", [128, 1])

        H2 = [sb(f"h2_{k}", [128, 512]) for k in range(4)]
        HSQ = sb("hsq", [128, 512])
        S1, S2, M2, V0, V1, VE, RV, MU2, NM, RS, SDM, RR = (
            sb(n, [128, 8]) for n in ("s1", "s2", "m2", "v0", "v1", "ve", "rv", "mu2", "nm", "rs", "sdm", "rr"))
        U0 = sb("u0", [128, 512])
        U = [sb(f"u_{k}", [128, 512]) for k in range(4)]
        UR = [sb(f"ur{k}", [128, 512]) for k in range(2)]
        URT = sb("urt", [128, 512])
        VT = [sb(f"vt{k}", [128, 4, 4, 32]) for k in range(2)]
        QC = [[sb(f"qc{k}_{i}", [128, 512]) for i in range(2)] for k in range(2)]
        KR = [[sb(f"kr{k}_{i}", [128, 512]) for i in range(2)] for k in range(2)]
        KC = [sb(f"kc{i}", [128, 512]) for i in range(2)]
        KS = [sb(f"ks{i}", [128, 512]) for i in range(2)]
        MX = [sb(f"mx{k}", [128, 4]) for k in range(3)]
        PR = [sb(f"pr{k}", [128, 512]) for k in range(4)]
        PTS = [sb(f"pts{k}", [128, 512]) for k in range(8)]
        SUM = [sb(f"sum{k}", [128, 4]) for k in range(4)]
        RSUM = [sb(f"rsum{k}", [128, 4]) for k in range(4)]
        YT = [sb(f"yt{k}", [128, 512]) for k in range(2)]
        X1 = sb("x1", [128, 512])
        XSQ = sb("xsq", [128, 512])
        S3, SDX, R2 = (sb(n, [128, 8]) for n in ("s3", "sdx", "r2"))
        XR = sb("xr", [128, 512])
        RES = [sb(f"res{k}", [128, 512]) for k in range(2)]
        FT = [sb(f"ft{k}", [128, 512]) for k in range(2)]
        RL, RLS, RE, RP, RK, SEL, W0 = (sb(n, [128, 64]) for n in ("rl", "rls", "re", "rp", "rk", "sel", "w0"))
        RMX, RZ, RRZ, WS, WSE, RWS = (sb(n, [128, 8]) for n in ("rmx", "rz", "rrz", "ws", "wse", "rws"))
        GT, EQ, EQM, BEFORE = (sb(n, [128, 512]) for n in ("gt", "eq", "eqm", "before"))
        G = [sb(f"g{k}", [128, 64]) for k in range(2)]

        def bank(name):
            return ctx.enter_context(nc.psum_tensor("c_" + name, [128, 512], F32))

        pS = [bank(f"ps{k}") for k in range(3)]
        pPT = [bank(f"ppt{k}") for k in range(2)]
        pYT = bank("pyt")
        pA, pB = bank("pa"), bank("pb")

        names = ("consts_loaded prep_act prep_dve prep_pool "
                 "hsq_ready sums_ready m2_ready v0_ready v1_ready ve_ready rv_ready mu2_ready nm_ready rs_ready "
                 "sdm_ready rr_ready u0_ready u_ready ur_ready ut_mm urt_ready v_mm vt_ready q_mm qc_ready "
                 "k_mm kc_ready ks_ready kr_ready scores_ready max_ready exp_ready rsum_ready probs_ready pt_mm "
                 "pts_even_ready pts_odd_ready pv_mm yt_ready wo_mm x1_ready xsq_ready s3_ready sdx_ready r2_ready xr_ready res_ready "
                 "ft_mm ft_ready router_mm rl_ready rmx_ready rls_ready re_ready rz_ready rrz_ready rp_ready "
                 "gt_ready eq_ready eqm_ready before_ready rank_ready sel_ready w0_ready ws_ready wse_ready rws_ready "
                 "g_ready").split()
        S = {n: new_semaphore(nc, held, "c_" + n) for n in names}
        h_loaded = [new_semaphore(nc, held, f"c_h_loaded{k}") for k in range(4)]
        res_stored, flat_stored, gates_stored = (
            [new_semaphore(nc, held, f"c_{n}_stored{k}") for k in range(2)] for n in ("res", "flat", "gates"))

        def wait(eng, name, value):
            if not isinstance(value, int) or value > 0:
                eng.wait_ge(S[name], value)

        def has(t):
            return not isinstance(t, int) or 0 <= t < GROUPS

        def run_steps(eng, step):
            for t in range(-2, 4):
                step(t, t % 4)
            with eng.Fori(0, GROUPS // 4 - 2) as j:
                for u in range(4):
                    step(4 * j + (4 + u), u)
            for t in range(GROUPS - 4, GROUPS + 3):
                step(t, t % 4)

        def slot_wait(eng, sems, t, u):
            if not isinstance(t, int) or t >= 2:
                eng.wait_ge(sems[u % 2], 8 * (t - u % 2))

        def tiles(ap, n=64):
            return ap.rearrange("p (k c) -> p k c", c=n)

        def each(ap, n=64):
            return ap.unsqueeze(2).broadcast_to([128, ap.shape[1], n])

        block = ctx.enter_context(nc.Block())

        @block.sync
        def _(sp):
            sp.dma_start(wsb[:], wpack).then_inc(S["consts_loaded"], 16)
            sp.dma_start(csb[:], cpack).then_inc(S["consts_loaded"], 16)

            def load(t, u):
                wait(sp, "res_ready", t - 3)
                sp.dma_start(H2[u][:], h2[bass.ds(t, 1)].rearrange("o p f -> (o p) f")).then_inc(h_loaded[u], 16)

            def store(t, u):
                sp.wait_ge(S["res_ready"], t + 1)
                sp.dma_start(res_out[bass.ds(t, 1)].rearrange("o p f -> (o p) f"), RES[u % 2][:]).then_inc(res_stored[u % 2], 16)

            def store_flat(t, u):
                sp.wait_ge(S["ft_ready"], t + 1)
                sp.dma_start(flat_out[bass.ds(t, 1)].rearrange("o p f -> (o p) f"), FT[u % 2][:]).then_inc(flat_stored[u % 2], 16)

            def store_gates(t, u):
                sp.wait_ge(S["g_ready"], t + 1)
                sp.dma_start(gates_out[bass.ds(t, 1)].rearrange("o p f -> (o p) f"), G[u % 2][:]).then_inc(gates_stored[u % 2], 16)

            load(0, 0)

            def step(t, u):
                if has(t + 3):
                    load(t + 3, (u + 3) % 4)
                if has(t - 1):
                    store(t - 1, u + 3)
                if has(t - 2):
                    store_flat(t - 2, u)
                if has(t - 3):
                    store_gates(t - 3, u + 1)

            run_steps(sp, step)
            for sems in (res_stored, flat_stored, gates_stored):
                for k in range(2):
                    sp.wait_ge(sems[k], 16 * GROUPS // 2)

        @block.gpsimd
        def _(pool):
            nc.gpsimd.memset(eps_ln[:], LN_EPS).then_inc(S["prep_pool"], 1)
            nc.gpsimd.memset(eps_rms[:], RMS_EPS).then_inc(S["prep_pool"], 1)
            for k in range(2):
                nc.gpsimd.memset(VT[k][:], 0.0).then_inc(S["prep_pool"], 1)

            def divide(t, n):
                segments = 4 if n < 4 else 2
                pool.wait_ge(S["rsum_ready"], 12 * t + (n + 1))
                p = PR[n % 4][:].rearrange("p (b f) -> p b f", b=segments)
                nc.gpsimd.tensor_tensor(p, p, each(RSUM[n % 4][:, 0:segments], 512 // segments), ALU.mult).then_inc(S["probs_ready"], 1)

            def residual(t, u):
                pool.wait_ge(S["x1_ready"], t + 1)
                slot_wait(pool, res_stored, t, u)
                nc.gpsimd.tensor_tensor(RES[u % 2][:], H2[u][:], X1[:], ALU.add).then_inc(S["res_ready"], 1)

            def flat(t, u):
                pool.wait_ge(S["r2_ready"], t + 1)
                wait(pool, "ft_mm", t)
                nc.gpsimd.tensor_tensor(tiles(XR[:]), tiles(X1[:]), each(R2[:]), ALU.mult).then_inc(S["xr_ready"], 1)

            def centre(t, u):
                pool.wait_ge(h_loaded[u], 4 * (t - u) + 16)
                pool.wait_ge(S["nm_ready"], t + 1)
                wait(pool, "u_ready", t)
                nc.gpsimd.tensor_tensor(tiles(U0[:]), tiles(H2[u][:]), each(NM[:]), ALU.subtract).then_inc(S["u0_ready"], 1)

            def normalise(t, u):
                pool.wait_ge(S["u0_ready"], t + 1)
                pool.wait_ge(S["rs_ready"], t + 1)
                wait(pool, "x1_ready", t - 3)
                nc.gpsimd.tensor_tensor(tiles(U[u][:]), tiles(U0[:]), each(RS[:]), ALU.mult).then_inc(S["u_ready"], 1)

            def rms_normalise(t, u):
                pool.wait_ge(S["u_ready"], t + 1)
                pool.wait_ge(S["rr_ready"], t + 1)
                wait(pool, "ut_mm", t - 1)
                nc.gpsimd.tensor_tensor(tiles(UR[u % 2][:]), tiles(U[u][:]), each(RR[:]), ALU.mult).then_inc(S["ur_ready"], 1)

            def step(t, u):
                for n in range(12):
                    if n == 11 and has(t + 2):
                        normalise(t + 2, (u + 2) % 4)
                    if n == 0 and has(t - 1):
                        divide(t - 1, 11)
                    if n > 0 and has(t):
                        divide(t, n - 1)
                    if n == 0 and has(t + 1):
                        rms_normalise(t + 1, (u + 1) % 4)
                    if n == 7 and has(t + 2):
                        centre(t + 2, (u + 2) % 4)
                    if n == 6 and has(t - 1):
                        residual(t - 1, (u + 3) % 4)
                    if n == 9 and has(t - 1):
                        flat(t - 1, u)

            run_steps(pool, step)

        @block.scalar
        def _(act):
            act.wait_ge(S["consts_loaded"], 32)
            nc.scalar.activation(ident_b[:], c("ident", 128), ACT.Copy).then_inc(S["prep_act"], 1)
            nc.scalar.activation(mask_b[:], c("mask", 1024).rearrange("p (a f) -> p a f", a=2), ACT.Copy).then_inc(S["prep_act"], 1)
            act.wait_ge(S["prep_pool"], 4)

            def squares(t, u):
                act.wait_ge(h_loaded[u], 4 * (t - u) + 16)
                wait(act, "sums_ready", 2 * t)
                nc.scalar.activation(HSQ[:], H2[u][:], ACT.Square).then_inc(S["hsq_ready"], 1)

            def roots(t):
                if has(t + 2):
                    act.wait_ge(S["rv_ready"], t + 3)
                    wait(act, "u_ready", t + 2)
                    nc.scalar.activation(RS[:], RV[:], ACT.Sqrt).then_inc(S["rs_ready"], 1)
                    act.wait_ge(S["mu2_ready"], t + 3)
                    wait(act, "rr_ready", t + 2)
                    nc.scalar.activation(SDM[:], MU2[:], ACT.Sqrt, bias=eps_rms[:]).then_inc(S["sdm_ready"], 1)
                if has(t - 1):
                    act.wait_ge(S["s3_ready"], t)
                    wait(act, "r2_ready", t - 1)
                    nc.scalar.activation(SDX[:], S3[:], ACT.Sqrt, bias=eps_rms[:], scale=1.0 / 64).then_inc(S["sdx_ready"], 1)

            def exponents(t, n):
                part = n // 4
                act.wait_ge(S["max_ready"], 12 * t + (n + 1))
                wait(act, "pt_mm", 12 * t + (n - 3))
                segments = 4 if part == 0 else 2
                for b in range(segments):
                    o = slice(b * 512 // segments, (b + 1) * 512 // segments)
                    last = nc.scalar.activation(PR[n % 4][:, o], pS[n % 3][:, o], ACT.Exp, bias=MX[n % 3][:, b:b + 1],
                                                accum_out=SUM[n % 4][:, b:b + 1])
                last.then_inc(S["exp_ready"], 1)

            def copy_probs(t, u, n):
                act.wait_ge(S["pt_mm"], 12 * t + (n + 1))
                wait(act, "pv_mm", 3 * t + (n // 4 - 1))
                nc.scalar.activation(PTS[(4 * (u % 2) + n) % 8][:], pPT[n % 2][:], ACT.Copy).then_inc(S["pts_odd_ready"], 1)

            def copy_yt(t, half):
                act.wait_ge(S["pv_mm"], 3 * t + (1 if half == 0 else 3))
                wait(act, "wo_mm", t)
                nc.scalar.activation(YT[half][:], pYT[:], ACT.Copy).then_inc(S["yt_ready"], 1)

            def copy_v(t, u):
                act.wait_ge(S["v_mm"], t + 1)
                wait(act, "pv_mm", 3 * (t - 1))
                nc.scalar.activation(VT[u % 2][:, :, :, 0:16], pA[:, 0:256].rearrange("p (q g f) -> p q g f", q=4, g=4),
                                     ACT.Copy).then_inc(S["vt_ready"], 1)

            def x_squares(t):
                act.wait_ge(S["x1_ready"], t + 1)
                wait(act, "s3_ready", t)
                nc.scalar.activation(XSQ[:], X1[:], ACT.Square).then_inc(S["xsq_ready"], 1)

            def copy_ft(t, u):
                act.wait_ge(S["ft_mm"], t + 1)
                wait(act, "router_mm", t - 1)
                slot_wait(act, flat_stored, t, u)
                nc.scalar.activation(FT[u % 2][:], pA[:], ACT.Copy, scale=w("ln2_w", 1)).then_inc(S["ft_ready"], 1)

            def router_exp(t):
                act.wait_ge(S["rls_ready"], t + 1)
                wait(act, "rp_ready", t)
                nc.scalar.activation(RE[:], RLS[:], ACT.Exp).then_inc(S["re_ready"], 1)

            def step(t, u):
                for n in range(12):
                    if n == 0 and has(t - 2):
                        copy_ft(t - 2, u)
                    if n == 4 and has(t + 1):
                        copy_v(t + 1, u + 1)
                    if n == 7 and has(t - 1):
                        x_squares(t - 1)
                    if has(t):
                        exponents(t, n)
                    if n == 4 and has(t - 1):
                        copy_yt(t - 1, 1)
                    if n == 8 and has(t):
                        copy_yt(t, 0)
                    if n % 2 == 0 and n < 3 and has(t - 1):
                        copy_probs(t - 1, u + 1, n + 9)
                    if n % 2 == 0 and n >= 3 and has(t):
                        copy_probs(t, u, n - 3)
                    if n == 4 and has(t + 2):
                        squares(t + 2, (u + 2) % 4)
                    if n == 5 and has(t - 2):
                        router_exp(t - 2)
                    if n == 8:
                        roots(t)

            run_steps(act, step)

        @block.tensor
        def _(pe):
            pe.wait_ge(S["consts_loaded"], 32)
            pe.wait_ge(S["prep_act"], 2)
            pe.wait_ge(S["prep_dve"], 7)

            def scores(t, u, n):
                part, head = divmod(n, 4)
                if n == 0:
                    pe.wait_ge(S["qc_ready"], 2 * t + 2)
                    pe.wait_ge(S["kr_ready"], 2 * t + 2)
                wait(pe, "exp_ready", 12 * t + (n - 2))
                nc.tensor.matmul(pS[n % 3][:], ident_b[:], mask_b[:, min(part, 1), :], start=True, stop=False)
                r = slice(32 * head, 32 * head + 32)
                q, k = QC[u % 2], KR[u % 2]
                if part == 0:
                    for m in range(4):
                        o = 256 * (m // 2)
                        last = nc.tensor.matmul(pS[n % 3][:, 128 * m:128 * m + 128], q[m % 2][r, o:o + 128], k[m % 2][r, o:o + 128],
                                                start=False, stop=(m == 3))
                else:
                    o = 256 * (part - 1)
                    for i in range(2):
                        last = nc.tensor.matmul(pS[n % 3][:, 256 * i:256 * i + 256], q[i][r, o + 128:o + 256], k[i][r, o:o + 256],
                                                start=False, stop=(i == 1))
                last.then_inc(S["scores_ready"], 1)

            def transpose_probs(t, n):
                pe.wait_ge(S["probs_ready"], 12 * t + (n + 1))
                wait(pe, "pts_even_ready" if n % 2 == 0 else "pts_odd_ready", 6 * t + n // 2)
                for b in range(4):
                    o = slice(128 * b, 128 * b + 128)
                    last = nc.tensor.transpose(pPT[n % 2][:, o], PR[n % 4][:, o], c("ident", 128))
                last.then_inc(S["pt_mm"], 1)

            def values(t, u, part):
                pe.wait_ge(S["pts_even_ready"], 6 * t + (2 * part + 2))
                pe.wait_ge(S["pts_odd_ready"], 6 * t + (2 * part + 2))
                if part == 0:
                    pe.wait_ge(S["vt_ready"], t + 1)
                if part < 2:
                    wait(pe, "yt_ready", 2 * t + part)
                for b in range(4):
                    if part == 0:
                        j, i, kb, first, final = b // 2, b % 2, 0, True, True
                    else:
                        j, i, kb = part - 1, b // 2, b % 2
                        first, final = kb == 0, kb == 1
                    o = 128 * (2 * j + i)
                    for head in range(4):
                        moving = PTS[(4 * (u % 2) + 4 * part + head) % 8][:, 128 * b:128 * b + 128]
                        last = nc.tensor.matmul(pYT[32 * head:32 * head + 32, o:o + 128], VT[u % 2][:, 2 * j + kb, 2 * i + head // 2, :],
                                                moving, start=first, stop=final)
                last.then_inc(S["pv_mm"], 1)

            def transpose_four(dst, src, done):
                for q in range(4):
                    last = nc.tensor.transpose(dst[:, 128 * q:128 * q + 128], src[:, 128 * q:128 * q + 128], c("ident", 128))
                last.then_inc(S[done], 1)

            def use_router(t, u):
                pe.wait_ge(S["ft_ready"], t + 1)
                for q in range(4):
                    last = nc.tensor.matmul(pA[:, 16 * q:16 * q + 16], FT[u % 2][:, 128 * q:128 * q + 128], w("router", 16), start=True, stop=True)
                last.then_inc(S["router_mm"], 1)

            def use_ut(t, u):
                pe.wait_ge(S["ur_ready"], t + 1)
                wait(pe, "ks_ready", 2 * t)
                transpose_four(pB, UR[u % 2], "ut_mm")

            def use_v(t):
                pe.wait_ge(S["urt_ready"], t + 1)
                wait(pe, "kc_ready", 2 * t)
                wait(pe, "rl_ready", t - 2)
                for q in range(4):
                    last = nc.tensor.matmul(pA[:, 64 * q:64 * q + 64], URT[:, 128 * q:128 * q + 128], w_in[:, 384:448], start=True, stop=True)
                last.then_inc(S["v_mm"], 1)

            def project(dst, i, which, done):
                nc.tensor.matmul(dst[:], w_img[:, i, 128 * which:128 * which + 128], URT[:], start=True, stop=True).then_inc(S[done], 1)

            def use_q0(t):
                project(pB, 0, 0, "q_mm")

            def use_q1(t):
                pe.wait_ge(S["vt_ready"], t + 1)
                project(pA, 1, 0, "q_mm")

            def use_wo(t):
                pe.wait_ge(S["yt_ready"], 2 * t + 2)
                if has(t + 1):
                    pe.wait_ge(S["ks_ready"], 2 * t + 4)
                if has(t + 2):
                    pe.wait_ge(S["qc_ready"], 2 * t + 5)
                wait(pe, "x1_ready", t)
                for k in range(8):
                    pair, half, image = k // 4, k // 2 % 2, k % 2
                    o = 128 * (2 * pair + image)
                    last = nc.tensor.matmul(pB[:, 64 * k:64 * k + 64], YT[half][:, o:o + 128], w("wo", 64), start=True, stop=True)
                last.then_inc(S["wo_mm"], 1)

            def use_k0(t):
                pe.wait_ge(S["qc_ready"], 2 * t + 2)
                project(pA, 0, 1, "k_mm")

            def use_ks0(t):
                wait(pe, "x1_ready", t - 1)
                project(pB, 0, 2, "k_mm")

            def use_k1(t):
                pe.wait_ge(S["kc_ready"], 2 * t + 1)
                project(pA, 1, 1, "k_mm")

            def use_ks1(t):
                pe.wait_ge(S["ks_ready"], 2 * t + 1)
                project(pB, 1, 2, "k_mm")

            def use_ft(t):
                pe.wait_ge(S["xr_ready"], t + 1)
                wait(pe, "rl_ready", t)
                if has(t + 2):
                    pe.wait_ge(S["kc_ready"], 2 * t + 6)
                transpose_four(pA, XR, "ft_mm")

            def step(t, u):
                for n in range(12):
                    if has(t):
                        scores(t, u, n)
                    if n == 0 and has(t - 1):
                        values(t - 1, u + 1, 1)
                    if n == 4 and has(t - 1):
                        values(t - 1, u + 1, 2)
                    if n == 8 and has(t):
                        values(t, u, 0)
                    if n < 3 and has(t - 1):
                        transpose_probs(t - 1, n + 9)
                    if n >= 3 and has(t):
                        transpose_probs(t, n - 3)
                    if n == 1 and has(t - 2):
                        use_router(t - 2, u)
                    if n == 2 and has(t + 1):
                        use_ut(t + 1, u + 1)
                    if n == 5 and has(t - 1):
                        use_wo(t - 1)
                    if n == 11 and has(t - 1):
                        use_ft(t - 1)
                    for m, use in ((3, use_v), (3, use_q0), (4, use_q1), (6, use_k0), (7, use_ks0), (8, use_k1), (9, use_ks1)):
                        if n == m and has(t + 1):
                            use(t + 1)

            run_steps(pe, step)

        @block.vector
        def _(dve):
            dve.wait_ge(S["consts_loaded"], 32)
            for a, b in ((0, 128), (128, 256), (256, 384), (384, 448)):
                nc.vector.tensor_scalar(w_in[:, a:b], wsb[:, C_W["w_in"] + a:C_W["w_in"] + b], w("ln1_w", 1), None,
                                        ALU.mult).then_inc(S["prep_dve"], 1)
            dve.wait_ge(S["prep_dve"], 4)
            nc.vector.memset(w_img[:], 0.0).then_inc(S["prep_dve"], 1)
            dve.wait_ge(S["prep_dve"], 5)
            for i in range(2):
                r = slice(64 * i, 64 * i + 64)
                nc.vector.tensor_copy(w_img[r, i], w_in[r, 0:384]).then_inc(S["prep_dve"], 1)

            def statistics(t, u):
                dve.wait_ge(h_loaded[u], 4 * (t - u) + 16)
                wait(dve, "v0_ready", t)
                wait(dve, "nm_ready", t)
                nc.vector.tensor_reduce(S1[:], tiles(H2[u][:]), AX.X, ALU.add).then_inc(S["sums_ready"], 1)
                dve.wait_ge(S["hsq_ready"], t + 1)
                nc.vector.tensor_reduce(S2[:], tiles(HSQ[:]), AX.X, ALU.add).then_inc(S["sums_ready"], 1)
                dve.wait_ge(S["sums_ready"], 2 * t + 2)
                nc.vector.tensor_tensor(M2[:], S1[:], S1[:], ALU.mult).then_inc(S["m2_ready"], 1)
                wait(dve, "u0_ready", t)
                nc.vector.tensor_scalar(NM[:], S1[:], 1.0 / 64, None, ALU.mult).then_inc(S["nm_ready"], 1)

            def variances(t):
                dve.wait_ge(S["m2_ready"], t + 1)
                nc.vector.scalar_tensor_tensor(V0[:], S2[:], 64.0, M2[:], ALU.mult, ALU.subtract).then_inc(S["v0_ready"], 1)
                dve.wait_ge(S["v0_ready"], t + 1)
                wait(dve, "mu2_ready", t)
                nc.vector.tensor_scalar(V1[:], V0[:], 1.0 / 4096, 0.0, ALU.mult, ALU.max).then_inc(S["v1_ready"], 1)
                dve.wait_ge(S["v1_ready"], t + 1)
                wait(dve, "rv_ready", t)
                nc.vector.tensor_scalar(VE[:], V1[:], LN_EPS, None, ALU.add).then_inc(S["ve_ready"], 1)
                dve.wait_ge(S["ve_ready"], t + 1)
                wait(dve, "rs_ready", t)
                nc.vector.reciprocal(RV[:], VE[:]).then_inc(S["rv_ready"], 1)
                dve.wait_ge(S["rv_ready"], t + 1)
                wait(dve, "sdm_ready", t)
                nc.vector.tensor_tensor(MU2[:], V1[:], RV[:], ALU.mult).then_inc(S["mu2_ready"], 1)

            def rms_factor(t):
                dve.wait_ge(S["sdm_ready"], t + 1)
                wait(dve, "ur_ready", t)
                nc.vector.reciprocal(RR[:], SDM[:]).then_inc(S["rr_ready"], 1)

            def maxima(t, n):
                part = n // 4
                dve.wait_ge(S["scores_ready"], 12 * t + (n + 1))
                wait(dve, "exp_ready", 12 * t + (n - 2))
                segments = 4 if part == 0 else 2
                nc.vector.tensor_reduce(MX[n % 3][:, 0:segments], pS[n % 3][:].rearrange("p (b f) -> p b f", b=segments),
                                        AX.X, ALU.max, negate=True).then_inc(S["max_ready"], 1)

            def reciprocals(t, n):
                segments = 4 if n < 4 else 2
                dve.wait_ge(S["exp_ready"], 12 * t + (n + 1))
                wait(dve, "probs_ready", 12 * t + (n - 3))
                nc.vector.reciprocal(RSUM[n % 4][:, 0:segments], SUM[n % 4][:, 0:segments]).then_inc(S["rsum_ready"], 1)

            def copy_probs(t, u, n):
                dve.wait_ge(S["pt_mm"], 12 * t + (n + 1))
                wait(dve, "pv_mm", 3 * t + (n // 4 - 1))
                nc.vector.tensor_copy(PTS[(4 * (u % 2) + n) % 8][:], pPT[n % 2][:]).then_inc(S["pts_even_ready"], 1)

            def add_attention(t, u):
                dve.wait_ge(S["wo_mm"], t + 1)
                wait(dve, "xsq_ready", t)
                wait(dve, "res_ready", t)
                wait(dve, "xr_ready", t)
                nc.vector.tensor_tensor(X1[:], U[u][:], pB[:], ALU.add).then_inc(S["x1_ready"], 1)

            def x_sums(t):
                dve.wait_ge(S["xsq_ready"], t + 1)
                wait(dve, "sdx_ready", t)
                nc.vector.tensor_reduce(S3[:], tiles(XSQ[:]), AX.X, ALU.add).then_inc(S["s3_ready"], 1)

            def x_factor(t):
                dve.wait_ge(S["sdx_ready"], t + 1)
                wait(dve, "xr_ready", t)
                nc.vector.reciprocal(R2[:], SDX[:]).then_inc(S["r2_ready"], 1)

            def with_table(dst, src, name):
                t = c(name, 256).unsqueeze(1).broadcast_to([128, 2, 256])
                return nc.vector.tensor_tensor(dst.rearrange("p (j f) -> p j f", j=2), src.rearrange("p (j f) -> p j f", j=2), t, ALU.mult)

            def rotate_query(t, u, i):
                dve.wait_ge(S["q_mm"], 2 * t + (i + 1))
                wait(dve, "scores_ready", 12 * (t - 1))
                with_table(QC[u % 2][i][:], (pB, pA)[i][:], "rope_q").then_inc(S["qc_ready"], 1)

            def key_cos(t, i):
                dve.wait_ge(S["k_mm"], 4 * t + (1 if i == 0 else 3))
                wait(dve, "kr_ready", 2 * t + (i - 1))
                with_table(KC[i][:], pA[:], "rope_kc").then_inc(S["kc_ready"], 1)

            def key_sin(t, i):
                dve.wait_ge(S["k_mm"], 4 * t + (2 if i == 0 else 4))
                wait(dve, "kr_ready", 2 * t + (i - 1))
                with_table(KS[i][:], pB[:], "rope_ks").then_inc(S["ks_ready"], 1)

            def rotate_key(t, u, i):
                dve.wait_ge(S["kc_ready"], 2 * t + (i + 1))
                dve.wait_ge(S["ks_ready"], 2 * t + (i + 1))
                wait(dve, "scores_ready", 12 * (t - 1))
                nc.vector.tensor_tensor(KR[u % 2][i][:], KC[i][:], KS[i][:], ALU.add).then_inc(S["kr_ready"], 1)

            def copy_urt(t):
                dve.wait_ge(S["ut_mm"], t + 1)
                wait(dve, "k_mm", 4 * t)
                nc.vector.tensor_copy(URT[:], pB[:]).then_inc(S["urt_ready"], 1)

            def router_logits(t):
                dve.wait_ge(S["router_mm"], t + 1)
                wait(dve, "rls_ready", t)
                nc.vector.tensor_copy(RL[:], pA[:, 0:64]).then_inc(S["rl_ready"], 1)

            def router_shift(t):
                dve.wait_ge(S["rl_ready"], t + 1)
                nc.vector.tensor_reduce(RMX[:], tiles(RL[:], 8), AX.X, ALU.max).then_inc(S["rmx_ready"], 1)
                dve.wait_ge(S["rmx_ready"], t + 1)
                wait(dve, "re_ready", t)
                nc.vector.tensor_tensor(tiles(RLS[:], 8), tiles(RL[:], 8), each(RMX[:], 8), ALU.subtract).then_inc(S["rls_ready"], 1)

            def router_probs(t):
                dve.wait_ge(S["re_ready"], t + 1)
                nc.vector.tensor_reduce(RZ[:], tiles(RE[:], 8), AX.X, ALU.add).then_inc(S["rz_ready"], 1)
                dve.wait_ge(S["rz_ready"], t + 1)
                wait(dve, "rp_ready", t)
                nc.vector.reciprocal(RRZ[:], RZ[:]).then_inc(S["rrz_ready"], 1)
                dve.wait_ge(S["rrz_ready"], t + 1)
                wait(dve, "w0_ready", t)
                nc.vector.tensor_tensor(tiles(RP[:], 8), tiles(RE[:], 8), each(RRZ[:], 8), ALU.mult).then_inc(S["rp_ready"], 1)

            def pairs(ap):
                return ap.rearrange("p (k e f) -> p k e f", k=8, e=8)

            def rivals():
                return tiles(RP[:], 8).unsqueeze(2).broadcast_to([128, 8, 8, 8])

            def own():
                return tiles(RP[:], 8).unsqueeze(3).broadcast_to([128, 8, 8, 8])

            def router_greater(t):
                dve.wait_ge(S["rp_ready"], t + 1)
                wait(dve, "before_ready", t)
                nc.vector.tensor_tensor(pairs(GT[:]), rivals(), own(), ALU.is_gt).then_inc(S["gt_ready"], 1)

            def router_equal(t):
                wait(dve, "eqm_ready", t)
                nc.vector.tensor_tensor(pairs(EQ[:]), rivals(), own(), ALU.is_equal).then_inc(S["eq_ready"], 1)
                dve.wait_ge(S["eq_ready"], t + 1)
                wait(dve, "before_ready", t)
                nc.vector.tensor_tensor(tiles(EQM[:]), tiles(EQ[:]), c("lower", 64).unsqueeze(1).broadcast_to([128, 8, 64]),
                                        ALU.mult).then_inc(S["eqm_ready"], 1)

            def router_rank(t):
                dve.wait_ge(S["gt_ready"], t + 1)
                dve.wait_ge(S["eqm_ready"], t + 1)
                wait(dve, "rank_ready", t)
                nc.vector.tensor_tensor(BEFORE[:], GT[:], EQM[:], ALU.add).then_inc(S["before_ready"], 1)
                dve.wait_ge(S["before_ready"], t + 1)
                wait(dve, "sel_ready", t)
                nc.vector.tensor_reduce(RK[:], tiles(BEFORE[:], 8), AX.X, ALU.add).then_inc(S["rank_ready"], 1)

            def router_select(t):
                dve.wait_ge(S["rank_ready"], t + 1)
                wait(dve, "w0_ready", t)
                nc.vector.tensor_scalar(SEL[:], RK[:], 2.0, None, ALU.is_lt).then_inc(S["sel_ready"], 1)
                dve.wait_ge(S["sel_ready"], t + 1)
                wait(dve, "g_ready", t)
                nc.vector.tensor_tensor(W0[:], RP[:], SEL[:], ALU.mult).then_inc(S["w0_ready"], 1)

            def router_gates(t, u):
                dve.wait_ge(S["w0_ready"], t + 1)
                nc.vector.tensor_reduce(WS[:], tiles(W0[:], 8), AX.X, ALU.add).then_inc(S["ws_ready"], 1)
                dve.wait_ge(S["ws_ready"], t + 1)
                wait(dve, "rws_ready", t)
                nc.vector.tensor_scalar(WSE[:], WS[:], 1e-9, None, ALU.add).then_inc(S["wse_ready"], 1)
                dve.wait_ge(S["wse_ready"], t + 1)
                wait(dve, "g_ready", t)
                nc.vector.reciprocal(RWS[:], WSE[:]).then_inc(S["rws_ready"], 1)
                dve.wait_ge(S["rws_ready"], t + 1)
                slot_wait(dve, gates_stored, t, u)
                nc.vector.tensor_tensor(tiles(G[u % 2][:], 8), tiles(W0[:], 8), each(RWS[:], 8), ALU.mult).then_inc(S["g_ready"], 1)

            def step(t, u):
                for n in range(12):
                    if n == 0 and has(t - 1):
                        reciprocals(t - 1, 11)
                    if has(t):
                        maxima(t, n)
                    if n > 0 and has(t):
                        reciprocals(t, n - 1)
                    if has(t + 1):
                        if n == 4:
                            rotate_query(t + 1, u + 1, 0)
                        if n == 5:
                            rotate_query(t + 1, u + 1, 1)
                        if n == 7:
                            key_cos(t + 1, 0)
                        if n == 8:
                            key_sin(t + 1, 0)
                            rotate_key(t + 1, u + 1, 0)
                            key_cos(t + 1, 1)
                        if n == 9:
                            key_sin(t + 1, 1)
                            rotate_key(t + 1, u + 1, 1)
                    if n == 2 and has(t - 2):
                        router_logits(t - 2)
                    if n == 2 and has(t + 1):
                        copy_urt(t + 1)
                    if n == 6 and has(t - 1):
                        add_attention(t - 1, (u + 3) % 4)
                    if n == 9 and has(t - 1):
                        x_factor(t - 1)
                    if n % 2 == 1 and n < 3 and has(t - 1):
                        copy_probs(t - 1, u + 1, n + 9)
                    if n % 2 == 1 and n >= 3 and has(t):
                        copy_probs(t, u, n - 3)
                    if has(t + 2):
                        if n == 5:
                            statistics(t + 2, (u + 2) % 4)
                        if n == 6:
                            variances(t + 2)
                        if n == 9:
                            rms_factor(t + 2)
                    if n == 7 and has(t - 1):
                        x_sums(t - 1)
                    if has(t - 2):
                        if n == 3:
                            router_shift(t - 2)
                        if n == 6:
                            router_probs(t - 2)
                        if n == 7:
                            router_greater(t - 2)
                        if n == 10:
                            router_equal(t - 2)
                        if n == 11:
                            router_rank(t - 2)
                    if has(t - 3):
                        if n == 1:
                            router_select(t - 3)
                        if n == 2:
                            router_gates(t - 3, u + 1)

            run_steps(dve, step)
def experts_phase(nc, held, flat, gates, res, wpack, out):
    STEPS = 2 * GROUPS
    with ExitStack() as ctx:
        def sb(name, shape, dt=F32):
            return ctx.enter_context(nc.sbuf_tensor("d_" + name, shape, dt))

        wsb = sb("wsb", [128, D_W["end"]])
        w_high = sb("w_high", [128, 2, UNITS * 128], F32R)
        w_low = sb("w_low", [128, 2, UNITS * 128], F32R)
        F2 = [sb(f"f2_{k}", [128, 512]) for k in range(4)]
        HL = [sb(f"hl{k}", [128, 512], F32R) for k in range(2)]
        SG = [sb(f"sg{k}", [128, 512]) for k in range(2)]
        HH = [sb(f"hh{k}", [128, 512]) for k in range(4)]
        GB = [sb(f"g{k}", [128, 64]) for k in range(2)]
        RB = [sb(f"r{k}", [128, 512]) for k in range(2)]
        GY = [sb(f"gy{k}", [128, 4, 512]) for k in range(2)]
        Y4 = sb("y4", [128, 4, 256])
        Y2 = sb("y2", [128, 4, 128])
        Y1 = sb("y1", [128, 4, 64])
        OUT = [sb(f"out{k}", [128, 512]) for k in range(2)]

        def bank(name):
            return ctx.enter_context(nc.psum_tensor("d_" + name, [128, 512], F32))

        pH1 = [bank(f"ph1_{k}") for k in range(2)]
        pH3 = [bank(f"ph3_{k}") for k in range(2)]
        pY = [bank(f"py{k}") for k in range(4)]

        names = ("weights_loaded w_high_ready w_low_ready high_ready low_ready hidden_mm silu_ready hh_ready w2_mm "
                 "gated_ready y4_ready y2_ready y1_ready out_ready").split()
        S = {n: new_semaphore(nc, held, "d_" + n) for n in names}
        f_loaded = [new_semaphore(nc, held, f"d_f_loaded{k}") for k in range(4)]
        g_loaded, r_loaded, out_stored = (
            [new_semaphore(nc, held, f"d_{n}{k}") for k in range(2)] for n in ("g_loaded", "r_loaded", "out_stored"))

        def wait(eng, name, value):
            if not isinstance(value, int) or value > 0:
                eng.wait_ge(S[name], value)

        def has(t):
            return not isinstance(t, int) or 0 <= t < STEPS

        def run_steps(eng, step):
            for t in range(-1, 4):
                step(t, t % 4)
            with eng.Fori(0, STEPS // 4 - 2) as j:
                for u in range(4):
                    step(4 * j + (4 + u), u)
            for t in range(STEPS - 4, STEPS + 1):
                step(t, t % 4)

        block = ctx.enter_context(nc.Block())

        @block.sync
        def _(sp):
            sp.dma_start(wsb[:], wpack).then_inc(S["weights_loaded"], 16)

            def load(s, v):
                wait(sp, "low_ready", 2 * s - 2)
                for i in range(2):
                    rows = flat[bass.ds(s, 1), 64 * i:64 * i + 64].rearrange("o p f -> (o p) f")
                    for half in range(2):
                        sp.dma_start(F2[2 * v + i][64 * half:64 * half + 64, :], rows).then_inc(f_loaded[2 * v + i], 16)
                wait(sp, "gated_ready", 8 * (s - 1))
                sp.dma_start(GB[v][:], gates[bass.ds(s, 1)].rearrange("o p f -> (o p) f")).then_inc(g_loaded[v], 16)
                wait(sp, "out_ready", 2 * (s - 1))
                sp.dma_start(RB[v][:], res[bass.ds(s, 1)].rearrange("o p f -> (o p) f")).then_inc(r_loaded[v], 16)

            def store(s, v):
                sp.wait_ge(S["out_ready"], 2 * s + 2)
                dst = out[bass.ds(s, 1)].rearrange("o q p c -> p (o q) c")
                sp.dma_start(dst, OUT[v][:].rearrange("p (q c) -> p q c", c=64)).then_inc(out_stored[v], 16)

            load(0, 0)
            load(1, 1)
            store(0, 0)
            with sp.Fori(0, GROUPS // 2 - 1) as j:
                for v in range(2):
                    load(2 * j + (2 + v), v)
                    store(2 * j + (1 + v), (1 + v) % 2)
            store(GROUPS - 1, 1)
            for v in range(2):
                sp.wait_ge(out_stored[v], 16 * GROUPS // 2)

        @block.gpsimd
        def _(pool):
            def fold(t, u):
                i, v = u % 2, u // 2
                gy = GY[i]
                pool.wait_ge(S["gated_ready"], 4 * t + 4)
                wait(pool, "y2_ready", t)
                nc.gpsimd.tensor_tensor(Y4[:], gy[:, :, 0:256], gy[:, :, 256:512], ALU.add).then_inc(S["y4_ready"], 1)
                pool.wait_ge(S["y4_ready"], t + 1)
                wait(pool, "y1_ready", t)
                nc.gpsimd.tensor_tensor(Y2[:], Y4[:, :, 0:128], Y4[:, :, 128:256], ALU.add).then_inc(S["y2_ready"], 1)
                pool.wait_ge(S["y2_ready"], t + 1)
                wait(pool, "out_ready", t)
                nc.gpsimd.tensor_tensor(Y1[:], Y2[:, :, 0:64], Y2[:, :, 64:128], ALU.add).then_inc(S["y1_ready"], 1)
                pool.wait_ge(S["y1_ready"], t + 1)
                pool.wait_ge(r_loaded[v], 4 * (t - u) + 16)
                if i == 0 and (not isinstance(t, int) or t >= 4):
                    pool.wait_ge(out_stored[v], 4 * (t - u))
                r = RB[v][:].rearrange("p (a h i c) -> p a h i c", a=2, h=2, i=2)[:, :, :, i]
                o = OUT[v][:].rearrange("p (a i h c) -> p a i h c", a=2, i=2, h=2)[:, :, i]
                y = Y1[:].rearrange("p (a h) c -> p a h c", a=2)
                nc.gpsimd.tensor_tensor(o, r, y, ALU.add).then_inc(S["out_ready"], 1)

            def step(t, u):
                if has(t - 1):
                    fold(t - 1, (u + 3) % 4)

            run_steps(pool, step)

        @block.scalar
        def _(act):
            act.wait_ge(S["weights_loaded"], 16)
            for k in range(2):
                nc.scalar.activation(w_high[:, k], wsb[:, UNITS * 128 * k:UNITS * 128 * (k + 1)], ACT.Copy).then_inc(S["w_high_ready"], 1)

            def high(t, u):
                act.wait_ge(f_loaded[u], 8 * (t - u) + 32)
                wait(act, "hidden_mm", UNITS * (t - 1))
                nc.scalar.activation(HL[u % 2][:], F2[u][:], ACT.Copy).then_inc(S["high_ready"], 1)

            def silu(t, u, n):
                k = (UNITS * u + n) % 2
                act.wait_ge(S["hidden_mm"], UNITS * t + (n + 1))
                wait(act, "hh_ready", UNITS * t + (n - 1))
                nc.scalar.activation(SG[k][:], pH1[k][:], ACT.Silu).then_inc(S["silu_ready"], 1)

            def step(t, u):
                for n in range(UNITS):
                    if has(t):
                        silu(t, u, n)
                    if n == 5 and has(t + 1):
                        high(t + 1, (u + 1) % 4)

            run_steps(act, step)

        @block.tensor
        def _(pe):
            pe.wait_ge(S["w_low_ready"], 2)

            def hidden(t, u, n):
                k = (UNITS * u + n) % 2
                if n == 0:
                    pe.wait_ge(S["low_ready"], t + 1)
                wait(pe, "hh_ready", UNITS * t + (n - 1))
                cols = slice(128 * n, 128 * n + 128)
                for m, dst in ((0, pH1[k]), (1, pH3[k])):
                    nc.tensor.matmul(dst[:], w_high[:, m, cols], HL[u % 2][:], start=True, stop=False)
                    last = nc.tensor.matmul(dst[:], w_low[:, m, cols], HL[u % 2][:], start=False, stop=True)
                last.then_inc(S["hidden_mm"], 1)

            def down(t, u, n):
                pe.wait_ge(S["hh_ready"], UNITS * t + (n + 1))
                if n < len(TAIL_EXPERTS):
                    experts, row = TAIL_EXPERTS[n], 0
                else:
                    experts, row = [n - len(TAIL_EXPERTS)], 1
                a, b = 64 * experts[0], 64 * (experts[-1] + 1)
                moving = wsb[:, D_W["w2"] + 512 * row + a:D_W["w2"] + 512 * row + b]
                for m in range(4):
                    if n == 0:
                        wait(pe, "gated_ready", 4 * (t - 1) + (m + 1))
                    last = nc.tensor.matmul(pY[m][:, a:b], HH[(UNITS * u + n) % 4][:, 128 * m:128 * m + 128], moving,
                                            start=n == 0, stop=n == UNITS - 1, skip_group_check=True)
                last.then_inc(S["w2_mm"], 1)

            def step(t, u):
                for n in range(UNITS):
                    if has(t):
                        hidden(t, u, n)
                    if n < 2 and has(t - 1):
                        down(t - 1, (u + 3) % 4, UNITS - 2 + n)
                    if n == 3 and has(t):
                        down(t, u, 0)
                    if n >= 3 and has(t):
                        down(t, u, n - 2)

            run_steps(pe, step)

        @block.vector
        def _(dve):
            for k in range(2):
                dve.wait_ge(S["w_high_ready"], k + 1)
                nc.vector.tensor_tensor(w_low[:, k], wsb[:, UNITS * 128 * k:UNITS * 128 * (k + 1)], w_high[:, k].bitcast(F32),
                                        ALU.subtract).then_inc(S["w_low_ready"], 1)

            def low(t, u):
                dve.wait_ge(S["high_ready"], t + 1)
                rows = HL[u % 2][64:128, :]
                nc.vector.tensor_tensor(rows, F2[u][64:128, :], rows.bitcast(F32), ALU.subtract).then_inc(S["low_ready"], 1)

            def product(t, u, n):
                g = UNITS * u + n
                dve.wait_ge(S["silu_ready"], UNITS * t + (n + 1))
                wait(dve, "w2_mm", UNITS * t + (n - 3))
                nc.vector.tensor_tensor(HH[g % 4][:], SG[g % 2][:], pH3[g % 2][:], ALU.mult).then_inc(S["hh_ready"], 1)

            def gated(t, u, m):
                v, i = u // 2, u % 2
                if m == 0:
                    dve.wait_ge(g_loaded[v], 4 * (t - u) + 16)
                    dve.wait_ge(S["w2_mm"], UNITS * t + UNITS)
                    wait(dve, "y4_ready", t - 1)
                k = 2 * m + i
                gate = GB[v][:, 8 * k:8 * k + 8].unsqueeze(2).broadcast_to([128, 8, 64])
                nc.vector.tensor_tensor(GY[i][:, m].rearrange("p (e c) -> p e c", c=64), pY[m][:].rearrange("p (e c) -> p e c", c=64),
                                        gate, ALU.mult).then_inc(S["gated_ready"], 1)

            def step(t, u):
                for n in range(UNITS):
                    if has(t):
                        product(t, u, n)
                    if n == 1 and has(t - 1):
                        for m in range(4):
                            gated(t - 1, (u + 3) % 4, m)
                    if n == 6 and has(t + 1):
                        low(t + 1, (u + 1) % 4)

            run_steps(dve, step)


def _pair(a, np):
    return np.concatenate([a, a], 0)


def _blocks(a, np, swap=False):
    out = np.zeros((128, 128), a.dtype)
    for i in range(2):
        o = 1 - i if swap else i
        out[64 * i:64 * i + 64, 64 * o:64 * o + 64] = a
    return out


def pack_a(inputs, np):
    g = {k[len("L0_tok_"):]: np.asarray(v) for k, v in inputs.items() if k.startswith("L0_tok_")}
    col = lambda v: _pair(v.reshape(64, 1), np)
    return np.ascontiguousarray(np.concatenate([
        _pair(g["Wkv"].T, np), _blocks(g["Wkv"][64:].T, np, True), _blocks(g["proj_w"].T, np, True),
        _blocks(g["Wq"].T, np), col(g["ln_kv_w"]), col(g["ln_kv_b"]), col(g["ln_q_w"]), col(g["ln_q_b"]),
        col(g["proj_b"])], 1))


def consts_a(np):
    p = np.arange(128)
    same = (p[:, None] // 64 == p[None] // 64).astype(np.float32)
    c = np.arange(32)
    parts = [np.eye(128, dtype=np.float32) - same / 64, same / 64]
    for sub in range(2):
        parts.append(((c[None] // 16 == sub) & (p[:, None] // 64 == (c[None] % 16) // 8)) / np.float32(64))
    for sub in range(2):
        parts.append((c[None] // 16 == sub) & (p[:, None] // 8 == c[None] % 16))
    head = (1 - p // 64) * 8 + (p % 64) // 8
    for g in range(CHUNKS):
        parts.append((p[:, None] // 16 == g) & (p[:, None] % 16 == head[None]))
    return np.ascontiguousarray(np.concatenate(parts, 1).astype(np.float32))


def pack_b(inputs, np):
    g = {k[len("L0_attn_"):]: np.asarray(v) for k, v in inputs.items() if k.startswith("L0_attn_")}
    rows = lambda v: np.broadcast_to(v[None], (128, v.shape[0]))
    wv, bv = g["W_qkv"][:, 128:], g["b_qkv"][128:]
    return np.ascontiguousarray(np.concatenate([
        _pair(g["W_qkv"], np), _pair(np.concatenate([wv.T, wv.T], 1), np), _pair(g["W_out"], np),
        _pair(np.broadcast_to(bv[:, None], (64, 128)), np), rows(g["b_qkv"]), rows(g["b_out"])], 1))


def consts_b(np):
    p = np.arange(128)
    same = (p[:, None] // 64 == p[None] // 64).astype(np.float32)
    eye = np.eye(128, dtype=np.float32)
    return np.ascontiguousarray(np.concatenate([eye, eye - same / 64, np.ones((128, 1), np.float32)], 1))


def pack_c(inputs, np):
    g = {k[len("L0_ffn_"):]: np.asarray(v) for k, v in inputs.items() if k.startswith("L0_ffn_")}
    swap = (np.arange(16) + 8) % 16
    q = g["wq"].reshape(4, 16, 64)
    k = g["wk"].reshape(2, 16, 64)[np.array([0, 0, 1, 1])]
    q = np.concatenate([q, q[:, swap]], 1).reshape(128, 64).T
    kc = np.concatenate([k, k], 1).reshape(128, 64).T
    ks = np.concatenate([k[:, swap], k[:, swap]], 1).reshape(128, 64).T

    def blocks(a):
        out = np.zeros((128, 2 * a.shape[1]), a.dtype)
        out[:64, :a.shape[1]] = a
        out[64:, a.shape[1]:] = a
        return out

    def heads(a):
        out = np.zeros((4, 32, 64), a.dtype)
        out[:, :16] = a.reshape(4, 16, 64)
        return out.reshape(128, 64)

    col = lambda v: _pair(v.reshape(64, 1), np)
    return np.ascontiguousarray(np.concatenate([
        _pair(q, np), _pair(kc, np), _pair(ks, np), blocks(g["wv"].T), heads(g["wo"].T), blocks(g["router_w"].T),
        col(g["ln1_w"]), col(g["ln2_w"])], 1))


def consts_c(np):
    p = np.arange(128)
    later = np.where(p[None] > p[:, None], np.float32(-1e30), np.float32(0))
    zero = np.zeros((128, 128), np.float32)
    mask = [later] * 4 + [zero, later] * 2
    inv_freq = 1.0 / 10000.0 ** (np.arange(0, 16, 2, dtype=np.float32) / 16)
    freqs = np.outer(np.arange(256, dtype=np.float32), inv_freq)
    emb = np.concatenate([freqs, freqs], axis=-1)
    cos, sin = np.cos(emb).T, np.sin(emb).T
    sin = np.where(np.arange(16)[:, None] < 8, -sin, sin)
    rope_q = np.tile(np.concatenate([cos, sin], 0) * np.float32(0.25), (4, 1))
    lower = (np.arange(8)[None] < np.arange(8)[:, None]).astype(np.float32).reshape(1, 64)
    return np.ascontiguousarray(np.concatenate(
        [np.eye(128, dtype=np.float32)] + mask + [rope_q, np.tile(cos, (8, 1)), np.tile(sin, (8, 1)), np.tile(lower, (128, 1))],
        1).astype(np.float32))


def pack_d(inputs, np):
    w1, w2, w3 = (np.asarray(inputs["L0_ffn_" + n]) for n in ("w1", "w2", "w3"))

    def units(a):
        out = np.zeros((64, UNITS, 128), a.dtype)
        for n, experts in enumerate(TAIL_EXPERTS):
            for i, e in enumerate(experts):
                out[:, n, i * TAIL:(i + 1) * TAIL] = a[e, 128:].T
        for e in range(EXPERTS):
            out[:, len(TAIL_EXPERTS) + e] = a[e, :128].T
        return _pair(out.reshape(64, UNITS * 128), np)

    down = np.zeros((128, 2, EXPERTS, 64), w2.dtype)
    for e in range(EXPERTS):
        i = e % PER_TAIL
        down[i * TAIL:(i + 1) * TAIL, 0, e] = w2[e, :, 128:].T
        down[:, 1, e] = w2[e, :, :128].T
    return np.ascontiguousarray(np.concatenate([units(w1), units(w3), down.reshape(128, -1)], 1))


def end_phase(nc, held):
    nc.all_engine_barrier()
    nc.clear_and_free_semaphores(held)
    held.clear()
    nc.all_engine_barrier()


def build(nc, ap, out):
    def scratch(name, shape):
        return nc.dram_tensor(name, shape, F32).ap()

    tokens = scratch("tokens", [PAIRS, 128, NPATCH])
    mixed = scratch("mixed", [GROUPS, 128, 512])
    residual = scratch("residual", [GROUPS, 128, 512])
    flat = scratch("flat", [GROUPS, 128, 512])
    gates = scratch("gates", [GROUPS, 128, 8 * EXPERTS])
    held = []
    tokenize_phase(nc, held, ap["x"], ap["wa"], ap["ca"], tokens)
    end_phase(nc, held)
    linear_attention_phase(nc, held, tokens, ap["wb"], ap["cb"], mixed)
    end_phase(nc, held)
    causal_attention_phase(nc, held, mixed, ap["wc"], ap["cc"], residual, flat, gates)
    end_phase(nc, held)
    experts_phase(nc, held, flat, gates, residual, ap["wd"], out)


def kernel(**inputs):
    import numpy as np
    import concourse.bacc as bacc
    from concourse.bass_utils import run_bass_kernel_spmd

    arrays = {"x": np.ascontiguousarray(inputs["x"]), "wa": pack_a(inputs, np), "ca": consts_a(np),
              "wb": pack_b(inputs, np), "cb": consts_b(np), "wc": pack_c(inputs, np), "cc": consts_c(np),
              "wd": pack_d(inputs, np)}
    nc = bacc.Bacc("TRN2", target_bir_lowering=False, num_devices=1)
    ap = {n: nc.dram_tensor(f"in_{n}", a.shape, mybir.dt.from_np(a.dtype), kind="ExternalInput").ap() for n, a in arrays.items()}
    out = nc.dram_tensor("out_0_dram", (IMAGES, NPATCH, CH), F32, kind="ExternalOutput").ap()
    build(nc, ap, out.rearrange("(s a) (h p) c -> s (a h) p c", a=4, p=128))
    results = run_bass_kernel_spmd(nc, [{f"in_{n}": a for n, a in arrays.items()}], core_ids=[0])
    return results.results[0]["out_0_dram"]
```
